# Optimizing a Trainium2 kernel written in Bass

```python
import numpy as np
import jax
import jax.numpy as jnp

def _softmax(x, axis=-1):
    return jax.nn.softmax(x, axis=axis)

def _gelu(x):
    return jax.nn.gelu(x, approximate=True)

def _silu(x):
    return jax.nn.silu(x)

def _sigmoid(x):
    return jax.nn.sigmoid(x)

def _layernorm(x, axis=-1, eps=1e-05):
    m = jnp.mean(x, axis=axis, keepdims=True)
    v = jnp.var(x, axis=axis, keepdims=True)
    return (x - m) / jnp.sqrt(v + eps)

def _scatter_add(tgt, idx, src, axis=0):
    return tgt.at[idx].add(src)

def _segment_sum(src, seg, n):
    return jax.ops.segment_sum(src, seg, n)
kernel_name = 'mk_hybrid_d1_jaxref_r4_e04c9b'

def setup_inputs(seed: int=0):
    np.random.seed(seed)
    _w = jnp.asarray

    def _L0_attn_a_setup():
        import jax, jax.numpy as jnp
        import numpy as np
        B, S, HID = (1, 256, 512)
        H, DQK, DV = (16, 128, 128)
        K = 4
        SCALE = DQK ** (-0.5)

        def _dwconv_causal(x_btc, wk, bk, seq):
            y = jax.lax.conv_general_dilated(x_btc.transpose(0, 2, 1), wk, (1,), [(K - 1, K - 1)], dimension_numbers=('NCH', 'OIH', 'NCH'), feature_group_count=wk.shape[0])
            return (y[:, :, :seq] + bk[None, :, None]).transpose(0, 2, 1)

        def _kda_forward(x, Wq, Wk, Wv, Wa, ba, Wb, bb, Wg, Wo, qc_w, qc_b, kc_w, kc_b, vc_w, vc_b, ln_g, ln_b):
            Bb, Ss, _ = x.shape
            q = x @ Wq.T
            k = x @ Wk.T
            v = x @ Wv.T
            q = jax.nn.silu(_dwconv_causal(q, qc_w, qc_b, Ss))
            k = jax.nn.silu(_dwconv_causal(k, kc_w, kc_b, Ss))
            v = jax.nn.silu(_dwconv_causal(v, vc_w, vc_b, Ss))
            q = q.reshape(Bb, Ss, H, DQK)
            k = k.reshape(Bb, Ss, H, DQK) * SCALE
            v = v.reshape(Bb, Ss, H, DV)
            a = jax.nn.sigmoid(x @ Wa.T + ba).reshape(Bb, Ss, H, DV)
            beta = jax.nn.sigmoid(x @ Wb.T + bb)

            def step(St, inp):
                kt, qt, vt, at, bt = inp
                Sk = jnp.einsum('bhij,bhj->bhi', St, kt)
                err = Sk - vt
                Sn = at[..., None] * St - (bt[..., None] * err)[..., None] * kt[:, :, None, :]
                ot = jnp.einsum('bhij,bhj->bhi', Sn, qt)
                return (Sn, ot)
            tfirst = lambda u: u.transpose(1, 0, 2, 3)
            S0 = jnp.zeros((Bb, H, DV, DQK), x.dtype)
            _, outs = jax.lax.scan(step, S0, (tfirst(k), tfirst(q), tfirst(v), tfirst(a), beta.transpose(1, 0, 2)))
            out = outs.transpose(1, 0, 2, 3)
            mu = out.mean(-1, keepdims=True)
            var = out.var(-1, keepdims=True)
            o = (out - mu) * jax.lax.rsqrt(var + 1e-05) * ln_g + ln_b
            g = jax.nn.sigmoid(x @ Wg.T).reshape(Bb, Ss, H, DV)
            o = (o * g).reshape(Bb, Ss, H * DV)
            return o @ Wo.T
        key = jax.random.key(seed)
        ks = jax.random.split(key, 12)
        w = lambda i, shape, sc=0.02: jax.random.normal(ks[i], shape, jnp.float32) * sc
        return dict(x=jax.random.normal(ks[0], (B, S, HID), jnp.float32), Wq=w(1, (H * DQK, HID)), Wk=w(2, (H * DQK, HID)), Wv=w(3, (H * DV, HID)), Wa=w(4, (H * DV, HID)), ba=jnp.zeros((H * DV,), jnp.float32), Wb=w(5, (H, HID)), bb=jnp.zeros((H,), jnp.float32), Wg=w(6, (H * DV, HID)), Wo=w(7, (HID, H * DV)), qc_w=w(8, (H * DQK, 1, K), 0.2), qc_b=jnp.zeros((H * DQK,), jnp.float32), kc_w=w(9, (H * DQK, 1, K), 0.2), kc_b=jnp.zeros((H * DQK,), jnp.float32), vc_w=w(10, (H * DV, 1, K), 0.2), vc_b=jnp.zeros((H * DV,), jnp.float32), ln_g=jnp.ones((DV,), jnp.float32), ln_b=jnp.zeros((DV,), jnp.float32))
    _L0_attn_a_in = _L0_attn_a_setup()

    def _L0_attn_b_setup():
        import jax, jax.numpy as jnp
        import numpy as np
        import math
        NUM_HEADS = 16
        HEAVY_RATIO = 0.1
        RECENT_RATIO = 0.1
        ROPE_THETA = 10000.0

        def _rotate_half(x):
            d = x.shape[-1]
            return jnp.concatenate([-x[..., d // 2:], x[..., :d // 2]], axis=-1)

        def _rope(q, k, seq_len, head_dim, dtype):
            inv_freq = 1.0 / ROPE_THETA ** (jnp.arange(0, head_dim, 2, dtype=jnp.float32) / head_dim)
            pos = jnp.arange(seq_len, dtype=jnp.float32)
            freqs = pos[:, None] * inv_freq[None, :]
            emb = jnp.concatenate([freqs, freqs], axis=-1)
            cos = jnp.cos(emb).astype(dtype)[None, None]
            sin = jnp.sin(emb).astype(dtype)[None, None]
            q = q * cos + _rotate_half(q) * sin
            k = k * cos + _rotate_half(k) * sin
            return (q, k)
        key = jax.random.key(seed)
        ks = jax.random.split(key, 5)
        b, s, h = (1, 512, 512)
        return {'hidden_states': jax.random.normal(ks[0], (b, s, h), dtype=jnp.float32), 'Wq': jax.random.normal(ks[1], (h, h), dtype=jnp.float32) * 0.02, 'Wk': jax.random.normal(ks[2], (h, h), dtype=jnp.float32) * 0.02, 'Wv': jax.random.normal(ks[3], (h, h), dtype=jnp.float32) * 0.02, 'Wo': jax.random.normal(ks[4], (h, h), dtype=jnp.float32) * 0.02}
    _L0_attn_b_in = _L0_attn_b_setup()

    def _L0_ffn_setup():
        import jax, jax.numpy as jnp
        import numpy as np
        B, S, D, H = (4, 512, 512, 2048)

        def fwht(x):
            orig_shape = x.shape
            n = orig_shape[-1]
            x = x.reshape(-1, n)
            h = 1
            while h < n:
                xb = x.reshape(-1, n // (2 * h), 2, h)
                a = xb[:, :, 0, :]
                b = xb[:, :, 1, :]
                x = jnp.stack([a + b, a - b], axis=2).reshape(-1, n)
                h *= 2
            scale = jnp.asarray(1.0 / np.sqrt(n), dtype=x.dtype)
            return (x * scale).reshape(orig_shape)
        key = jax.random.key(seed)
        kx, k1, k2, k3 = jax.random.split(key, 4)
        x = jax.random.normal(kx, (B, S, D), dtype=jnp.float32)
        W1 = jax.random.normal(k1, (H, D), dtype=jnp.float32) * (1.0 / np.sqrt(D))
        W2 = jax.random.normal(k2, (D, H), dtype=jnp.float32) * (1.0 / np.sqrt(H))
        W3 = jax.random.normal(k3, (H, D), dtype=jnp.float32) * (1.0 / np.sqrt(D))
        return {'x': x, 'W1': W1, 'W2': W2, 'W3': W3}
    _L0_ffn_in = _L0_ffn_setup()
    _d = {'L0_attn_a_x': _L0_attn_a_in['x'], 'L0_attn_a_Wq': _L0_attn_a_in['Wq'], 'L0_attn_a_Wk': _L0_attn_a_in['Wk'], 'L0_attn_a_Wv': _L0_attn_a_in['Wv'], 'L0_attn_a_Wa': _L0_attn_a_in['Wa'], 'L0_attn_a_ba': _L0_attn_a_in['ba'], 'L0_attn_a_Wb': _L0_attn_a_in['Wb'], 'L0_attn_a_bb': _L0_attn_a_in['bb'], 'L0_attn_a_Wg': _L0_attn_a_in['Wg'], 'L0_attn_a_Wo': _L0_attn_a_in['Wo'], 'L0_attn_a_qc_w': _L0_attn_a_in['qc_w'], 'L0_attn_a_qc_b': _L0_attn_a_in['qc_b'], 'L0_attn_a_kc_w': _L0_attn_a_in['kc_w'], 'L0_attn_a_kc_b': _L0_attn_a_in['kc_b'], 'L0_attn_a_vc_w': _L0_attn_a_in['vc_w'], 'L0_attn_a_vc_b': _L0_attn_a_in['vc_b'], 'L0_attn_a_ln_g': _L0_attn_a_in['ln_g'], 'L0_attn_a_ln_b': _L0_attn_a_in['ln_b'], 'L0_attn_b_Wq': _L0_attn_b_in['Wq'], 'L0_attn_b_Wk': _L0_attn_b_in['Wk'], 'L0_attn_b_Wv': _L0_attn_b_in['Wv'], 'L0_attn_b_Wo': _L0_attn_b_in['Wo'], 'L0_ffn_W1': _L0_ffn_in['W1'], 'L0_ffn_W2': _L0_ffn_in['W2'], 'L0_ffn_W3': _L0_ffn_in['W3']}
    _x0 = _d['L0_attn_a_x']
    _d['L0_attn_a_x'] = jax.random.normal(jax.random.fold_in(jax.random.key(seed), 1), (1, 2048, 512), dtype=_x0.dtype)
    del _x0
    return _d

def reference(L0_attn_a_x, L0_attn_a_Wq, L0_attn_a_Wk, L0_attn_a_Wv, L0_attn_a_Wa, L0_attn_a_ba, L0_attn_a_Wb, L0_attn_a_bb, L0_attn_a_Wg, L0_attn_a_Wo, L0_attn_a_qc_w, L0_attn_a_qc_b, L0_attn_a_kc_w, L0_attn_a_kc_b, L0_attn_a_vc_w, L0_attn_a_vc_b, L0_attn_a_ln_g, L0_attn_a_ln_b, L0_attn_b_Wq, L0_attn_b_Wk, L0_attn_b_Wv, L0_attn_b_Wo, L0_ffn_W1, L0_ffn_W2, L0_ffn_W3):

    def _L0_attn_a_ref(x, Wq, Wk, Wv, Wa, ba, Wb, bb, Wg, Wo, qc_w, qc_b, kc_w, kc_b, vc_w, vc_b, ln_g, ln_b):
        import jax, jax.numpy as jnp
        import numpy as np
        B, S, HID = (1, 256, 512)
        H, DQK, DV = (16, 128, 128)
        K = 4
        SCALE = DQK ** (-0.5)

        def _dwconv_causal(x_btc, wk, bk, seq):
            y = jax.lax.conv_general_dilated(x_btc.transpose(0, 2, 1), wk, (1,), [(K - 1, K - 1)], dimension_numbers=('NCH', 'OIH', 'NCH'), feature_group_count=wk.shape[0])
            return (y[:, :, :seq] + bk[None, :, None]).transpose(0, 2, 1)

        def _kda_forward(x, Wq, Wk, Wv, Wa, ba, Wb, bb, Wg, Wo, qc_w, qc_b, kc_w, kc_b, vc_w, vc_b, ln_g, ln_b):
            Bb, Ss, _ = x.shape
            q = x @ Wq.T
            k = x @ Wk.T
            v = x @ Wv.T
            q = jax.nn.silu(_dwconv_causal(q, qc_w, qc_b, Ss))
            k = jax.nn.silu(_dwconv_causal(k, kc_w, kc_b, Ss))
            v = jax.nn.silu(_dwconv_causal(v, vc_w, vc_b, Ss))
            q = q.reshape(Bb, Ss, H, DQK)
            k = k.reshape(Bb, Ss, H, DQK) * SCALE
            v = v.reshape(Bb, Ss, H, DV)
            a = jax.nn.sigmoid(x @ Wa.T + ba).reshape(Bb, Ss, H, DV)
            beta = jax.nn.sigmoid(x @ Wb.T + bb)

            def step(St, inp):
                kt, qt, vt, at, bt = inp
                Sk = jnp.einsum('bhij,bhj->bhi', St, kt)
                err = Sk - vt
                Sn = at[..., None] * St - (bt[..., None] * err)[..., None] * kt[:, :, None, :]
                ot = jnp.einsum('bhij,bhj->bhi', Sn, qt)
                return (Sn, ot)
            tfirst = lambda u: u.transpose(1, 0, 2, 3)
            S0 = jnp.zeros((Bb, H, DV, DQK), x.dtype)
            _, outs = jax.lax.scan(step, S0, (tfirst(k), tfirst(q), tfirst(v), tfirst(a), beta.transpose(1, 0, 2)))
            out = outs.transpose(1, 0, 2, 3)
            mu = out.mean(-1, keepdims=True)
            var = out.var(-1, keepdims=True)
            o = (out - mu) * jax.lax.rsqrt(var + 1e-05) * ln_g + ln_b
            g = jax.nn.sigmoid(x @ Wg.T).reshape(Bb, Ss, H, DV)
            o = (o * g).reshape(Bb, Ss, H * DV)
            return o @ Wo.T
        return _kda_forward(x, Wq, Wk, Wv, Wa, ba, Wb, bb, Wg, Wo, qc_w, qc_b, kc_w, kc_b, vc_w, vc_b, ln_g, ln_b)

    def _L0_attn_b_ref(hidden_states, Wq, Wk, Wv, Wo):
        import jax, jax.numpy as jnp
        import numpy as np
        import math
        NUM_HEADS = 16
        HEAVY_RATIO = 0.1
        RECENT_RATIO = 0.1
        ROPE_THETA = 10000.0

        def _rotate_half(x):
            d = x.shape[-1]
            return jnp.concatenate([-x[..., d // 2:], x[..., :d // 2]], axis=-1)

        def _rope(q, k, seq_len, head_dim, dtype):
            inv_freq = 1.0 / ROPE_THETA ** (jnp.arange(0, head_dim, 2, dtype=jnp.float32) / head_dim)
            pos = jnp.arange(seq_len, dtype=jnp.float32)
            freqs = pos[:, None] * inv_freq[None, :]
            emb = jnp.concatenate([freqs, freqs], axis=-1)
            cos = jnp.cos(emb).astype(dtype)[None, None]
            sin = jnp.sin(emb).astype(dtype)[None, None]
            q = q * cos + _rotate_half(q) * sin
            k = k * cos + _rotate_half(k) * sin
            return (q, k)
        b, s, hidden = hidden_states.shape
        H = NUM_HEADS
        d = hidden // H

        def proj(W):
            return (hidden_states @ W.T).reshape(b, s, H, d).transpose(0, 2, 1, 3)
        q, k, v = (proj(Wq), proj(Wk), proj(Wv))
        q, k = _rope(q, k, s, d, hidden_states.dtype)
        scores = jnp.einsum('bhqd,bhkd->bhqk', q, k) / math.sqrt(d)
        neg = jnp.finfo(scores.dtype).min
        i = jnp.arange(s)[:, None]
        j = jnp.arange(s)[None, :]
        causal = jnp.where(j <= i, jnp.array(0.0, scores.dtype), neg)
        scores = jnp.maximum(scores + causal, neg)
        heavy_budget = int(HEAVY_RATIO * s)
        recent_budget = int(RECENT_RATIO * s)
        tmp_attn = jax.nn.softmax(scores.astype(jnp.float32), axis=-1).astype(scores.dtype)
        tmp_sum = jnp.sum(tmp_attn, axis=-2)
        _, topk_idx = jax.lax.top_k(tmp_sum, heavy_budget)
        heavy_mask = jnp.any(topk_idx[..., :, None] == jnp.arange(s)[None, None, None, :], axis=-2)
        band = jnp.abs(i - j) <= recent_budget
        mask = heavy_mask[:, :, None, :] | band[None, None]
        scores = jnp.where(mask, scores, neg)
        probs = jax.nn.softmax(scores.astype(jnp.float32), axis=-1).astype(q.dtype)
        attn = jnp.einsum('bhqk,bhkd->bhqd', probs, v)
        attn = attn.transpose(0, 2, 1, 3).reshape(b, s, hidden)
        return attn @ Wo.T

    def _L0_ffn_ref(x, W1, W2, W3):
        import jax, jax.numpy as jnp
        import numpy as np
        B, S, D, H = (4, 512, 512, 2048)

        def fwht(x):
            orig_shape = x.shape
            n = orig_shape[-1]
            x = x.reshape(-1, n)
            h = 1
            while h < n:
                xb = x.reshape(-1, n // (2 * h), 2, h)
                a = xb[:, :, 0, :]
                b = xb[:, :, 1, :]
                x = jnp.stack([a + b, a - b], axis=2).reshape(-1, n)
                h *= 2
            scale = jnp.asarray(1.0 / np.sqrt(n), dtype=x.dtype)
            return (x * scale).reshape(orig_shape)
        up_gate = jnp.einsum('bsd,hd->bsh', x, W1)
        up_lin = jnp.einsum('bsd,hd->bsh', x, W3)
        hidden = jax.nn.silu(up_gate) * up_lin
        hidden = fwht(hidden)
        out = jnp.einsum('bsh,dh->bsd', hidden, W2)
        return out
    x = L0_attn_a_x
    x = x + _L0_attn_a_ref(_layernorm(x, axis=-1), L0_attn_a_Wq, L0_attn_a_Wk, L0_attn_a_Wv, L0_attn_a_Wa, L0_attn_a_ba, L0_attn_a_Wb, L0_attn_a_bb, L0_attn_a_Wg, L0_attn_a_Wo, L0_attn_a_qc_w, L0_attn_a_qc_b, L0_attn_a_kc_w, L0_attn_a_kc_b, L0_attn_a_vc_w, L0_attn_a_vc_b, L0_attn_a_ln_g, L0_attn_a_ln_b)
    x = x + _L0_ffn_ref(_layernorm(x, axis=-1), L0_ffn_W1, L0_ffn_W2, L0_ffn_W3)
    x = x + _L0_attn_b_ref(_layernorm(x, axis=-1), L0_attn_b_Wq, L0_attn_b_Wk, L0_attn_b_Wv, L0_attn_b_Wo)
    x = x + _L0_ffn_ref(_layernorm(x, axis=-1), L0_ffn_W1, L0_ffn_W2, L0_ffn_W3)
    return x

_drawn_inputs = setup_inputs


def setup_inputs(seed=0):
    import zlib

    import numpy as np

    out = dict(_drawn_inputs(seed))
    spreads = {'L0_attn_a_ba': (0.0, 0.8),
     'L0_attn_a_bb': (0.0, 0.8),
     'L0_attn_a_qc_b': (0.0, 0.1),
     'L0_attn_a_kc_b': (0.0, 0.1),
     'L0_attn_a_vc_b': (0.0, 0.1),
     'L0_attn_a_ln_g': (1.0, 0.559),
     'L0_attn_a_ln_b': (0.0, 0.1)}
    factors = {'L0_attn_a_Wa': 3.209,
     'L0_attn_b_Wq': 8.0,
     'L0_attn_b_Wk': 8.0,
     'L0_attn_b_Wv': 4.495,
     'L0_attn_b_Wo': 4.386}
    for name, (base, spread) in spreads.items():
        noise = np.random.default_rng([zlib.crc32(name.encode()), seed]).standard_normal(out[name].shape)
        drawn = base * np.exp(spread * noise) if base else spread * noise
        out[name] = jnp.asarray(drawn.astype(out[name].dtype))
    for name, factor in factors.items():
        out[name] = (out[name] * factor).astype(out[name].dtype)
    return out
```

```python
import numpy as np
import concourse.bass as bass
from concourse import mybir
from contextlib import ExitStack

F32 = mybir.dt.float32
ALU = mybir.AluOpType
ACT = mybir.ActivationFunctionType
AX = mybir.AxisListType
P = 128
D = 512
KT = D // P
TOK = 512
EPS = 1e-5


class Memory:

    def __init__(self, nc, ctx, phase):
        self.nc, self.ctx, self.phase = nc, ctx, phase
        self.sems = []
        ctx.callback(self.release)

    def sb(self, name, shape):
        return self.ctx.enter_context(self.nc.sbuf_tensor(f"{self.phase}_{name}", shape, F32))

    def ps(self, name, shape):
        return self.ctx.enter_context(self.nc.psum_tensor(f"{self.phase}_{name}", shape, F32))

    def sem(self, name):
        self.sems.append(self.nc.alloc_semaphore(f"{self.phase}_{name}"))
        return self.sems[-1]

    def release(self):
        self.nc.clear_and_free_semaphores(self.sems)
        self.nc.all_engine_barrier()


def run_turns(eng, n, turn):
    turn(0)
    with eng.Fori(1, n) as i:
        turn(i)


def layernorm_phase(nc, phase, x, xnT, ident, T):
    NT = T // P
    with ExitStack() as ctx:
        m = Memory(nc, ctx, phase)
        xs = m.sb("xs", [P, NT, D])
        xn = m.sb("xn", [P, 2, D])
        xt = m.sb("xt", [P, 4, KT, P])
        idt = m.sb("ident", [P, P])
        stats = m.sb("stats", [P, NT, nc.vector.BN_STATS_DIM])
        mv = m.sb("mv", [P, NT, nc.vector.BN_AGGR_DIM])
        sd = m.sb("sd", [P, NT])
        rstd = m.sb("rstd", [P, NT])
        tr = m.ps("tr", [P, 2, KT, P])
        x_in = m.sem("x_in")
        ident_in = m.sem("ident_in")
        stat = m.sem("stat")
        var_ready = m.sem("var_ready")
        sd_ready = m.sem("sd_ready")
        rstd_ready = m.sem("rstd_ready")
        normed = m.sem("normed")
        turned = m.sem("turned")
        copied = m.sem("copied")
        stored = m.sem("stored")
        block = ctx.enter_context(nc.Block())

        @block.sync
        def _(sp):
            sp.dma_start(idt[:, :], ident).then_inc(ident_in, 16)
            sp.dma_start(xs[:, :, :], x.rearrange("(n p) d -> p n d", p=P)).then_inc(x_in, 16)
            for g in range(NT // 4):
                sp.wait_ge(copied, 4 * (g + 1))
                for k in range(KT):
                    sp.dma_start(xnT[k, :, g * 4 * P:(g + 1) * 4 * P].rearrange("p (n t) -> p n t", n=4),
                                 xt[:, :, k, :]).then_inc(stored, 16)
            sp.wait_ge(stored, 16 * KT * (NT // 4))

        @block.vector
        def _(dve):
            dve.wait_ge(x_in, 16)
            for n in range(NT):
                dve.bn_stats(stats[:, n, :], xs[:, n, :]).then_inc(stat, 1)
            for n in range(NT):
                dve.wait_ge(stat, n + 1)
                last = dve.bn_aggr(mv[:, n, :], stats[:, n, :])
            last.then_inc(stat, 1)
            dve.wait_ge(stat, NT + 1)
            dve.tensor_scalar(sd[:, :], mv[:, :, 1], EPS, None, ALU.add).then_inc(var_ready, 1)
            dve.wait_ge(sd_ready, 1)
            dve.reciprocal(rstd[:, :], sd[:, :]).then_inc(rstd_ready, 1)
            dve.wait_ge(rstd_ready, 1)
            for n in range(NT):
                if n >= 2:
                    dve.wait_ge(turned, n - 1)
                dve.tensor_scalar(xn[:, n % 2, :], xs[:, n, :], mv[:, n, 0:1], rstd[:, n:n + 1],
                                  ALU.subtract, ALU.mult).then_inc(normed, 1)

        @block.scalar
        def _(act):
            act.wait_ge(var_ready, 1)
            act.activation(sd[:, :], sd[:, :], ACT.Sqrt).then_inc(sd_ready, 1)
            for n in range(NT):
                act.wait_ge(turned, n + 1)
                if n >= 4:
                    act.wait_ge(stored, 16 * KT * (n // 4))
                act.activation(xt[:, n % 4], tr[:, n % 2], ACT.Copy).then_inc(copied, 1)

        @block.tensor
        def _(pe):
            pe.wait_ge(ident_in, 16)
            for n in range(NT):
                pe.wait_ge(normed, n + 1)
                if n >= 2:
                    pe.wait_ge(copied, n - 1)
                for k in range(KT):
                    t = pe.transpose(tr[:, n % 2, k, :], xn[:, n % 2, k * P:(k + 1) * P], idt[:, :])
                t.then_inc(turned, 1)


def project_phase(nc, xnT, w_kvqa, w_beta, conv_w, conv_b, a_bias, beta_bias, streams, beta_dram, T, H, scale):
    phase = "proj"
    TT = T // TOK
    TAPS = 4
    KB, QQ, KK, VB, AA = range(5)
    with ExitStack() as ctx:
        m = Memory(nc, ctx, phase)
        xn = m.sb("xn", [P, KT, T])
        w = m.sb("w", [P, 2, 4, KT, P])
        wb = m.sb("wb", [P, KT, H])
        cw = m.sb("cw", [P, 3, H, TAPS])
        cb = m.sb("cb", [P, 3, H])
        ab = m.sb("ab", [P, 2])
        bb = m.sb("bb", [H, 1])
        beta = m.sb("beta", [H, T])
        beta_rows = m.sb("beta_rows", [P, 2, T])
        raw = m.sb("raw", [P, 2, TAPS - 1 + T])
        y = m.sb("y", [P, 2, T])
        gate = m.sb("gate", [P, 2, T])
        res = m.sb("res", [P, 2, T])
        resb = m.sb("resb", [P, 2, T])
        decay = m.sb("decay", [P, 2, T])
        acc = m.ps("acc", [P, 8, TOK])
        params_in = m.sem("params_in")
        w_in = [m.sem("w_in0"), m.sem("w_in1")]
        beta_in = [m.sem("beta_in0"), m.sem("beta_in1")]
        zeroed = m.sem("zeroed")
        beta_mm = m.sem("beta_mm")
        beta_done = m.sem("beta_done")
        beta_stored = m.sem("beta_stored")
        unit_done = m.sem("unit_done")
        evacuated = m.sem("evacuated")
        conv_step = m.sem("conv_step")
        gated = m.sem("gated")
        res_done = m.sem("res_done")
        resb_done = m.sem("resb_done")
        res_stored = [m.sem("res_stored0"), m.sem("res_stored1")]
        resb_stored = [m.sem("resb_stored0"), m.sem("resb_stored1")]
        decay_stored = [m.sem("decay_stored0"), m.sem("decay_stored1")]
        block = ctx.enter_context(nc.Block())
        OUT = [KK, None, QQ]
        OUTB = [KB, VB, None]

        def evac0(j, t, TT):
            return max(j * TT + t - 7, 0)

        def res_count(i, s):
            before = sum(1 for r in range(s) if r % 2 == s % 2 and r % 3 != 1)
            return (i * 2 + before) * 16

        @block.sync
        def _(sp):
            for k in range(KT):
                sp.dma_start(xn[:, k, :], xnT[k]).then_inc(params_in, 16)
            sp.dma_start(wb[:, :, :], w_beta.rearrange("(k p) h -> p k h", p=P)).then_inc(params_in, 16)
            for j in range(3):
                sp.dma_start(cw[:, j], conv_w[j]).then_inc(params_in, 16)
            sp.dma_start(bb[:, :], beta_bias).then_inc(params_in, 16)
            for j in range(3):
                sp.dma_start(cb[:, j], conv_b[j]).then_inc(params_in, 16)

            def load(h, u):
                for j in range(4):
                    sp.dma_start(w[:, u, j], w_kvqa[j][:, bass.ds(h * P, P)].rearrange("(k p) c -> p k c", p=P)).then_inc(w_in[u], 16)
                sp.dma_start(ab[:, u:u + 1], a_bias[bass.ds(h, 1), :].rearrange("o p -> p o")).then_inc(w_in[u], 16)
                sp.dma_start(beta_rows[:, u, :], beta_dram[bass.ds(h, 1), :].to_broadcast([P, T])).then_inc(beta_in[u], 16)
            sp.wait_ge(beta_done, TT)
            sp.dma_start(beta_dram, beta[:, :]).then_inc(beta_stored, 16)
            sp.wait_ge(beta_stored, 16)
            load(0, 0)
            load(1, 1)

            def stores(i, u, ahead):
                h = i * 2 + u
                for j in range(3):
                    s = 3 * u + j
                    if OUT[j] is not None:
                        sp.wait_ge(res_done, i * 6 + s + 1)
                        sp.dma_start(streams[OUT[j]][bass.ds(h, 1)].rearrange("o p t -> p (o t)"), res[:, s % 2]).then_inc(res_stored[s % 2], 16)
                    if OUTB[j] is not None:
                        sp.wait_ge(resb_done, h * 2 + j + 1)
                        sp.dma_start(streams[OUTB[j]][bass.ds(h, 1)].rearrange("o p t -> p (o t)"), resb[:, s % 2]).then_inc(resb_stored[s % 2], 16)
                sp.wait_ge(evacuated, (h + 1) * 4 * TT)
                sp.dma_start(streams[AA][bass.ds(h, 1)].rearrange("o p t -> p (o t)"), decay[:, u]).then_inc(decay_stored[u], 16)
                if ahead:
                    load(h + 2, u)
            def turn(i):
                for u in range(2):
                    stores(i, u, True)
            run_turns(sp, H // 2 - 1, turn)
            for u in range(2):
                stores(H // 2 - 1, u, False)
            for u in range(2):
                sp.wait_ge(decay_stored[u], 16 * (H // 2))
                sp.wait_ge(res_stored[u], 16 * (H // 2) * 2)
                sp.wait_ge(resb_stored[u], 16 * (H // 2) * 2)

        @block.tensor
        def _(pe):
            pe.wait_ge(params_in, 16 * (KT + 1 + 3 + 3 + 1))
            for t in range(TT):
                for k in range(KT):
                    mm = pe.matmul(acc[0:H, 4 + t % 4, :], wb[:, k, :], xn[:, k, t * TOK:(t + 1) * TOK], start=(k == 0), stop=(k == KT - 1))
                mm.then_inc(beta_mm, 1)
            pe.wait_ge(beta_done, TT)
            def turn(i):
                for u in range(2):
                    pe.wait_ge(w_in[u], (i + 1) * 80)
                    for j in range(4):
                        for t in range(TT):
                            n = (i * 2 + u) * 4 * TT + j * TT + t
                            if u == 0 and j < 2:
                                pe.wait_ge(evacuated, i * (8 * TT) + evac0(j, t, TT))
                            else:
                                pe.wait_ge(evacuated, n - 7)
                            for k in range(KT):
                                mm = pe.matmul(acc[:, (j * TT + t) % 8, :], w[:, u, j, k, :],
                                               xn[:, k, t * TOK:(t + 1) * TOK], start=(k == 0), stop=(k == KT - 1))
                            mm.then_inc(unit_done, 1)
            run_turns(pe, H // 2, turn)

        @block.scalar
        def _(act):
            act.wait_ge(params_in, 16 * (KT + 1 + 3 + 3 + 1))
            for t in range(TT):
                act.wait_ge(beta_mm, t + 1)
                act.activation(beta[:, t * TOK:(t + 1) * TOK], acc[0:H, 4 + t % 4, :], ACT.Sigmoid, bias=bb[:, 0:1]).then_inc(beta_done, 1)
            act.wait_ge(zeroed, 2)

            def gate_unit(i, s):
                act.wait_ge(conv_step, (i * 6 + s + 1) * TAPS)
                if s >= 2:
                    act.wait_ge(res_done, i * 6 + s - 1)
                else:
                    act.wait_ge(res_done, i * 6)
                act.activation(gate[:, s % 2, :], y[:, s % 2, :], ACT.Sigmoid).then_inc(gated, 1)
            def turn(i):
                for u in range(2):
                    h = i * 2 + u
                    for j in range(4):
                        s = 3 * u + j
                        if j < 3:
                            if s >= 2:
                                act.wait_ge(conv_step, (i * 6 + s - 1) * TAPS)
                            else:
                                act.wait_ge(conv_step, (i * 6) * TAPS)
                        else:
                            act.wait_ge(decay_stored[u], i * 16)
                            act.wait_ge(w_in[u], (i + 1) * 80)
                        for t in range(TT):
                            n = h * 4 * TT + j * TT + t
                            act.wait_ge(unit_done, n + 1)
                            if j < 3:
                                lo = TAPS - 1 + t * TOK
                                act.activation(raw[:, s % 2, lo:lo + TOK], acc[:, (j * TT + t) % 8, :], ACT.Copy).then_inc(evacuated, 1)
                            else:
                                act.activation(decay[:, u, t * TOK:(t + 1) * TOK], acc[:, (j * TT + t) % 8, :], ACT.Sigmoid,
                                               bias=ab[:, u:u + 1]).then_inc(evacuated, 1)
                        if j < 3 and j > 0:
                            gate_unit(i, s - 1)
                    gate_unit(i, 3 * u + 2)
            run_turns(act, H // 2, turn)

        @block.vector
        def _(dve):
            for s in range(2):
                dve.memset(raw[:, s, 0:TAPS - 1], 0.0).then_inc(zeroed, 1)
            dve.wait_ge(params_in, 16 * (KT + 1 + 3 + 3 + 1))
            dve.wait_ge(zeroed, 2)

            def finish(i, s):
                j = s % 3
                dve.wait_ge(gated, i * 6 + s + 1)
                if s >= 2:
                    dve.wait_ge(resb_done, i * 4 + [0, 0, 1, 2, 2, 3][s] )
                else:
                    dve.wait_ge(resb_done, i * 4)
                dve.wait_ge(res_stored[s % 2], res_count(i, s))
                dve.scalar_tensor_tensor(res[:, s % 2, :], y[:, s % 2, :], scale if j == 0 else 1.0, gate[:, s % 2, :],
                                         ALU.mult, ALU.mult).then_inc(res_done, 1)

            def turn(i):
                for u in range(2):
                    for j in range(3):
                        s = 3 * u + j
                        h = i * 2 + u
                        dve.wait_ge(evacuated, h * 4 * TT + (j + 1) * TT)
                        dve.wait_ge(res_done, i * 6 + max(s - 1, 0))
                        for tap in range(TAPS):
                            src = raw[:, s % 2, tap:tap + T]
                            cwt = cw[:, j, bass.ds(h, 1), tap]
                            if tap == 0:
                                dve.tensor_scalar(y[:, s % 2, :], src, cwt, cb[:, j, bass.ds(h, 1)],
                                                  ALU.mult, ALU.add).then_inc(conv_step, 1)
                            else:
                                dve.wait_ge(conv_step, (i * 6 + s) * TAPS + tap)
                                dve.scalar_tensor_tensor(y[:, s % 2, :], src, cwt, y[:, s % 2, :],
                                                         ALU.mult, ALU.add).then_inc(conv_step, 1)
                        finish(i, s)
            run_turns(dve, H // 2, turn)

        @block.gpsimd
        def _(pool):
            def turn(i):
                for u in range(2):
                    for j in range(2):
                        s = 3 * u + j
                        if j == 0:
                            pool.wait_ge(beta_in[u], (i + 1) * 16)
                        pool.wait_ge(res_done, i * 6 + s + 1)
                        before = sum(1 for r in range(s) if r % 2 == s % 2 and r % 3 != 2)
                        pool.wait_ge(resb_stored[s % 2], (i * 2 + before) * 16)
                        pool.tensor_tensor(resb[:, s % 2, :], res[:, s % 2, :], beta_rows[:, u, :], ALU.mult).then_inc(resb_done, 1)
            run_turns(pool, H // 2, turn)


def mix_phase(nc, xnT, wg, o_dram, wo, ln_g, ln_b, x, x_out, T, H):
    phase = "mix"
    TT = T // TOK
    SUB = TOK // P
    with ExitStack() as ctx:
        m = Memory(nc, ctx, phase)
        wgs = m.sb("wg", [P, KT, H * P])
        wos = m.sb("wo", [P, H, D])
        xn = m.sb("xn", [P, KT, TOK])
        o = m.sb("o", [P, 4, TOK])
        oc = m.sb("oc", [P, 4, TOK])
        sq = m.sb("sq", [P, 2, TOK])
        sd = m.sb("sd", [P, 2, TOK])
        rs = m.sb("rs", [P, 2, TOK])
        sg = m.sb("sg", [P, 4, TOK])
        of = m.sb("of", [P, 2, TOK])
        mean_w = m.sb("mean_w", [P, P])
        gb = m.sb("gb", [P, 2])
        eps = m.sb("eps", [P, 1])
        xs = m.sb("xs", [P, 2, SUB, D])
        out_ps = m.ps("out", [P, SUB, D])
        g_ps = m.ps("g", [P, 2, TOK])
        mean_ps = m.ps("mean", [P, TOK])
        var_ps = m.ps("var", [P, TOK])
        w_in = m.sem("w_in")
        init = m.sem("init")
        xn_in = m.sem("xn_in")
        x_in = m.sem("x_in")
        o_in = [m.sem(f"o_in{i}") for i in range(4)]
        g_done = m.sem("g_done")
        mean_done = m.sem("mean_done")
        var_done = m.sem("var_done")
        out_done = m.sem("out_done")
        centred = m.sem("centred")
        squared = m.sem("squared")
        sd_done = m.sem("sd_done")
        sg_done = m.sem("sg_done")
        rs_done = m.sem("rs_done")
        norm_step = m.sem("norm_step")
        of_done = m.sem("of_done")
        added = m.sem("added")
        stored = m.sem("stored")
        block = ctx.enter_context(nc.Block())

        @block.sync
        def _(sp):
            for k in range(KT):
                sp.dma_start(wgs[:, k, :], wg[k * P:(k + 1) * P, :]).then_inc(w_in, 16)
            sp.dma_start(wos[:, :, :], wo.rearrange("(h p) n -> p h n", p=P)).then_inc(w_in, 16)
            sp.dma_start(gb[:, 0:1], ln_g).then_inc(w_in, 16)
            sp.dma_start(gb[:, 1:2], ln_b).then_inc(w_in, 16)
            def turn(i):
                sp.wait_ge(g_done, i * H)
                sp.dma_start(xn[:, :, :], xnT[:, :, bass.ds(i * TOK, TOK)].rearrange("k p t -> p k t")).then_inc(xn_in, 16)
                sp.wait_ge(stored, i * 16)
                sp.dma_start(xs[:, 0, :, :], x[bass.ds(i * TOK, TOK), :].rearrange("(s p) d -> p s d", p=P)).then_inc(x_in, 16)
                for h in range(H):
                    if h >= 4:
                        sp.wait_ge(centred, i * H + h - 3)
                    else:
                        sp.wait_ge(centred, i * H)
                    sp.dma_start(o[:, h % 4, :], o_dram[h, :, bass.ds(i * TOK, TOK)]).then_inc(o_in[h % 4], 16)
                sp.wait_ge(added, (i + 1) * SUB)
                sp.dma_start(x_out[bass.ds(i * TOK, TOK), :].rearrange("(s p) d -> p s d", p=P), xs[:, 1, :, :]).then_inc(stored, 16)
            run_turns(sp, TT, turn)
            sp.wait_ge(stored, 16 * TT)

        @block.tensor
        def _(pe):
            pe.wait_ge(w_in, 16 * (KT + 3))
            pe.wait_ge(init, 2)
            def turn(i):
                pe.wait_ge(xn_in, (i + 1) * 16)
                for n in range(H + 3):
                    if n < H:
                        h = n
                        if h < 2:
                            pe.wait_ge(sg_done, i * H)
                        else:
                            pe.wait_ge(sg_done, i * H + h - 1)
                        for k in range(KT):
                            mm = pe.matmul(g_ps[:, h % 2, :], wgs[:, k, h * P:(h + 1) * P], xn[:, k, :], start=(k == 0), stop=(k == KT - 1))
                        mm.then_inc(g_done, 1)
                        pe.wait_ge(o_in[h % 4], i * 64 + (h // 4 + 1) * 16)
                        pe.wait_ge(centred, i * H + h)
                        pe.matmul(mean_ps[:, :], mean_w[:, :], o[:, h % 4, :], start=True, stop=True).then_inc(mean_done, 1)
                    if 1 <= n <= H:
                        h = n - 1
                        pe.wait_ge(squared, i * H + h + 1)
                        pe.wait_ge(sd_done, i * H + h)
                        pe.matmul(var_ps[:, :], mean_w[:, :], sq[:, h % 2, :], start=True, stop=True).then_inc(var_done, 1)
                    if n >= 3:
                        h = n - 3
                        if h == 0:
                            pe.wait_ge(added, i * SUB)
                        pe.wait_ge(of_done, i * H + h + 1)
                        for s in range(SUB):
                            mm = pe.matmul(out_ps[:, s, :], of[:, h % 2, s * P:(s + 1) * P], wos[:, h, :], start=(h == 0), stop=(h == H - 1))
                        mm.then_inc(out_done, 1)
            run_turns(pe, TT, turn)

        @block.scalar
        def _(act):
            act.wait_ge(init, 2)
            def turn(i):
                for n in range(H + 1):
                    if n < H:
                        h = n
                        act.wait_ge(g_done, i * H + h + 1)
                        act.wait_ge(of_done, i * H + max(h - 3, 0))
                        act.activation(sg[:, h % 4, :], g_ps[:, h % 2, :], ACT.Sigmoid).then_inc(sg_done, 1)
                    if n >= 1:
                        h = n - 1
                        act.wait_ge(var_done, i * H + h + 1)
                        act.wait_ge(rs_done, i * H + max(h - 1, 0))
                        act.activation(sd[:, h % 2, :], var_ps[:, :], ACT.Sqrt, bias=eps[:, 0:1]).then_inc(sd_done, 1)
            run_turns(act, TT, turn)

        @block.gpsimd
        def _(pool):
            def turn(i):
                for h in range(H):
                    pool.wait_ge(centred, i * H + h + 1)
                    pool.wait_ge(var_done, i * H + max(h - 1, 0))
                    pool.tensor_tensor(sq[:, h % 2, :], oc[:, h % 4, :], oc[:, h % 4, :], ALU.mult).then_inc(squared, 1)
            run_turns(pool, TT, turn)

        @block.vector
        def _(dve):
            dve.memset(mean_w[:, :], 1.0 / P).then_inc(init, 1)
            dve.memset(eps[:, :], EPS).then_inc(init, 1)
            dve.wait_ge(w_in, 16 * (KT + 3))
            def turn(i):
                for n in range(H + 2):
                    if n < H:
                        h = n
                        dve.wait_ge(mean_done, i * H + h + 1)
                        dve.wait_ge(squared, i * H + max(h - 3, 0))
                        dve.wait_ge(of_done, i * H + max(h - 3, 0))
                        dve.tensor_tensor(oc[:, h % 4, :], o[:, h % 4, :], mean_ps[:, :], ALU.subtract).then_inc(centred, 1)
                    if n >= 2:
                        h = n - 2
                        g = i * H + h
                        dve.wait_ge(sd_done, g + 1)
                        dve.wait_ge(norm_step, i * H + max(h - 1, 0))
                        dve.reciprocal(rs[:, h % 2, :], sd[:, h % 2, :]).then_inc(rs_done, 1)
                        dve.wait_ge(rs_done, g + 1)
                        dve.scalar_tensor_tensor(oc[:, h % 4, :], oc[:, h % 4, :], gb[:, 0:1], rs[:, h % 2, :], ALU.mult, ALU.mult).then_inc(norm_step, 1)
                        dve.wait_ge(norm_step, g + 1)
                        dve.wait_ge(sg_done, g + 1)
                        dve.wait_ge(out_done, i * H + max(h - 1, 0))
                        dve.scalar_tensor_tensor(of[:, h % 2, :], oc[:, h % 4, :], gb[:, 1:2], sg[:, h % 4, :], ALU.add, ALU.mult).then_inc(of_done, 1)
                dve.wait_ge(out_done, (i + 1) * H)
                dve.wait_ge(x_in, (i + 1) * 16)
                dve.wait_ge(stored, i * 16)
                for s in range(SUB):
                    dve.tensor_tensor(xs[:, 1, s, :], xs[:, 0, s, :], out_ps[:, s, :], ALU.add).then_inc(added, 1)
            run_turns(dve, TT, turn)


def ffn_phase(nc, phase, xnT, w1, w3, w2, hadamard, x, x_out, T, F):
    TT = T // TOK
    SUB = TOK // P
    FB = F // P
    with ExitStack() as ctx:
        m = Memory(nc, ctx, phase)
        w1s = m.sb("w1", [P, KT, F])
        w3s = m.sb("w3", [P, KT, F])
        w2a = m.sb("w2a", [P, FB, D])
        w2b = m.sb("w2b", [P, FB, D])
        had = m.sb("had", [P, P])
        xn = m.sb("xn", [P, KT, TOK])
        gate = m.sb("gate", [P, 2, TOK])
        hid = m.sb("hid", [P, 2, TOK])
        xs = m.sb("xs", [P, SUB, D])
        out_ps = m.ps("out", [P, SUB, D])
        g_ps = m.ps("g", [P, 2, TOK])
        l_ps = m.ps("l", [P, 2, TOK])
        w2_in = m.sem("w2_in")
        w_in = m.sem("w_in")
        xn_in = m.sem("xn_in")
        x_in = m.sem("x_in")
        had_done = m.sem("had_done")
        had_copied = m.sem("had_copied")
        fly = m.sem("fly")
        gate_done = m.sem("gate_done")
        lin_done = m.sem("lin_done")
        silu_done = m.sem("silu_done")
        hid_done = m.sem("hid_done")
        out_done = m.sem("out_done")
        added = m.sem("added")
        stored = m.sem("stored")
        block = ctx.enter_context(nc.Block())

        @block.sync
        def _(sp):
            sp.dma_start(w2a[:, :, :], w2.rearrange("(f p) n -> p f n", p=P)).then_inc(w2_in, 16)
            sp.dma_start(had[:, :], hadamard).then_inc(w2_in, 16)
            for k in range(KT):
                sp.dma_start(w1s[:, k, :], w1[k * P:(k + 1) * P, :]).then_inc(w_in, 16)
                sp.dma_start(w3s[:, k, :], w3[k * P:(k + 1) * P, :]).then_inc(w_in, 16)
            def turn(i):
                sp.wait_ge(lin_done, i * FB)
                sp.dma_start(xn[:, :, :], xnT[:, :, bass.ds(i * TOK, TOK)].rearrange("k p t -> p k t")).then_inc(xn_in, 16)
                sp.wait_ge(stored, i * 16)
                sp.dma_start(xs[:, :, :], x[bass.ds(i * TOK, TOK), :].rearrange("(s p) d -> p s d", p=P)).then_inc(x_in, 16)
                sp.wait_ge(added, (i + 1) * SUB)
                sp.dma_start(x_out[bass.ds(i * TOK, TOK), :].rearrange("(s p) d -> p s d", p=P), xs[:, :, :]).then_inc(stored, 16)
            run_turns(sp, TT, turn)
            sp.wait_ge(stored, 16 * TT)

        @block.tensor
        def _(pe):
            pe.wait_ge(w2_in, 32)
            for f in range(FB):
                if f >= 4:
                    pe.wait_ge(had_copied, f - 3)
                pe.matmul(out_ps[:, f % 4, :], had[:, :], w2a[:, f, :], start=True, stop=True).then_inc(had_done, 1)
            pe.wait_ge(w_in, 16 * 2 * KT)
            pe.wait_ge(had_copied, FB)
            pe.wait_ge(fly, 8)
            def turn(i):
                pe.wait_ge(xn_in, (i + 1) * 16)
                for n in range(FB + 1):
                    if n < FB:
                        pe.wait_ge(silu_done, i * FB + max(n - 1, 0))
                        for k in range(KT):
                            mm = pe.matmul(g_ps[:, n % 2, :], w1s[:, k, n * P:(n + 1) * P], xn[:, k, :], start=(k == 0), stop=(k == KT - 1))
                        mm.then_inc(gate_done, 1)
                        pe.wait_ge(hid_done, i * FB + max(n - 1, 0))
                        for k in range(KT):
                            mm = pe.matmul(l_ps[:, n % 2, :], w3s[:, k, n * P:(n + 1) * P], xn[:, k, :], start=(k == 0), stop=(k == KT - 1))
                        mm.then_inc(lin_done, 1)
                    if n >= 1:
                        f = n - 1
                        if f == 0:
                            pe.wait_ge(added, i * SUB)
                        pe.wait_ge(hid_done, i * FB + f + 1)
                        for s in range(SUB):
                            mm = pe.matmul(out_ps[:, s, :], hid[:, f % 2, s * P:(s + 1) * P], w2b[:, f, :], start=(f == 0), stop=(f == FB - 1))
                        mm.then_inc(out_done, 1)
            run_turns(pe, TT, turn)

        @block.scalar
        def _(act):
            for f in range(FB):
                act.wait_ge(had_done, f + 1)
                act.activation(w2b[:, f, :], out_ps[:, f % 4, :], ACT.Copy, scale=float(F) ** -0.5).then_inc(had_copied, 1)
            def turn(i):
                for n in range(FB):
                    act.wait_ge(gate_done, i * FB + n + 1)
                    act.wait_ge(hid_done, i * FB + max(n - 1, 0))
                    act.activation(gate[:, n % 2, :], g_ps[:, n % 2, :], ACT.Silu).then_inc(silu_done, 1)
            run_turns(act, TT, turn)

        @block.vector
        def _(dve):
            dve.wait_ge(had_copied, FB)
            src, dst = w2b, w2a
            for stage in range(4):
                step = 1 << stage
                dve.wait_ge(fly, 2 * stage)
                s = src[:, :, :].rearrange("p (a two b) n -> p a two (b n)", two=2, b=step)
                d = dst[:, :, :].rearrange("p (a two b) n -> p a two (b n)", two=2, b=step)
                dve.tensor_tensor(d[:, :, 0], s[:, :, 0], s[:, :, 1], ALU.add).then_inc(fly, 1)
                dve.tensor_tensor(d[:, :, 1], s[:, :, 0], s[:, :, 1], ALU.subtract).then_inc(fly, 1)
                src, dst = dst, src
            def turn(i):
                for n in range(FB):
                    dve.wait_ge(silu_done, i * FB + n + 1)
                    dve.wait_ge(lin_done, i * FB + n + 1)
                    dve.wait_ge(out_done, i * FB + max(n - 1, 0))
                    dve.tensor_tensor(hid[:, n % 2, :], gate[:, n % 2, :], l_ps[:, n % 2, :], ALU.mult).then_inc(hid_done, 1)
                dve.wait_ge(out_done, (i + 1) * FB)
                dve.wait_ge(x_in, (i + 1) * 16)
                for s in range(SUB):
                    dve.tensor_tensor(xs[:, s, :], xs[:, s, :], out_ps[:, s, :], ALU.add).then_inc(added, 1)
            run_turns(dve, TT, turn)


H = 16
C = 16
RING = 128
CHUNK = RING // 2
BPC = CHUNK // C
BPR = RING // C
GH = P // C
ROWS = 4
NR = C // ROWS
KB, QQ, KK, VB, AA = range(5)


def scan_phase(nc, streams, o_dram, ident, head_mask, T):
    NB = T // C
    TURNS = T // RING
    with ExitStack() as ctx:
        m = Memory(nc, ctx, "scan")
        sb, ps, sem = m.sb, m.ps, m.sem
        ring = sb("ring", [P, 5, H, RING])
        blk = sb("blk", [P, 2, 5, C, H])
        stage = sb("stage", [P, 2, ROWS * ROWS * H * (NR * (NR + 1) // 2)])
        pairs = sb("pairs", [P, 2, 2, C, C + 1, H])
        ud = sb("ud", [P, C + 1, C + 1, H])
        prod = sb("prod", [P, C * H])
        red = sb("red", [P, H])
        ktin = sb("ktin", [P, 2, C, GH])
        utin = sb("utin", [P, 2, C, GH])
        S = sb("S", [P, H, P])
        ST = sb("ST", [P, H, P])
        kbd = sb("kbd", [P, 2, GH, P])
        uT = sb("uT", [P, 2, P])
        oring = sb("oring", [P, H, RING])
        idt = sb("idt", [P, P])
        ones = sb("ones", [P, P])
        hmask = sb("hmask", [P, GH])

        bc_ps = ps("bc_ps", [P, 2, 512])
        pq_ps = ps("pq_ps", [P, H, 2, C])
        tr_ps = ps("tr_ps", [P, 4, P])
        ds_ps = ps("ds_ps", [P, 2, 4, P])
        st_ps = ps("st_ps", [P, 2, 4, P])

        const_in = sem("const_in")
        init_done = sem("init_done")
        ud_zeroed = sem("ud_zeroed")
        chunk_in = [sem("chunk_in0"), sem("chunk_in1")]
        blk_ready = sem("blk_ready")
        kk_staged = sem("kk_staged")
        qk_staged = sem("qk_staged")
        bcast_done = sem("bcast_done")
        bcast_evac = sem("bcast_evac")
        kt_done = sem("kt_done")
        kbd_ready = sem("kbd_ready")
        pq_done = sem("pq_done")
        pq_copied = sem("pq_copied")
        u_step = sem("u_step")
        dec_step = sem("dec_step")
        dot_step = sem("dot_step")
        ut_done = sem("ut_done")
        u_grouped = sem("u_grouped")
        ut_copied = sem("ut_copied")
        ds_done = sem("ds_done")
        s_decayed = sem("s_decayed")
        s_added = sem("s_added")
        st_done = sem("st_done")
        st_evac = sem("st_evac")
        po_done = sem("po_done")
        o_reduced = sem("o_reduced")
        o_stored = [sem("o_stored0"), sem("o_stored1")]
        NINIT = 4
        soff = [ROWS * ROWS * H * (r * (r + 1) // 2) for r in range(NR)]
        npair = [ROWS * (r + 1) for r in range(NR)]

        def stage_rows(eng, w, r, u):
            n = npair[r]
            left = blk[:, u % 2, w, ROWS * r:ROWS * (r + 1), :].unsqueeze(2).to_broadcast([P, ROWS, n, H])
            right = blk[:, u % 2, KK, 0:n, :].unsqueeze(1).to_broadcast([P, ROWS, n, H])
            out = stage[:, w, soff[r]:soff[r] + ROWS * n * H].rearrange("p (t j h) -> p t j h", t=ROWS, h=H)
            return eng.tensor_tensor(out, left, right, ALU.mult)

        def run(eng, prologue, body):
            prologue()
            for u in range(BPR):
                body(0, u, False)
            with eng.Fori(1, TURNS - 1) as it:
                for u in range(BPR):
                    body(it, u, False)
            for u in range(BPR):
                body(TURNS - 1, u, u == BPR - 1)

        block = ctx.enter_context(nc.Block())

        @block.sync
        def _(sp):
            sp.dma_start(idt[:, :], ident).then_inc(const_in, 16)
            sp.dma_start(hmask[:, :], head_mask).then_inc(const_in, 16)

            def load(it, half):
                for w in range(5):
                    sp.dma_start(ring[:, w, :, half * CHUNK:(half + 1) * CHUNK],
                                 streams[w][:, :, bass.ds(it * RING + half * CHUNK, CHUNK)]
                                 .rearrange("h p t -> p h t")).then_inc(chunk_in[half], 16)

            def store(it, half):
                sp.wait_ge(o_reduced, ((it * 2 + half + 1) * BPC) * NR)
                sp.dma_start(o_dram[:, :, bass.ds(it * RING + half * CHUNK, CHUNK)]
                             .rearrange("h p t -> p h t"),
                             oring[:, :, half * CHUNK:(half + 1) * CHUNK]).then_inc(o_stored[half], 16)
            load(0, 0)
            load(0, 1)
            with sp.Fori(0, TURNS - 1) as it:
                for half in range(2):
                    sp.wait_ge(blk_ready, (it * 2 + half + 1) * BPC)
                    load(it + 1, half)
                    store(it, half)
            for half in range(2):
                store(TURNS - 1, half)
                sp.wait_ge(o_stored[half], 16 * TURNS)

        @block.scalar
        def _(act):
            def copy_block(it, u):
                it, u = (it + 1, 0) if u == BPR else (it, u)
                b = it * BPR + u
                act.wait_ge(chunk_in[u // BPC], 80 * (it + 1))
                if not (isinstance(b, int) and b < 1):
                    act.wait_ge(kt_done, b)
                if not (isinstance(b, int) and b < 2):
                    act.wait_ge(pq_done, b - 1)
                    act.wait_ge(u_step, C * (b - 1))
                    act.wait_ge(dec_step, C * (b - 1))
                act.activation(blk[:, u % 2].rearrange("p w t h -> p w h t"),
                               ring[:, :, :, u * C:(u + 1) * C], ACT.Copy)
                for g in range(2):
                    last = act.activation(ktin[:, g].rearrange("p t h -> p h t"),
                                          ring[:, KK, g * GH:(g + 1) * GH, u * C:(u + 1) * C], ACT.Copy)
                last.then_inc(blk_ready, 1)

            def spread(it, u):
                it, u = (it + 1, 0) if u == BPR else (it, u)
                b = it * BPR + u
                n = 0
                for r in range(NR):
                    for w in range(2):
                        for p in range(2):
                            act.wait_ge(bcast_done, 16 * b + n + 1)
                            t = r * ROWS + 2 * p
                            act.activation(pairs[:, u % 2, w, t:t + 2, 1:1 + npair[r], :],
                                           bc_ps[:, n % 2, 0:2 * npair[r] * H]
                                           .rearrange("p (t j h) -> p t j h", t=2, h=H),
                                           ACT.Copy).then_inc(bcast_evac, 1)
                            n += 1

            def block_diagonal(it, u):
                it, u = (it + 1, 0) if u == BPR else (it, u)
                b = it * BPR + u
                act.wait_ge(kt_done, b + 1)
                if not (isinstance(b, int) and b < 1):
                    act.wait_ge(ds_done, 4 * b)
                for g in range(2):
                    for h in range(GH):
                        last = act.activation(kbd[:, g, h, :], tr_ps[:, g, :], ACT.Copy,
                                              scale=hmask[:, h:h + 1])
                last.then_inc(kbd_ready, 1)

            def prologue():
                act.wait_ge(const_in, 32)
                act.wait_ge(init_done, NINIT)
                for q in range(4):
                    act.activation(ST[:, 4 * q:4 * q + 4, :], S[:, 4 * q:4 * q + 4, :], ACT.Copy).then_inc(st_evac, 1)
                copy_block(0, 0)
                spread(0, 0)
                block_diagonal(0, 0)

            def body(it, u, last):
                b = it * BPR + u
                act.wait_ge(pq_done, b + 1)
                for w in range(2):
                    c = act.activation(pairs[:, u % 2, w, :, 0, :].rearrange("p t h -> p h t"),
                                       pq_ps[:, :, w, :], ACT.Copy)
                c.then_inc(pq_copied, 1)
                if not last:
                    copy_block(it, u + 1)
                    spread(it, u + 1)
                act.wait_ge(ut_done, b + 1)
                act.activation(uT[:, :, :], tr_ps[:, 2:4, :], ACT.Copy).then_inc(ut_copied, 1)
                for q in range(4):
                    act.wait_ge(st_done, 4 * b + q + 1)
                    act.activation(ST[:, 4 * q:4 * q + 4, :], st_ps[:, q % 2], ACT.Copy).then_inc(st_evac, 1)
                if not last:
                    block_diagonal(it, u + 1)
            run(act, prologue, body)

        @block.tensor
        def _(pe):
            def prep(it, u):
                it, u = (it + 1, 0) if u == BPR else (it, u)
                b = it * BPR + u
                pe.wait_ge(blk_ready, b + 1)
                if not (isinstance(b, int) and b < 1):
                    pe.wait_ge(kbd_ready, b)
                for g in range(2):
                    tr = pe.transpose(tr_ps[:, g, :], ktin[:, g].rearrange("p t h -> p (t h)"), idt[:, :])
                tr.then_inc(kt_done, 1)
                n = 0
                for r in range(NR):
                    for w in range(2):
                        pe.wait_ge((kk_staged, qk_staged)[w], NR * b + r + 1)
                        for p in range(2):
                            if isinstance(b, int) and 16 * b + n < 2:
                                pass
                            else:
                                pe.wait_ge(bcast_evac, 16 * b + n - 1)
                            m = 2 * npair[r] * H
                            pe.matmul(bc_ps[:, n % 2, 0:m], ones[:, :],
                                      stage[:, w, soff[r] + p * m:soff[r] + (p + 1) * m],
                                      start=True, stop=True).then_inc(bcast_done, 1)
                            n += 1

            def prologue():
                pe.wait_ge(const_in, 32)
                pe.wait_ge(init_done, NINIT)
                prep(0, 0)

            def body(it, u, last):
                b = it * BPR + u
                first = isinstance(b, int) and b == 0
                if not first:
                    pe.wait_ge(pq_copied, b)
                for q in range(4):
                    pe.wait_ge(st_evac, 4 * b + q + 1)
                    for h in range(4 * q, 4 * q + 4):
                        m = pe.matmul(pq_ps[:, h], ST[:, h, :], blk[:, u % 2, 0:2, :, h], start=True, stop=True)
                m.then_inc(pq_done, 1)
                if not last:
                    prep(it, u + 1)
                pe.wait_ge(u_grouped, b + 1)
                for g in range(2):
                    tr = pe.transpose(tr_ps[:, 2 + g, :], utin[:, g].rearrange("p t h -> p (t h)"), idt[:, :])
                tr.then_inc(ut_done, 1)
                pe.wait_ge(ut_copied, b + 1)
                pe.wait_ge(kbd_ready, b + 1)

                def rank_update(q):
                    if q >= 2:
                        pe.wait_ge(s_added, 4 * b + q - 1)
                    pe.matmul(ds_ps[:, q % 2], uT[:, q // 2, :],
                              kbd[:, q // 2, 4 * (q % 2):4 * (q % 2) + 4, :], start=True, stop=True).then_inc(ds_done, 1)

                def turn(q):
                    pe.wait_ge(s_added, 4 * b + q + 1)
                    if q >= 2:
                        pe.wait_ge(st_evac, 4 * (b + 1) + q - 1)
                    for h in range(4):
                        t = pe.transpose(st_ps[:, q % 2, h, :], S[:, 4 * q + h, :], idt[:, :])
                    t.then_inc(st_done, 1)
                rank_update(0)
                rank_update(1)
                turn(0)
                rank_update(2)
                turn(1)
                rank_update(3)
                turn(2)
                turn(3)
            run(pe, prologue, body)

        @block.gpsimd
        def _(pool):
            def stage_kk(it, u):
                it, u = (it + 1, 0) if u == BPR else (it, u)
                b = it * BPR + u
                pool.wait_ge(blk_ready, b + 1)
                for r in range(NR):
                    if not (isinstance(b, int) and b < 1):
                        pool.wait_ge(bcast_done, 16 * (b - 1) + 4 * r + 2)
                    stage_rows(pool, 0, r, u).then_inc(kk_staged, 1)

            def prologue():
                pool.memset(ud[:, :, :, :], 0.0).then_inc(ud_zeroed, 1)
                pool.wait_ge(ud_zeroed, 1)
                pool.memset(ud[:, 0, 0, :], 1.0).then_inc(init_done, 1)
                pool.memset(pairs[:, :, :, :, :, :], 0.0).then_inc(init_done, 1)
                pool.wait_ge(init_done, NINIT)
                stage_kk(0, 0)

            def body(it, u, last):
                b = it * BPR + u
                first = isinstance(b, int) and b == 0
                if not last:
                    stage_kk(it, u + 1)
                if not first:
                    pool.wait_ge(s_decayed, 4 * b)
                    pool.wait_ge(po_done, NR * b)
                    pool.wait_ge(u_grouped, b)
                    pool.wait_ge(u_step, C * b)
                for t in range(C):
                    if t:
                        pool.wait_ge(u_step, C * b + t)
                        pool.wait_ge(dec_step, C * b + t)
                    pool.tensor_tensor(ud[:, t + 1, 0:t + 1, :], ud[:, t, 0:t + 1, :],
                                       blk[:, u % 2, AA, t, :].unsqueeze(1).to_broadcast([P, t + 1, H]),
                                       ALU.mult).then_inc(dec_step, 1)
                pool.wait_ge(u_step, C * (b + 1))
                pool.wait_ge(dec_step, C * (b + 1))
                for r in range(NR):
                    t, n = ROWS * r, ROWS * (r + 1) + 1
                    pool.tensor_tensor(pairs[:, u % 2, 1, t:t + ROWS, 0:n, :], pairs[:, u % 2, 1, t:t + ROWS, 0:n, :],
                                       ud[:, t + 1:t + 1 + ROWS, 0:n, :], ALU.mult).then_inc(po_done, 1)
            run(pool, prologue, body)

        @block.vector
        def _(dve):
            def stage_qk(it, u):
                it, u = (it + 1, 0) if u == BPR else (it, u)
                b = it * BPR + u
                dve.wait_ge(blk_ready, b + 1)
                for r in range(NR):
                    if not (isinstance(b, int) and b < 1):
                        dve.wait_ge(bcast_done, 16 * (b - 1) + 4 * r + 4)
                    stage_rows(dve, 1, r, u).then_inc(qk_staged, 1)

            def prologue():
                dve.memset(S[:, :, :], 0.0).then_inc(init_done, 1)
                dve.memset(ones[:, :], 1.0).then_inc(init_done, 1)
                dve.wait_ge(init_done, NINIT)
                stage_qk(0, 0)

            def body(it, u, last):
                b = it * BPR + u
                first = isinstance(b, int) and b == 0
                if not last:
                    stage_qk(it, u + 1)
                dve.wait_ge(pq_copied, b + 1)
                dve.wait_ge(bcast_evac, 16 * (b + 1))
                if not first:
                    dve.wait_ge(po_done, NR * b)
                    dve.wait_ge(ut_done, b)
                for t in range(C):
                    if not (first and t == 0):
                        dve.wait_ge(dec_step, C * b + t)
                        dve.wait_ge(u_step, C * b + t)
                    n = (t + 1) * H
                    step = C * b + t
                    dve.tensor_tensor(prod[:, 0:n].rearrange("p (s h) -> p s h", h=H),
                                      pairs[:, u % 2, 0, t, 0:t + 1, :], ud[:, t, 0:t + 1, :],
                                      ALU.mult).then_inc(dot_step, 1)
                    dve.wait_ge(dot_step, 2 * step + 1)
                    dve.tensor_reduce(red[:, :], prod[:, 0:n].rearrange("p (s h) -> p h s", h=H),
                                      AX.X, ALU.add).then_inc(dot_step, 1)
                    dve.wait_ge(dot_step, 2 * step + 2)
                    dve.tensor_tensor(ud[:, t + 1, t + 1, :], blk[:, u % 2, VB, t, :], red[:, :],
                                      ALU.subtract).then_inc(u_step, 1)
                dve.wait_ge(dec_step, C * (b + 1))
                dve.wait_ge(u_step, C * (b + 1))
                dve.tensor_copy(utin[:, :, :, :].rearrange("p g t h -> p t g h"),
                                ud[:, C, 1:C + 1, :].rearrange("p t (g h) -> p t g h", g=2)).then_inc(u_grouped, 1)
                if not first:
                    dve.wait_ge(st_done, 4 * b)
                for q in range(4):
                    h = slice(4 * q, 4 * q + 4)
                    dve.tensor_tensor(S[:, h, :], S[:, h, :],
                                      ud[:, C, 0, h].unsqueeze(2).to_broadcast([P, 4, P]),
                                      ALU.mult).then_inc(s_decayed, 1)
                for q in range(4):
                    h = slice(4 * q, 4 * q + 4)
                    dve.wait_ge(s_decayed, 4 * b + q + 1)
                    dve.wait_ge(ds_done, 4 * b + q + 1)
                    dve.tensor_tensor(S[:, h, :], S[:, h, :], ds_ps[:, q % 2], ALU.add).then_inc(s_added, 1)
                half = u // BPC
                if u % BPC == 0 and not (isinstance(it, int) and it == 0):
                    dve.wait_ge(o_stored[half], 16 * it)
                for r in range(NR):
                    t, n = ROWS * r, ROWS * (r + 1) + 1
                    dve.wait_ge(po_done, NR * b + r + 1)
                    dve.tensor_reduce(oring[:, :, u * C + t:u * C + t + ROWS].rearrange("p h t -> p t h"),
                                      pairs[:, u % 2, 1, t:t + ROWS, 0:n, :].rearrange("p t s h -> p t h s"),
                                      AX.X, ALU.add).then_inc(o_reduced, 1)
            run(dve, prologue, body)


NEG = -1.0e30
FIRST_BIG = 1.0e30


def rope_phase(nc, xnT, w_rot, wv, cos, sin, qk_dram, v_dram, T):
    phase = "rope"
    TT = T // TOK
    NT = T // P
    CB = D // P
    with ExitStack() as ctx:
        m = Memory(nc, ctx, phase)
        xn = m.sb("xn", [P, KT, T])
        w = m.sb("w", [P, 4, KT, D])
        wvs = m.sb("wv", [P, KT, D])
        tab = m.sb("tab", [P, 2, T])
        part = m.sb("part", [P, 2, 2, TOK])
        rot = m.sb("rot", [P, 4, TOK])
        vrow = m.sb("vrow", [P, 4, D])
        acc = m.ps("acc", [P, 3, 2, TOK])
        v_ps = m.ps("v_ps", [P, 2, D])
        loaded = m.sem("loaded")
        pair_done = m.sem("pair_done")
        turned = m.sem("turned")
        rot_done = m.sem("rot_done")
        rot_stored = [m.sem(f"rot_stored{i}") for i in range(4)]
        v_done = m.sem("v_done")
        v_copied = m.sem("v_copied")
        v_stored = [m.sem(f"v_stored{i}") for i in range(4)]
        NLOAD = 2 * KT + 4 * KT + 2
        units = [(c, j, t) for c in range(CB) for j in range(2) for t in range(TT)]
        block = ctx.enter_context(nc.Block())

        @block.sync
        def _(sp):
            for k in range(KT):
                sp.dma_start(xn[:, k, :], xnT[k]).then_inc(loaded, 16)
                sp.dma_start(wvs[:, k, :], wv[k * P:(k + 1) * P, :]).then_inc(loaded, 16)
                for j in range(4):
                    sp.dma_start(w[:, j, k, :], w_rot[j][k * P:(k + 1) * P, :]).then_inc(loaded, 16)
            sp.dma_start(tab[:, 0, :], cos).then_inc(loaded, 16)
            sp.dma_start(tab[:, 1, :], sin).then_inc(loaded, 16)
            for n, (c, j, t) in enumerate(units):
                sp.wait_ge(rot_done, n + 1)
                sp.dma_start(qk_dram[j, c * P:(c + 1) * P, t * TOK:(t + 1) * TOK], rot[:, n % 4, :]).then_inc(rot_stored[n % 4], 16)
                if n % 2:
                    v = n // 2
                    sp.wait_ge(v_copied, v + 1)
                    sp.dma_start(v_dram[v * P:(v + 1) * P, :], vrow[:, v % 4, :]).then_inc(v_stored[v % 4], 16)
            for r in range(4):
                sp.wait_ge(rot_stored[r], 16 * (len(units) // 4))
                sp.wait_ge(v_stored[r], 16 * (NT // 4))

        @block.tensor
        def _(pe):
            pe.wait_ge(loaded, 16 * NLOAD)
            for n, (c, j, t) in enumerate(units):
                if n >= 3:
                    pe.wait_ge(rot_done, n - 2)
                for r in range(2):
                    for k in range(KT):
                        mm = pe.matmul(acc[:, n % 3, r, :], w[:, 2 * j + r, k, c * P:(c + 1) * P],
                                       xn[:, k, t * TOK:(t + 1) * TOK], start=(k == 0), stop=(k == KT - 1))
                mm.then_inc(pair_done, 1)
                if n % 2:
                    v = n // 2
                    if v >= 2:
                        pe.wait_ge(v_copied, v - 1)
                    for k in range(KT):
                        mm = pe.matmul(v_ps[:, v % 2, :], xn[:, k, v * P:(v + 1) * P], wvs[:, k, :], start=(k == 0), stop=(k == KT - 1))
                    mm.then_inc(v_done, 1)

        @block.vector
        def _(dve):
            dve.wait_ge(loaded, 16 * NLOAD)
            for n, (c, j, t) in enumerate(units):
                dve.wait_ge(pair_done, n + 1)
                if n >= 2:
                    dve.wait_ge(rot_done, n - 1)
                for r in range(2):
                    dve.tensor_tensor(part[:, n % 2, r, :], acc[:, n % 3, r, :], tab[:, r, t * TOK:(t + 1) * TOK], ALU.mult).then_inc(turned, 1)
                dve.wait_ge(turned, 2 * n + 2)
                if n >= 4:
                    dve.wait_ge(rot_stored[n % 4], 16 * (n // 4))
                dve.tensor_tensor(rot[:, n % 4, :], part[:, n % 2, 0, :], part[:, n % 2, 1, :], ALU.add).then_inc(rot_done, 1)

        @block.scalar
        def _(act):
            for v in range(NT):
                act.wait_ge(v_done, v + 1)
                if v >= 4:
                    act.wait_ge(v_stored[v % 4], 16 * (v // 4))
                act.activation(vrow[:, v % 4, :], v_ps[:, v % 2, :], ACT.Copy).then_inc(v_copied, 1)


def chunks_of(q):
    n = (q + 1) * P
    return [(c, min(TOK, n - c)) for c in range(0, n, TOK)]


def column_sum_phase(nc, qk_dram, causal, sums, T, NH, DH):
    phase = "csum"
    NT = T // P
    NC = T // TOK
    SCALE = float(DH) ** -0.5
    order = list(range(NT - 1, -1, -1))
    with ExitStack() as ctx:
        m = Memory(nc, ctx, phase)
        qk = m.sb("qk", [DH, 2, 2, T])
        cm = m.sb("cm", [P, P])
        e = m.sb("e", [P, 2, T])
        mx = m.sb("mx", [P, 2])
        nb = m.sb("nb", [P, 2])
        rsum = m.sb("rsum", [P, 2])
        rinv = m.sb("rinv", [P, 2])
        tot = m.sb("tot", [P, T])
        ones = m.sb("ones", [P, 1])
        row = m.sb("row", [1, T])
        sc = m.ps("sc", [P, 2, T])
        cm_in = m.sem("cm_in")
        init = m.sem("init")
        qk_in = [m.sem("qk_in0"), m.sem("qk_in1")]
        scored = m.sem("scored")
        masked = m.sem("masked")
        maxed = m.sem("maxed")
        biased = m.sem("biased")
        expd = m.sem("expd")
        inverted = m.sem("inverted")
        totalled = m.sem("totalled")
        summed = m.sem("summed")
        row_done = m.sem("row_done")
        row_stored = m.sem("row_stored")
        block = ctx.enter_context(nc.Block())
        TILES = NT

        @block.sync
        def _(sp):
            sp.dma_start(cm[:, :], causal).then_inc(cm_in, 16)

            def load(h, u):
                for j in range(2):
                    sp.dma_start(qk[:, u, j, :], qk_dram[j, bass.ds(h * DH, DH), :]).then_inc(qk_in[u], 16)
            load(0, 0)
            load(1, 1)
            def turn(i):
                for u in range(2):
                    sp.wait_ge(summed, i * 2 + u + 1)
                    load(i * 2 + u + 2, u)
                    sp.wait_ge(row_done, i * 2 + u + 1)
                    sp.dma_start(sums[bass.ds(i * 2 + u, 1), :], row[:, :]).then_inc(row_stored, 16)
            run_turns(sp, NH // 2 - 1, turn)
            for u in range(2):
                sp.wait_ge(row_done, NH - 1 + u)
                sp.dma_start(sums[NH - 2 + u:NH - 1 + u, :], row[:, :]).then_inc(row_stored, 16)
            sp.wait_ge(row_stored, 16 * NH)

        @block.tensor
        def _(pe):
            pe.wait_ge(init, 1)
            def turn(i):
                for u in range(2):
                    h = i * 2 + u
                    pe.wait_ge(qk_in[u], (i + 1) * 32)
                    for n, q in enumerate(order):
                        g = h * TILES + n
                        if n >= 2:
                            pe.wait_ge(expd, g - 1)
                        else:
                            pe.wait_ge(expd, h * TILES)
                            pe.wait_ge(row_done, h)
                        for c, w in chunks_of(q):
                            mm = pe.matmul(sc[:, n % 2, c:c + w], qk[:, u, 0, q * P:(q + 1) * P], qk[:, u, 1, c:c + w], start=True, stop=True)
                        mm.then_inc(scored, 1)
                    pe.wait_ge(totalled, (h + 1) * TILES)
                    pe.wait_ge(expd, (h + 1) * TILES)
                    for c in range(NC):
                        mm = pe.matmul(sc[0:1, 0, c * TOK:(c + 1) * TOK], ones[:, :], tot[:, c * TOK:(c + 1) * TOK], start=True, stop=True)
                    mm.then_inc(summed, 1)
            run_turns(pe, NH // 2, turn)

        @block.scalar
        def _(act):
            def turn(i):
                for u in range(2):
                    h = i * 2 + u
                    for n, q in enumerate(order):
                        g = h * TILES + n
                        act.wait_ge(biased, g + 1)
                        act.wait_ge(totalled, h * TILES + max(n - 1, 0))
                        act.activation(e[:, n % 2, 0:(q + 1) * P], sc[:, n % 2, 0:(q + 1) * P], ACT.Exp,
                                       bias=nb[:, n % 2:n % 2 + 1], scale=SCALE, accum_out=rsum[:, n % 2:n % 2 + 1]).then_inc(expd, 1)
                    act.wait_ge(summed, h + 1)
                    act.wait_ge(row_stored, h * 16)
                    act.activation(row[:, :], sc[0:1, 0, :], ACT.Copy).then_inc(row_done, 1)
            run_turns(act, NH // 2, turn)

        @block.vector
        def _(dve):
            dve.memset(ones[:, :], 1.0).then_inc(init, 1)
            dve.wait_ge(cm_in, 16)
            def turn(i):
                for u in range(2):
                    h = i * 2 + u

                    def peak(n, q):
                        g = h * TILES + n
                        dve.wait_ge(scored, g + 1)
                        d = sc[:, n % 2, q * P:(q + 1) * P]
                        dve.tensor_tensor(d, d, cm[:, :], ALU.add).then_inc(masked, 1)
                        dve.wait_ge(masked, g + 1)
                        dve.tensor_reduce(mx[:, n % 2:n % 2 + 1], sc[:, n % 2, 0:(q + 1) * P], AX.X, ALU.max).then_inc(maxed, 1)
                        dve.wait_ge(maxed, g + 1)
                        dve.wait_ge(expd, h * TILES + max(n - 1, 0))
                        dve.tensor_scalar(nb[:, n % 2:n % 2 + 1], mx[:, n % 2:n % 2 + 1], -SCALE, None, ALU.mult).then_inc(biased, 1)

                    def total(n, q):
                        g = h * TILES + n
                        w = (q + 1) * P
                        dve.wait_ge(expd, g + 1)
                        dve.wait_ge(totalled, g)
                        dve.reciprocal(rinv[:, n % 2:n % 2 + 1], rsum[:, n % 2:n % 2 + 1]).then_inc(inverted, 1)
                        dve.wait_ge(inverted, g + 1)
                        if n == 0:
                            dve.wait_ge(summed, h)
                            dve.tensor_scalar(tot[:, 0:w], e[:, n % 2, 0:w], rinv[:, n % 2:n % 2 + 1], None, ALU.mult).then_inc(totalled, 1)
                        else:
                            dve.scalar_tensor_tensor(tot[:, 0:w], e[:, n % 2, 0:w], rinv[:, n % 2:n % 2 + 1], tot[:, 0:w],
                                                     ALU.mult, ALU.add).then_inc(totalled, 1)
                    for n, q in enumerate(order):
                        peak(n, q)
                        if n:
                            total(n - 1, order[n - 1])
                    total(NT - 1, order[-1])
            run_turns(dve, NH // 2, turn)


def heavy_phase(nc, sums, bias_dram, T, NH, BUDGET):
    phase = "heavy"
    ROUNDS = -(-BUDGET // 8)
    REST = BUDGET - 8 * (ROUNDS - 1)
    with ExitStack() as ctx:
        m = Memory(nc, ctx, phase)
        s = m.sb("s", [NH, T])
        top = m.sb("top", [NH, 8])
        bias = m.sb("bias", [NH, T])
        s_in = m.sem("s_in")
        step = m.sem("step")
        bias_done = m.sem("bias_done")
        stored = m.sem("stored")
        block = ctx.enter_context(nc.Block())

        @block.sync
        def _(sp):
            sp.dma_start(s[:, :], sums).then_inc(s_in, 16)
            sp.wait_ge(bias_done, 1)
            sp.dma_start(bias_dram, bias[:, :]).then_inc(stored, 16)
            sp.wait_ge(stored, 16)

        @block.vector
        def _(dve):
            dve.wait_ge(s_in, 16)
            for r in range(ROUNDS):
                if r:
                    dve.wait_ge(step, 2 * r)
                dve.max(top[:, :], s[:, :]).then_inc(step, 1)
                dve.wait_ge(step, 2 * r + 1)
                if r == ROUNDS - 1 and REST < 8:
                    dve.memset(top[:, REST:8], -1.0).then_inc(step, 1)
                    dve.wait_ge(step, 2 * r + 2)
                dve.match_replace(s[:, :], top[:, :], s[:, :], -1.0).then_inc(step, 1)
            dve.wait_ge(step, 2 * ROUNDS + (REST < 8))
            dve.tensor_scalar(bias[:, :], s[:, :], 0.0, NEG, ALU.is_ge, ALU.mult).then_inc(bias_done, 1)


def attend_phase(nc, qk_dram, v_dram, bias_dram, causal, near, attnT, T, NH, DH, RECENT):
    phase = "attend"
    NT = T // P
    SCALE = float(DH) ** -0.5
    LEAD = -(-RECENT // 1)
    with ExitStack() as ctx:
        m = Memory(nc, ctx, phase)
        qk = m.sb("qk", [DH, 2, 2, T])
        v = m.sb("v", [P, 2, NT, DH])
        hb = m.sb("hb", [P, 2, T])
        cm = m.sb("cm", [P, P])
        idt = m.sb("ident", [P, P])
        nm = m.sb("near", [P, P])
        mixed = m.sb("mixed", [P, 2, P])
        s = m.sb("s", [P, 2, T])
        pr = m.sb("pr", [P, 2, T])
        mx = m.sb("mx", [P, 2])
        nb = m.sb("nb", [P, 2])
        rsum = m.sb("rsum", [P, 2])
        rinv = m.sb("rinv", [P, 2])
        pt = m.sb("pt", [P, 2, 4, P])
        orow = m.sb("orow", [DH, 2, T])
        sc = m.ps("sc", [P, 4, TOK])
        tr = m.ps("tr", [P, 2, 4, P])
        ot = m.ps("ot", [DH, 2, TOK])
        consts_in = m.sem("consts_in")
        head_in = [m.sem("head_in0"), m.sem("head_in1")]
        scored = m.sem("scored")
        mixed_done = m.sem("mixed_done")
        biased = m.sem("biased")
        maxed = m.sem("maxed")
        nb_done = m.sem("nb_done")
        expd = m.sem("expd")
        inverted = m.sem("inverted")
        normed = m.sem("normed")
        turned = m.sem("turned")
        pt_copied = m.sem("pt_copied")
        pv_done = m.sem("pv_done")
        out_copied = m.sem("out_copied")
        out_stored = [m.sem("out_stored0"), m.sem("out_stored1")]
        block = ctx.enter_context(nc.Block())
        order = list(range(NT - 1, -1, -1))
        chunk_list = [(n, q, c, w) for n, q in enumerate(order) for c, w in chunks_of(q)]
        CH = len(chunk_list)
        first_chunk = {}
        for x, (n, q, c, w) in enumerate(chunk_list):
            first_chunk.setdefault(n, x)

        def zones(q):
            base = q * P
            far = max(base - RECENT, 0)
            mid = max(base + P - RECENT, 0)
            out = []
            if far:
                out.append(("far", 0, far))
            if mid > far:
                out.append(("mid", far, mid))
            return out, far, mid

        def pieces(q, c, w):
            z, far, mid = zones(q)
            base = q * P
            cuts = sorted({c, c + w} | {x for x in (far, mid, base) if c < x < c + w})
            out = []
            for a, b in zip(cuts, cuts[1:]):
                kind = "far" if b <= far else "mid" if b <= mid else "diag" if a >= base else "near"
                out.append((kind, a, b))
            return out

        @block.sync
        def _(sp):
            sp.dma_start(cm[:, :], causal).then_inc(consts_in, 16)
            sp.dma_start(nm[:, :], near[0]).then_inc(consts_in, 16)
            sp.dma_start(idt[:, :], near[1]).then_inc(consts_in, 16)

            def load(h, u):
                for j in range(2):
                    sp.dma_start(qk[:, u, j, :], qk_dram[j, bass.ds(h * DH, DH), :]).then_inc(head_in[u], 16)
                sp.dma_start(v[:, u, :, :], v_dram[:, bass.ds(h * DH, DH)].rearrange("(n p) d -> p n d", p=P)).then_inc(head_in[u], 16)
                sp.dma_start(hb[:, u, :], bias_dram[bass.ds(h, 1), :].to_broadcast([P, T])).then_inc(head_in[u], 16)

            def store(h, u):
                sp.wait_ge(out_copied, (h + 1) * NT)
                sp.dma_start(attnT[bass.ds(h * DH, DH), :], orow[:, u, :]).then_inc(out_stored[u], 16)
            load(0, 0)
            load(1, 1)
            def turn(i):
                for u in range(2):
                    store(i * 2 + u, u)
                    load(i * 2 + u + 2, u)
            run_turns(sp, NH // 2 - 1, turn)
            for u in range(2):
                store(NH - 2 + u, u)
                sp.wait_ge(out_stored[u], 16 * (NH // 2))

        @block.tensor
        def _(pe):
            pe.wait_ge(consts_in, 48)
            def turn(i):
                for u in range(2):
                    h = i * 2 + u
                    pe.wait_ge(head_in[u], (i + 1) * 64)

                    def scores(n):
                        q = order[n]
                        for x, (c, w) in enumerate(chunks_of(q)):
                            x += first_chunk[n]
                            pe.wait_ge(biased, h * CH + max(x - 3, 0))
                            pe.matmul(sc[:, x % 4, 0:w], qk[:, u, 0, q * P:(q + 1) * P], qk[:, u, 1, c:c + w],
                                      start=True, stop=True).then_inc(scored, 1)

                    def values(n):
                        q = order[n]
                        g = h * NT + n
                        pe.wait_ge(normed, g + 1)
                        if n >= 2:
                            pe.wait_ge(out_copied, g - 1)
                        else:
                            pe.wait_ge(out_copied, h * NT)
                        cs = chunks_of(q)

                        def flip(x, c, w):
                            x += first_chunk[n]
                            pe.wait_ge(pt_copied, h * CH + max(x - 1, 0))
                            for j in range(w // P):
                                t = pe.transpose(tr[:, x % 2, j, :], pr[:, n % 2, c + j * P:c + (j + 1) * P], idt[:, :])
                            t.then_inc(turned, 1)

                        def weigh(x, c, w):
                            y = x + first_chunk[n]
                            pe.wait_ge(pt_copied, h * CH + y + 1)
                            for j in range(w // P):
                                mm = pe.matmul(ot[:, n % 2, 0:P], v[:, u, c // P + j, :], pt[:, y % 2, j, :],
                                               start=(c + j == 0), stop=(x == len(cs) - 1 and j == w // P - 1))
                            mm.then_inc(pv_done, 1)
                        for x, (c, w) in enumerate(cs):
                            flip(x, c, w)
                            if x:
                                weigh(x - 1, *cs[x - 1])
                        weigh(len(cs) - 1, *cs[-1])
                    for n in range(NT):
                        scores(n)
                        if n:
                            values(n - 1)
                    values(NT - 1)
            run_turns(pe, NH // 2, turn)

        @block.gpsimd
        def _(pool):
            pool.wait_ge(consts_in, 48)
            def turn(i):
                for u in range(2):
                    h = i * 2 + u
                    pool.wait_ge(head_in[u], (i + 1) * 64)

                    def mix(n):
                        q = order[n]
                        g = h * NT + n
                        far, mid = max(q * P - RECENT, 0), max(q * P + P - RECENT, 0)
                        pool.wait_ge(biased, h * CH + (first_chunk[n - 1] if n >= 1 else 0))
                        lo = far - (q * P - RECENT)
                        if mid > far:
                            op = pool.tensor_tensor(mixed[:, n % 2, lo:P], hb[:, u, far:mid], nm[:, lo:P], ALU.mult)
                        else:
                            op = pool.tensor_tensor(mixed[:, n % 2, 0:1], nm[:, 0:1], nm[:, 0:1], ALU.mult)
                        op.then_inc(mixed_done, 1)

                    def norm(n):
                        q = order[n]
                        g = h * NT + n
                        pool.wait_ge(inverted, g + 1)
                        w = (q + 1) * P
                        pool.tensor_tensor(pr[:, n % 2, 0:w], pr[:, n % 2, 0:w],
                                           rinv[:, n % 2:n % 2 + 1].to_broadcast([P, w]), ALU.mult).then_inc(normed, 1)
                    mix(0)
                    for n in range(NT):
                        if n + 1 < NT:
                            mix(n + 1)
                        norm(n)
            run_turns(pool, NH // 2, turn)

        @block.scalar
        def _(act):
            def turn(i):
                for u in range(2):
                    h = i * 2 + u

                    def exps(n):
                        q = order[n]
                        g = h * NT + n
                        w = (q + 1) * P
                        act.wait_ge(nb_done, g + 1)
                        act.wait_ge(turned, h * CH + (first_chunk[n - 1] if n >= 1 else 0))
                        act.wait_ge(inverted, h * NT + max(n - 1, 0))
                        act.activation(pr[:, n % 2, 0:w], s[:, n % 2, 0:w], ACT.Exp, bias=nb[:, n % 2:n % 2 + 1], scale=SCALE,
                                       accum_out=rsum[:, n % 2:n % 2 + 1]).then_inc(expd, 1)

                    def copies(n):
                        q = order[n]
                        g = h * NT + n
                        for x, (c, w) in enumerate(chunks_of(q)):
                            x += first_chunk[n]
                            act.wait_ge(turned, h * CH + x + 1)
                            act.wait_ge(pv_done, h * CH + max(x - 1, 0))
                            act.activation(pt[:, x % 2, 0:w // P, :], tr[:, x % 2, 0:w // P, :], ACT.Copy).then_inc(pt_copied, 1)
                        act.wait_ge(pv_done, h * CH + x + 1)
                        if n == 0:
                            act.wait_ge(out_stored[u], i * 16)
                        act.activation(orow[:, u, q * P:(q + 1) * P], ot[:, n % 2, 0:P], ACT.Copy).then_inc(out_copied, 1)
                    for n in range(NT):
                        exps(n)
                        if n:
                            copies(n - 1)
                    copies(NT - 1)
            run_turns(act, NH // 2, turn)

        @block.vector
        def _(dve):
            dve.wait_ge(consts_in, 48)
            def turn(i):
                for u in range(2):
                    h = i * 2 + u
                    dve.wait_ge(head_in[u], (i + 1) * 64)

                    def bias(n):
                        q = order[n]
                        g = h * NT + n
                        dve.wait_ge(mixed_done, g + 1)
                        dve.wait_ge(expd, h * NT + max(n - 1, 0))
                        for x, (c, w) in enumerate(chunks_of(q)):
                            x += first_chunk[n]
                            dve.wait_ge(scored, h * CH + x + 1)
                            for kind, a, b in pieces(q, c, w):
                                src, dst = sc[:, x % 4, a - c:b - c], s[:, n % 2, a:b]
                                lo = a - (q * P - RECENT)
                                if kind == "far":
                                    op = dve.tensor_tensor(dst, src, hb[:, u, a:b], ALU.add)
                                elif kind == "mid":
                                    op = dve.tensor_tensor(dst, src, mixed[:, n % 2, lo:lo + b - a], ALU.add)
                                elif kind == "diag":
                                    op = dve.tensor_tensor(dst, src, cm[:, a - q * P:b - q * P], ALU.add)
                                else:
                                    op = dve.tensor_copy(dst, src)
                            op.then_inc(biased, 1)
                        dve.wait_ge(biased, h * CH + x + 1)
                        dve.tensor_reduce(mx[:, n % 2:n % 2 + 1], s[:, n % 2, 0:(q + 1) * P], AX.X, ALU.max).then_inc(maxed, 1)
                        dve.wait_ge(maxed, g + 1)
                        dve.tensor_scalar(nb[:, n % 2:n % 2 + 1], mx[:, n % 2:n % 2 + 1], -SCALE, None, ALU.mult).then_inc(nb_done, 1)

                    def invert(n):
                        g = h * NT + n
                        dve.wait_ge(expd, g + 1)
                        dve.wait_ge(normed, h * NT + max(n - 1, 0))
                        dve.reciprocal(rinv[:, n % 2:n % 2 + 1], rsum[:, n % 2:n % 2 + 1]).then_inc(inverted, 1)
                    for n in range(NT):
                        bias(n)
                        if n:
                            invert(n - 1)
                    invert(NT - 1)
            run_turns(dve, NH // 2, turn)


def project_out_phase(nc, attnT, wo, x, x_out, T):
    phase = "oproj"
    NT = T // P
    with ExitStack() as ctx:
        m = Memory(nc, ctx, phase)
        at = m.sb("at", [P, KT, T])
        w = m.sb("w", [P, KT, D])
        xs = m.sb("xs", [P, NT, D])
        acc = m.ps("acc", [P, 4, D])
        w_in = m.sem("w_in")
        x_in = m.sem("x_in")
        done = m.sem("done")
        added = m.sem("added")
        stored = m.sem("stored")
        block = ctx.enter_context(nc.Block())

        @block.sync
        def _(sp):
            for k in range(KT):
                sp.dma_start(at[:, k, :], attnT[k * P:(k + 1) * P, :]).then_inc(w_in, 16)
                sp.dma_start(w[:, k, :], wo[k * P:(k + 1) * P, :]).then_inc(w_in, 16)
            sp.dma_start(xs[:, :, :], x.rearrange("(n p) d -> p n d", p=P)).then_inc(x_in, 16)
            for g in range(NT // 4):
                sp.wait_ge(added, 4 * (g + 1))
                sp.dma_start(x_out[g * 4 * P:(g + 1) * 4 * P, :].rearrange("(n p) d -> p n d", p=P), xs[:, 4 * g:4 * g + 4, :]).then_inc(stored, 16)
            sp.wait_ge(stored, 16 * (NT // 4))

        @block.tensor
        def _(pe):
            pe.wait_ge(w_in, 32 * KT)
            for n in range(NT):
                if n >= 4:
                    pe.wait_ge(added, n - 3)
                for k in range(KT):
                    mm = pe.matmul(acc[:, n % 4, :], at[:, k, n * P:(n + 1) * P], w[:, k, :], start=(k == 0), stop=(k == KT - 1))
                mm.then_inc(done, 1)

        @block.vector
        def _(dve):
            dve.wait_ge(x_in, 16)
            for n in range(NT):
                dve.wait_ge(done, n + 1)
                dve.tensor_tensor(xs[:, n, :], xs[:, n, :], acc[:, n % 4, :], ALU.add).then_inc(added, 1)


HEADS_B = 16
DH = D // HEADS_B
RATIO = 0.1
THETA = 10000.0


def constants(T):
    inv = (1.0 / THETA ** (np.arange(0, DH, 2, dtype=np.float32) / np.float32(DH))).astype(np.float32)
    freqs = np.arange(T, dtype=np.float32)[:, None] * inv[None, :]
    emb = np.concatenate([freqs, freqs], axis=-1)
    sign = np.where(np.arange(DH) < DH // 2, -1.0, 1.0).astype(np.float32)
    cos = np.tile(np.cos(emb).astype(np.float32).T, (P // DH, 1))
    sin = np.tile((np.sin(emb).astype(np.float32) * sign).T, (P // DH, 1))
    had = np.ones((1, 1), np.float32)
    while had.shape[0] < P:
        had = np.block([[had, had], [had, -had]])
    r, c = np.arange(P)[:, None], np.arange(P)[None, :]
    recent = int(RATIO * T)
    return {
        "c_ident": np.eye(P, dtype=np.float32),
        "c_hmask": (r % GH == np.arange(GH)[None, :]).astype(np.float32),
        "c_cos": np.ascontiguousarray(cos), "c_sin": np.ascontiguousarray(sin),
        "c_had": np.ascontiguousarray(had.astype(np.float32)),
        "c_causal": np.where(c <= r, 0.0, NEG).astype(np.float32),
        "c_far": (r > c).astype(np.float32),
    }


def program(nc, a, out):
    T = a["x"].shape[0]
    F = a["w1"].shape[1]
    scratch = lambda name, shape: nc.dram_tensor(name, shape, F32, kind="Internal").ap()
    xnT = [scratch(f"xnT{i}", (KT, P, T)) for i in range(4)]
    xs = [scratch(f"x{i}", (T, D)) for i in range(3)]
    streams = [scratch(f"stream_{n}", (H, P, T)) for n in ("beta_k", "q", "k", "beta_v", "a")]
    beta = scratch("beta", (H, T))
    o = scratch("o", (H, P, T))
    qk = scratch("qk", (2, D, T))
    v = scratch("v", (T, D))
    sums = scratch("sums", (HEADS_B, T))
    bias = scratch("bias", (HEADS_B, T))
    attnT = scratch("attnT", (D, T))
    layernorm_phase(nc, "ln0", a["x"], xnT[0], a["c_ident"], T)
    project_phase(nc, xnT[0], [a["wk"], a["wv"], a["wq"], a["wa"]], a["wb"],
                  [a["kc_w"], a["vc_w"], a["qc_w"]], [a["kc_b"], a["vc_b"], a["qc_b"]],
                  a["ba"], a["bb"], streams, beta, T, H, float(P) ** -0.5)
    scan_phase(nc, streams, o, a["c_ident"], a["c_hmask"], T)
    mix_phase(nc, xnT[0], a["wg"], o, a["wo"], a["ln_g"], a["ln_b"], a["x"], xs[0], T, H)
    layernorm_phase(nc, "ln1", xs[0], xnT[1], a["c_ident"], T)
    ffn_phase(nc, "ffn0", xnT[1], a["w1"], a["w3"], a["w2"], a["c_had"], xs[0], xs[1], T, F)
    layernorm_phase(nc, "ln2", xs[1], xnT[2], a["c_ident"], T)
    rope_phase(nc, xnT[2], [a["bq"], a["bq_swap"], a["bk"], a["bk_swap"]], a["bv"], a["c_cos"], a["c_sin"], qk, v, T)
    column_sum_phase(nc, qk, a["c_causal"], sums, T, HEADS_B, DH)
    heavy_phase(nc, sums, bias, T, HEADS_B, int(RATIO * T))
    attend_phase(nc, qk, v, bias, a["c_causal"], (a["c_far"], a["c_ident"]), attnT, T, HEADS_B, DH, int(RATIO * T))
    project_out_phase(nc, attnT, a["bo"], xs[1], xs[2], T)
    layernorm_phase(nc, "ln3", xs[2], xnT[3], a["c_ident"], T)
    ffn_phase(nc, "ffn1", xnT[3], a["w1"], a["w3"], a["w2"], a["c_had"], xs[2], out, T, F)


def laid_out(i):
    g = lambda n: np.asarray(i[n])
    t = lambda n: np.ascontiguousarray(g(n).T)
    A, B, FN = "L0_attn_a_", "L0_attn_b_", "L0_ffn_"
    swap = np.arange(D).reshape(HEADS_B, 2, DH // 2)[:, ::-1].reshape(-1)
    per_head = lambda n: np.ascontiguousarray(g(n).reshape(H, P).T)
    taps = lambda n: np.ascontiguousarray(g(n).reshape(H, P, -1).transpose(1, 0, 2))
    return {
        "x": np.ascontiguousarray(g(A + "x")[0]),
        "wq": t(A + "Wq"), "wk": t(A + "Wk"), "wv": t(A + "Wv"), "wa": t(A + "Wa"), "wb": t(A + "Wb"),
        "wg": t(A + "Wg"), "wo": t(A + "Wo"), "ba": np.ascontiguousarray(g(A + "ba").reshape(H, P)),
        "bb": np.ascontiguousarray(g(A + "bb").reshape(H, 1)),
        "qc_w": taps(A + "qc_w"), "kc_w": taps(A + "kc_w"), "vc_w": taps(A + "vc_w"),
        "qc_b": per_head(A + "qc_b"), "kc_b": per_head(A + "kc_b"), "vc_b": per_head(A + "vc_b"),
        "ln_g": np.ascontiguousarray(g(A + "ln_g").reshape(P, 1)),
        "ln_b": np.ascontiguousarray(g(A + "ln_b").reshape(P, 1)),
        "bq": t(B + "Wq"), "bk": t(B + "Wk"), "bv": t(B + "Wv"), "bo": t(B + "Wo"),
        "bq_swap": np.ascontiguousarray(g(B + "Wq")[swap].T),
        "bk_swap": np.ascontiguousarray(g(B + "Wk")[swap].T),
        "w1": t(FN + "W1"), "w3": t(FN + "W3"), "w2": t(FN + "W2"),
    }


def kernel(**inputs):
    import concourse.bacc as bacc
    from concourse.bass_utils import run_bass_kernel_spmd

    arrays = laid_out(inputs)
    T = arrays["x"].shape[0]
    arrays.update(constants(T))
    nc = bacc.Bacc("TRN2", target_bir_lowering=False, num_devices=1)
    a = {n: nc.dram_tensor(f"in_{n}", v.shape, mybir.dt.from_np(v.dtype), kind="ExternalInput").ap()
         for n, v in arrays.items()}
    out = nc.dram_tensor("out", (T, D), F32, kind="ExternalOutput").ap()
    program(nc, a, out)
    r = run_bass_kernel_spmd(nc, [{f"in_{n}": v for n, v in arrays.items()}], core_ids=[0])
    return r.results[0]["out"].reshape(1, T, D)
```

```python
import numpy as np
import concourse.bass as bass
from concourse import mybir
from contextlib import ExitStack

F32 = mybir.dt.float32
F32R = mybir.dt.float32r
ALU = mybir.AluOpType
ACT = mybir.ActivationFunctionType
AX = mybir.AxisListType
P = 128
D = 512
KT = D // P
TOK = 512
EPS = 1e-5


class Memory:

    def __init__(self, nc, ctx, phase):
        self.nc, self.ctx, self.phase = nc, ctx, phase
        self.sems = []
        ctx.callback(self.release)

    def sb(self, name, shape, dtype=F32):
        return self.ctx.enter_context(self.nc.sbuf_tensor(f"{self.phase}_{name}", shape, dtype))

    def ps(self, name, shape):
        return self.ctx.enter_context(self.nc.psum_tensor(f"{self.phase}_{name}", shape, F32))

    def sem(self, name):
        self.sems.append(self.nc.alloc_semaphore(f"{self.phase}_{name}"))
        return self.sems[-1]

    def release(self):
        self.nc.clear_and_free_semaphores(self.sems)
        self.nc.all_engine_barrier()


def run_turns(eng, n, turn):
    turn(0)
    with eng.Fori(1, n) as i:
        turn(i)


def layernorm_phase(nc, phase, x, xnT, ident, T):
    NT = T // P
    with ExitStack() as ctx:
        m = Memory(nc, ctx, phase)
        xs = m.sb("xs", [P, NT, D])
        xn = m.sb("xn", [P, 2, D])
        xt = m.sb("xt", [P, 4, KT, P])
        idt = m.sb("ident", [P, P])
        stats = m.sb("stats", [P, NT, nc.vector.BN_STATS_DIM])
        mv = m.sb("mv", [P, NT, nc.vector.BN_AGGR_DIM])
        sd = m.sb("sd", [P, NT])
        rstd = m.sb("rstd", [P, NT])
        tr = m.ps("tr", [P, 2, KT, P])
        x_in = m.sem("x_in")
        ident_in = m.sem("ident_in")
        stat = m.sem("stat")
        var_ready = m.sem("var_ready")
        sd_ready = m.sem("sd_ready")
        rstd_ready = m.sem("rstd_ready")
        normed = m.sem("normed")
        turned = m.sem("turned")
        copied = m.sem("copied")
        stored = m.sem("stored")
        block = ctx.enter_context(nc.Block())

        @block.sync
        def _(sp):
            sp.dma_start(idt[:, :], ident).then_inc(ident_in, 16)
            sp.dma_start(xs[:, :, :], x.rearrange("(n p) d -> p n d", p=P)).then_inc(x_in, 16)
            for g in range(NT // 4):
                sp.wait_ge(copied, 4 * (g + 1))
                for k in range(KT):
                    sp.dma_start(xnT[k, :, g * 4 * P:(g + 1) * 4 * P].rearrange("p (n t) -> p n t", n=4),
                                 xt[:, :, k, :]).then_inc(stored, 16)
            sp.wait_ge(stored, 16 * KT * (NT // 4))

        @block.vector
        def _(dve):
            dve.wait_ge(x_in, 16)
            for n in range(NT):
                dve.bn_stats(stats[:, n, :], xs[:, n, :]).then_inc(stat, 1)
            for n in range(NT):
                dve.wait_ge(stat, n + 1)
                last = dve.bn_aggr(mv[:, n, :], stats[:, n, :])
            last.then_inc(stat, 1)
            dve.wait_ge(stat, NT + 1)
            dve.tensor_scalar(sd[:, :], mv[:, :, 1], EPS, None, ALU.add).then_inc(var_ready, 1)
            dve.wait_ge(sd_ready, 1)
            dve.reciprocal(rstd[:, :], sd[:, :]).then_inc(rstd_ready, 1)
            dve.wait_ge(rstd_ready, 1)
            for n in range(NT):
                if n >= 2:
                    dve.wait_ge(turned, n - 1)
                dve.tensor_scalar(xn[:, n % 2, :], xs[:, n, :], mv[:, n, 0:1], rstd[:, n:n + 1],
                                  ALU.subtract, ALU.mult).then_inc(normed, 1)

        @block.scalar
        def _(act):
            act.wait_ge(var_ready, 1)
            act.activation(sd[:, :], sd[:, :], ACT.Sqrt).then_inc(sd_ready, 1)
            for n in range(NT):
                act.wait_ge(turned, n + 1)
                if n >= 4:
                    act.wait_ge(stored, 16 * KT * (n // 4))
                act.activation(xt[:, n % 4], tr[:, n % 2], ACT.Copy).then_inc(copied, 1)

        @block.tensor
        def _(pe):
            pe.wait_ge(ident_in, 16)
            for n in range(NT):
                pe.wait_ge(normed, n + 1)
                if n >= 2:
                    pe.wait_ge(copied, n - 1)
                for k in range(KT):
                    t = pe.transpose(tr[:, n % 2, k, :], xn[:, n % 2, k * P:(k + 1) * P], idt[:, :])
                t.then_inc(turned, 1)


def project_phase(nc, xnT, w_kvqa, w_beta, conv_w, conv_b, a_bias, beta_bias, streams, beta_dram, blocks_dram, T, H, scale, STEPS):
    phase = "proj"
    TT = T // TOK
    TAPS = 4
    KB, QQ, KK, VB, AA = range(5)
    with ExitStack() as ctx:
        m = Memory(nc, ctx, phase)
        xn = m.sb("xn", [P, KT, T])
        w = m.sb("w", [P, 2, 4, KT, P])
        wb = m.sb("wb", [P, KT, H])
        cw = m.sb("cw", [P, 3, H, TAPS])
        cb = m.sb("cb", [P, 3, H])
        ab = m.sb("ab", [P, 2])
        bb = m.sb("bb", [H, 1])
        beta = m.sb("beta", [H, T])
        beta_rows = m.sb("beta_rows", [P, 2, T])
        raw = m.sb("raw", [P, 2, TAPS - 1 + T])
        y = m.sb("y", [P, 2, T])
        gate = m.sb("gate", [P, 2, T])
        res = m.sb("res", [P, 2, T])
        resb = m.sb("resb", [P, 2, T])
        decay = m.sb("decay", [P, 2, T])
        folds = STEPS.bit_length() - 1
        fold = m.sb("fold", [P, 2, T // STEPS, STEPS])
        product = m.sb("product", [P, 2, T // STEPS])
        acc = m.ps("acc", [P, 8, TOK])
        params_in = m.sem("params_in")
        w_in = [m.sem("w_in0"), m.sem("w_in1")]
        beta_in = [m.sem("beta_in0"), m.sem("beta_in1")]
        zeroed = m.sem("zeroed")
        beta_mm = m.sem("beta_mm")
        beta_done = m.sem("beta_done")
        beta_stored = m.sem("beta_stored")
        unit_done = m.sem("unit_done")
        evacuated = m.sem("evacuated")
        conv_step = m.sem("conv_step")
        gated = m.sem("gated")
        res_done = m.sem("res_done")
        resb_done = m.sem("resb_done")
        res_stored = [m.sem("res_stored0"), m.sem("res_stored1")]
        resb_stored = [m.sem("resb_stored0"), m.sem("resb_stored1")]
        decay_stored = [m.sem("decay_stored0"), m.sem("decay_stored1")]
        folded = m.sem("folded")
        fold_stored = [m.sem("fold_stored0"), m.sem("fold_stored1")]
        block = ctx.enter_context(nc.Block())
        OUT = [KK, None, QQ]
        OUTB = [KB, VB, None]

        def evac0(j, t, TT):
            return max(j * TT + t - 7, 0)

        def res_count(i, s):
            before = sum(1 for r in range(s) if r % 2 == s % 2 and r % 3 != 1)
            return (i * 2 + before) * 16

        @block.sync
        def _(sp):
            for k in range(KT):
                sp.dma_start(xn[:, k, :], xnT[k]).then_inc(params_in, 16)
            sp.dma_start(wb[:, :, :], w_beta.rearrange("(k p) h -> p k h", p=P)).then_inc(params_in, 16)
            for j in range(3):
                sp.dma_start(cw[:, j], conv_w[j]).then_inc(params_in, 16)
            sp.dma_start(bb[:, :], beta_bias).then_inc(params_in, 16)
            for j in range(3):
                sp.dma_start(cb[:, j], conv_b[j]).then_inc(params_in, 16)

            def load(h, u):
                for j in range(4):
                    sp.dma_start(w[:, u, j], w_kvqa[j][:, bass.ds(h * P, P)].rearrange("(k p) c -> p k c", p=P)).then_inc(w_in[u], 16)
                sp.dma_start(ab[:, u:u + 1], a_bias[bass.ds(h, 1), :].rearrange("o p -> p o")).then_inc(w_in[u], 16)
                sp.dma_start(beta_rows[:, u, :], beta_dram[bass.ds(h, 1), :].to_broadcast([P, T])).then_inc(beta_in[u], 16)
            sp.wait_ge(beta_done, TT)
            sp.dma_start(beta_dram, beta[:, :]).then_inc(beta_stored, 16)
            sp.wait_ge(beta_stored, 16)
            load(0, 0)
            load(1, 1)

            def stores(i, u, ahead):
                h = i * 2 + u
                for j in range(3):
                    s = 3 * u + j
                    if OUT[j] is not None:
                        sp.wait_ge(res_done, i * 6 + s + 1)
                        sp.dma_start(streams[OUT[j]][bass.ds(h, 1)].rearrange("o p t -> p (o t)"), res[:, s % 2]).then_inc(res_stored[s % 2], 16)
                    if OUTB[j] is not None:
                        sp.wait_ge(resb_done, h * 2 + j + 1)
                        sp.dma_start(streams[OUTB[j]][bass.ds(h, 1)].rearrange("o p t -> p (o t)"), resb[:, s % 2]).then_inc(resb_stored[s % 2], 16)
                sp.wait_ge(evacuated, (h + 1) * 4 * TT)
                sp.dma_start(streams[AA][bass.ds(h, 1)].rearrange("o p t -> p (o t)"), decay[:, u]).then_inc(decay_stored[u], 16)
                sp.wait_ge(folded, (h + 1) * folds)
                sp.dma_start(blocks_dram[bass.ds(h, 1)].rearrange("o p n -> p (o n)"), product[:, u, :]).then_inc(fold_stored[u], 16)
                if ahead:
                    load(h + 2, u)
            def turn(i):
                for u in range(2):
                    stores(i, u, True)
            run_turns(sp, H // 2 - 1, turn)
            for u in range(2):
                stores(H // 2 - 1, u, False)
            for u in range(2):
                sp.wait_ge(decay_stored[u], 16 * (H // 2))
                sp.wait_ge(fold_stored[u], 16 * (H // 2))
                sp.wait_ge(res_stored[u], 16 * (H // 2) * 2)
                sp.wait_ge(resb_stored[u], 16 * (H // 2) * 2)

        @block.tensor
        def _(pe):
            pe.wait_ge(params_in, 16 * (KT + 1 + 3 + 3 + 1))
            for t in range(TT):
                for k in range(KT):
                    mm = pe.matmul(acc[0:H, 4 + t % 4, :], wb[:, k, :], xn[:, k, t * TOK:(t + 1) * TOK], start=(k == 0), stop=(k == KT - 1))
                mm.then_inc(beta_mm, 1)
            pe.wait_ge(beta_done, TT)
            def turn(i):
                for u in range(2):
                    pe.wait_ge(w_in[u], (i + 1) * 80)
                    for j in range(4):
                        for t in range(TT):
                            n = (i * 2 + u) * 4 * TT + j * TT + t
                            if u == 0 and j < 2:
                                pe.wait_ge(evacuated, i * (8 * TT) + evac0(j, t, TT))
                            else:
                                pe.wait_ge(evacuated, n - 7)
                            for k in range(KT):
                                mm = pe.matmul(acc[:, (j * TT + t) % 8, :], w[:, u, j, k, :],
                                               xn[:, k, t * TOK:(t + 1) * TOK], start=(k == 0), stop=(k == KT - 1))
                            mm.then_inc(unit_done, 1)
            run_turns(pe, H // 2, turn)

        @block.scalar
        def _(act):
            act.wait_ge(params_in, 16 * (KT + 1 + 3 + 3 + 1))
            for t in range(TT):
                act.wait_ge(beta_mm, t + 1)
                act.activation(beta[:, t * TOK:(t + 1) * TOK], acc[0:H, 4 + t % 4, :], ACT.Sigmoid, bias=bb[:, 0:1]).then_inc(beta_done, 1)
            act.wait_ge(zeroed, 2)

            def gate_unit(i, s):
                act.wait_ge(conv_step, (i * 6 + s + 1) * TAPS)
                if s >= 2:
                    act.wait_ge(res_done, i * 6 + s - 1)
                else:
                    act.wait_ge(res_done, i * 6)
                act.activation(gate[:, s % 2, :], y[:, s % 2, :], ACT.Sigmoid).then_inc(gated, 1)
            def turn(i):
                for u in range(2):
                    h = i * 2 + u
                    for j in range(4):
                        s = 3 * u + j
                        if j < 3:
                            if s >= 2:
                                act.wait_ge(conv_step, (i * 6 + s - 1) * TAPS)
                            else:
                                act.wait_ge(conv_step, (i * 6) * TAPS)
                        else:
                            act.wait_ge(decay_stored[u], i * 16)
                            act.wait_ge(folded, i * 2 * folds)
                            act.wait_ge(w_in[u], (i + 1) * 80)
                        for t in range(TT):
                            n = h * 4 * TT + j * TT + t
                            act.wait_ge(unit_done, n + 1)
                            if j < 3:
                                lo = TAPS - 1 + t * TOK
                                act.activation(raw[:, s % 2, lo:lo + TOK], acc[:, (j * TT + t) % 8, :], ACT.Copy).then_inc(evacuated, 1)
                            else:
                                act.activation(decay[:, u, t * TOK:(t + 1) * TOK], acc[:, (j * TT + t) % 8, :], ACT.Sigmoid,
                                               bias=ab[:, u:u + 1]).then_inc(evacuated, 1)
                        if j < 3 and j > 0:
                            gate_unit(i, s - 1)
                    gate_unit(i, 3 * u + 2)
            run_turns(act, H // 2, turn)

        @block.vector
        def _(dve):
            for s in range(2):
                dve.memset(raw[:, s, 0:TAPS - 1], 0.0).then_inc(zeroed, 1)
            dve.wait_ge(params_in, 16 * (KT + 1 + 3 + 3 + 1))
            dve.wait_ge(zeroed, 2)

            def finish(i, s):
                j = s % 3
                dve.wait_ge(gated, i * 6 + s + 1)
                if s >= 2:
                    dve.wait_ge(resb_done, i * 4 + [0, 0, 1, 2, 2, 3][s] )
                else:
                    dve.wait_ge(resb_done, i * 4)
                dve.wait_ge(res_stored[s % 2], res_count(i, s))
                dve.scalar_tensor_tensor(res[:, s % 2, :], y[:, s % 2, :], scale if j == 0 else 1.0, gate[:, s % 2, :],
                                         ALU.mult, ALU.mult).then_inc(res_done, 1)

            def turn(i):
                for u in range(2):
                    for j in range(3):
                        s = 3 * u + j
                        h = i * 2 + u
                        dve.wait_ge(evacuated, h * 4 * TT + (j + 1) * TT)
                        dve.wait_ge(res_done, i * 6 + max(s - 1, 0))
                        for tap in range(TAPS):
                            src = raw[:, s % 2, tap:tap + T]
                            cwt = cw[:, j, bass.ds(h, 1), tap]
                            if tap == 0:
                                dve.tensor_scalar(y[:, s % 2, :], src, cwt, cb[:, j, bass.ds(h, 1)],
                                                  ALU.mult, ALU.add).then_inc(conv_step, 1)
                            else:
                                dve.wait_ge(conv_step, (i * 6 + s) * TAPS + tap)
                                dve.scalar_tensor_tensor(y[:, s % 2, :], src, cwt, y[:, s % 2, :],
                                                         ALU.mult, ALU.add).then_inc(conv_step, 1)
                        finish(i, s)
            run_turns(dve, H // 2, turn)

        @block.gpsimd
        def _(pool):
            def turn(i):
                for u in range(2):
                    for j in range(2):
                        s = 3 * u + j
                        if j == 0:
                            pool.wait_ge(beta_in[u], (i + 1) * 16)
                        pool.wait_ge(res_done, i * 6 + s + 1)
                        before = sum(1 for r in range(s) if r % 2 == s % 2 and r % 3 != 2)
                        pool.wait_ge(resb_stored[s % 2], (i * 2 + before) * 16)
                        pool.tensor_tensor(resb[:, s % 2, :], res[:, s % 2, :], beta_rows[:, u, :], ALU.mult).then_inc(resb_done, 1)
                    h = i * 2 + u
                    pool.wait_ge(evacuated, (h + 1) * 4 * TT)
                    pool.wait_ge(fold_stored[u], i * 16)
                    tokens = decay[:, u, :].rearrange("p (n s) -> p n s", s=STEPS)
                    src, at = tokens, 0
                    for f in range(folds):
                        n = STEPS >> (f + 1)
                        dst = (STEPS // 2, 0)[f % 2]
                        out = product[:, u, :].unsqueeze(2) if n == 1 else fold[:, u, :, dst:dst + n]
                        if f:
                            pool.wait_ge(folded, h * folds + f)
                        pool.tensor_tensor(out, src[:, :, at:at + n], src[:, :, at + n:at + 2 * n],
                                           ALU.mult).then_inc(folded, 1)
                        src, at = fold[:, u], dst
            run_turns(pool, H // 2, turn)


def block_decay_phase(nc, blocks_dram, decays, ident, T, H, STEPS):
    NB = T // STEPS
    with ExitStack() as ctx:
        m = Memory(nc, ctx, "decays")
        cm = m.sb("cm", [P, H, NB])
        rows = m.sb("rows", [NB, H, P])
        idt = m.sb("ident", [P, P])
        tr = m.ps("tr", [NB, H, P])
        loaded = m.sem("loaded")
        turned = m.sem("turned")
        copied = m.sem("copied")
        stored = m.sem("stored")
        block = ctx.enter_context(nc.Block())

        @block.sync
        def _(sp):
            sp.dma_start(idt[:, :], ident).then_inc(loaded, 16)
            sp.dma_start(cm[:, :, :], blocks_dram.rearrange("h p n -> p h n")).then_inc(loaded, 16)
            sp.wait_ge(copied, H // 4)
            sp.dma_start(decays, rows[:, :, :].rearrange("n h p -> n (h p)")).then_inc(stored, 16)
            sp.wait_ge(stored, 16)

        @block.tensor
        def _(pe):
            pe.wait_ge(loaded, 32)
            for g in range(H // 4):
                for h in range(4 * g, 4 * g + 4):
                    t = pe.transpose(tr[:, h, :], cm[:, h, :], idt[:, :])
                t.then_inc(turned, 1)

        @block.vector
        def _(dve):
            for g in range(H // 4):
                dve.wait_ge(turned, g + 1)
                dve.tensor_copy(rows[:, 4 * g:4 * g + 4, :], tr[:, 4 * g:4 * g + 4, :]).then_inc(copied, 1)


def mix_phase(nc, xnT, wg, o_dram, wo, ln_g, ln_b, x, x_out, T, H):
    phase = "mix"
    TT = T // TOK
    SUB = TOK // P
    with ExitStack() as ctx:
        m = Memory(nc, ctx, phase)
        wgs = m.sb("wg", [P, KT, H * P])
        wos = m.sb("wo", [P, H, D])
        xn = m.sb("xn", [P, KT, TOK])
        o = m.sb("o", [P, 4, TOK])
        oc = m.sb("oc", [P, 4, TOK])
        sq = m.sb("sq", [P, 2, TOK])
        sd = m.sb("sd", [P, 2, TOK])
        rs = m.sb("rs", [P, 2, TOK])
        sg = m.sb("sg", [P, 4, TOK])
        of = m.sb("of", [P, 2, TOK])
        mean_w = m.sb("mean_w", [P, P])
        gb = m.sb("gb", [P, 2])
        eps = m.sb("eps", [P, 1])
        xs = m.sb("xs", [P, 2, SUB, D])
        out_ps = m.ps("out", [P, SUB, D])
        g_ps = m.ps("g", [P, 2, TOK])
        mean_ps = m.ps("mean", [P, TOK])
        var_ps = m.ps("var", [P, TOK])
        w_in = m.sem("w_in")
        init = m.sem("init")
        xn_in = m.sem("xn_in")
        x_in = m.sem("x_in")
        o_in = [m.sem(f"o_in{i}") for i in range(4)]
        g_done = m.sem("g_done")
        mean_done = m.sem("mean_done")
        var_done = m.sem("var_done")
        out_done = m.sem("out_done")
        centred = m.sem("centred")
        squared = m.sem("squared")
        sd_done = m.sem("sd_done")
        sg_done = m.sem("sg_done")
        rs_done = m.sem("rs_done")
        norm_step = m.sem("norm_step")
        of_done = m.sem("of_done")
        added = m.sem("added")
        stored = m.sem("stored")
        block = ctx.enter_context(nc.Block())

        @block.sync
        def _(sp):
            for k in range(KT):
                sp.dma_start(wgs[:, k, :], wg[k * P:(k + 1) * P, :]).then_inc(w_in, 16)
            sp.dma_start(wos[:, :, :], wo.rearrange("(h p) n -> p h n", p=P)).then_inc(w_in, 16)
            sp.dma_start(gb[:, 0:1], ln_g).then_inc(w_in, 16)
            sp.dma_start(gb[:, 1:2], ln_b).then_inc(w_in, 16)
            def turn(i):
                sp.wait_ge(g_done, i * H)
                sp.dma_start(xn[:, :, :], xnT[:, :, bass.ds(i * TOK, TOK)].rearrange("k p t -> p k t")).then_inc(xn_in, 16)
                sp.wait_ge(stored, i * 16)
                sp.dma_start(xs[:, 0, :, :], x[bass.ds(i * TOK, TOK), :].rearrange("(s p) d -> p s d", p=P)).then_inc(x_in, 16)
                for h in range(H):
                    if h >= 4:
                        sp.wait_ge(centred, i * H + h - 3)
                    else:
                        sp.wait_ge(centred, i * H)
                    sp.dma_start(o[:, h % 4, :], o_dram[h, :, bass.ds(i * TOK, TOK)]).then_inc(o_in[h % 4], 16)
                sp.wait_ge(added, (i + 1) * SUB)
                sp.dma_start(x_out[bass.ds(i * TOK, TOK), :].rearrange("(s p) d -> p s d", p=P), xs[:, 1, :, :]).then_inc(stored, 16)
            run_turns(sp, TT, turn)
            sp.wait_ge(stored, 16 * TT)

        @block.tensor
        def _(pe):
            pe.wait_ge(w_in, 16 * (KT + 3))
            pe.wait_ge(init, 2)
            def turn(i):
                pe.wait_ge(xn_in, (i + 1) * 16)
                for n in range(H + 3):
                    if n < H:
                        h = n
                        if h < 2:
                            pe.wait_ge(sg_done, i * H)
                        else:
                            pe.wait_ge(sg_done, i * H + h - 1)
                        for k in range(KT):
                            mm = pe.matmul(g_ps[:, h % 2, :], wgs[:, k, h * P:(h + 1) * P], xn[:, k, :], start=(k == 0), stop=(k == KT - 1))
                        mm.then_inc(g_done, 1)
                        pe.wait_ge(o_in[h % 4], i * 64 + (h // 4 + 1) * 16)
                        pe.wait_ge(centred, i * H + h)
                        pe.matmul(mean_ps[:, :], mean_w[:, :], o[:, h % 4, :], start=True, stop=True).then_inc(mean_done, 1)
                    if 1 <= n <= H:
                        h = n - 1
                        pe.wait_ge(squared, i * H + h + 1)
                        pe.wait_ge(sd_done, i * H + h)
                        pe.matmul(var_ps[:, :], mean_w[:, :], sq[:, h % 2, :], start=True, stop=True).then_inc(var_done, 1)
                    if n >= 3:
                        h = n - 3
                        if h == 0:
                            pe.wait_ge(added, i * SUB)
                        pe.wait_ge(of_done, i * H + h + 1)
                        for s in range(SUB):
                            mm = pe.matmul(out_ps[:, s, :], of[:, h % 2, s * P:(s + 1) * P], wos[:, h, :], start=(h == 0), stop=(h == H - 1))
                        mm.then_inc(out_done, 1)
            run_turns(pe, TT, turn)

        @block.scalar
        def _(act):
            act.wait_ge(init, 2)
            def turn(i):
                for n in range(H + 1):
                    if n < H:
                        h = n
                        act.wait_ge(g_done, i * H + h + 1)
                        act.wait_ge(of_done, i * H + max(h - 3, 0))
                        act.activation(sg[:, h % 4, :], g_ps[:, h % 2, :], ACT.Sigmoid).then_inc(sg_done, 1)
                    if n >= 1:
                        h = n - 1
                        act.wait_ge(var_done, i * H + h + 1)
                        act.wait_ge(rs_done, i * H + max(h - 1, 0))
                        act.activation(sd[:, h % 2, :], var_ps[:, :], ACT.Sqrt, bias=eps[:, 0:1]).then_inc(sd_done, 1)
            run_turns(act, TT, turn)

        @block.gpsimd
        def _(pool):
            def turn(i):
                for h in range(H):
                    pool.wait_ge(centred, i * H + h + 1)
                    pool.wait_ge(var_done, i * H + max(h - 1, 0))
                    pool.tensor_tensor(sq[:, h % 2, :], oc[:, h % 4, :], oc[:, h % 4, :], ALU.mult).then_inc(squared, 1)
            run_turns(pool, TT, turn)

        @block.vector
        def _(dve):
            dve.memset(mean_w[:, :], 1.0 / P).then_inc(init, 1)
            dve.memset(eps[:, :], EPS).then_inc(init, 1)
            dve.wait_ge(w_in, 16 * (KT + 3))
            def turn(i):
                for n in range(H + 2):
                    if n < H:
                        h = n
                        dve.wait_ge(mean_done, i * H + h + 1)
                        dve.wait_ge(squared, i * H + max(h - 3, 0))
                        dve.wait_ge(of_done, i * H + max(h - 3, 0))
                        dve.tensor_tensor(oc[:, h % 4, :], o[:, h % 4, :], mean_ps[:, :], ALU.subtract).then_inc(centred, 1)
                    if n >= 2:
                        h = n - 2
                        g = i * H + h
                        dve.wait_ge(sd_done, g + 1)
                        dve.wait_ge(norm_step, i * H + max(h - 1, 0))
                        dve.reciprocal(rs[:, h % 2, :], sd[:, h % 2, :]).then_inc(rs_done, 1)
                        dve.wait_ge(rs_done, g + 1)
                        dve.scalar_tensor_tensor(oc[:, h % 4, :], oc[:, h % 4, :], gb[:, 0:1], rs[:, h % 2, :], ALU.mult, ALU.mult).then_inc(norm_step, 1)
                        dve.wait_ge(norm_step, g + 1)
                        dve.wait_ge(sg_done, g + 1)
                        dve.wait_ge(out_done, i * H + max(h - 1, 0))
                        dve.scalar_tensor_tensor(of[:, h % 2, :], oc[:, h % 4, :], gb[:, 1:2], sg[:, h % 4, :], ALU.add, ALU.mult).then_inc(of_done, 1)
                dve.wait_ge(out_done, (i + 1) * H)
                dve.wait_ge(x_in, (i + 1) * 16)
                dve.wait_ge(stored, i * 16)
                for s in range(SUB):
                    dve.tensor_tensor(xs[:, 1, s, :], xs[:, 0, s, :], out_ps[:, s, :], ALU.add).then_inc(added, 1)
            run_turns(dve, TT, turn)


def ffn_phase(nc, phase, xnT, w1, w3, w2, hadamard, x, x_out, T, F):
    TT = T // TOK
    SUB = TOK // P
    FB = F // P
    with ExitStack() as ctx:
        m = Memory(nc, ctx, phase)
        w1s = m.sb("w1", [P, KT, F])
        w3s = m.sb("w3", [P, KT, F])
        w2a = m.sb("w2a", [P, FB, D])
        w2b = m.sb("w2b", [P, FB, D])
        had = m.sb("had", [P, P])
        xn = m.sb("xn", [P, KT, TOK])
        gate = m.sb("gate", [P, 2, TOK])
        hid = m.sb("hid", [P, 2, TOK])
        xs = m.sb("xs", [P, SUB, D])
        out_ps = m.ps("out", [P, SUB, D])
        g_ps = m.ps("g", [P, 2, TOK])
        l_ps = m.ps("l", [P, 2, TOK])
        w2_in = m.sem("w2_in")
        w_in = m.sem("w_in")
        xn_in = m.sem("xn_in")
        x_in = m.sem("x_in")
        had_done = m.sem("had_done")
        had_copied = m.sem("had_copied")
        fly = m.sem("fly")
        gate_done = m.sem("gate_done")
        lin_done = m.sem("lin_done")
        silu_done = m.sem("silu_done")
        hid_done = m.sem("hid_done")
        out_done = m.sem("out_done")
        added = m.sem("added")
        stored = m.sem("stored")
        block = ctx.enter_context(nc.Block())

        @block.sync
        def _(sp):
            sp.dma_start(w2a[:, :, :], w2.rearrange("(f p) n -> p f n", p=P)).then_inc(w2_in, 16)
            sp.dma_start(had[:, :], hadamard).then_inc(w2_in, 16)
            for k in range(KT):
                sp.dma_start(w1s[:, k, :], w1[k * P:(k + 1) * P, :]).then_inc(w_in, 16)
                sp.dma_start(w3s[:, k, :], w3[k * P:(k + 1) * P, :]).then_inc(w_in, 16)
            def turn(i):
                sp.wait_ge(lin_done, i * FB)
                sp.dma_start(xn[:, :, :], xnT[:, :, bass.ds(i * TOK, TOK)].rearrange("k p t -> p k t")).then_inc(xn_in, 16)
                sp.wait_ge(stored, i * 16)
                sp.dma_start(xs[:, :, :], x[bass.ds(i * TOK, TOK), :].rearrange("(s p) d -> p s d", p=P)).then_inc(x_in, 16)
                sp.wait_ge(added, (i + 1) * SUB)
                sp.dma_start(x_out[bass.ds(i * TOK, TOK), :].rearrange("(s p) d -> p s d", p=P), xs[:, :, :]).then_inc(stored, 16)
            run_turns(sp, TT, turn)
            sp.wait_ge(stored, 16 * TT)

        @block.tensor
        def _(pe):
            pe.wait_ge(w2_in, 32)
            for f in range(FB):
                if f >= 4:
                    pe.wait_ge(had_copied, f - 3)
                pe.matmul(out_ps[:, f % 4, :], had[:, :], w2a[:, f, :], start=True, stop=True).then_inc(had_done, 1)
            pe.wait_ge(w_in, 16 * 2 * KT)
            pe.wait_ge(had_copied, FB)
            pe.wait_ge(fly, 8)
            def turn(i):
                pe.wait_ge(xn_in, (i + 1) * 16)
                for n in range(FB + 1):
                    if n < FB:
                        pe.wait_ge(silu_done, i * FB + max(n - 1, 0))
                        for k in range(KT):
                            mm = pe.matmul(g_ps[:, n % 2, :], w1s[:, k, n * P:(n + 1) * P], xn[:, k, :], start=(k == 0), stop=(k == KT - 1))
                        mm.then_inc(gate_done, 1)
                        pe.wait_ge(hid_done, i * FB + max(n - 1, 0))
                        for k in range(KT):
                            mm = pe.matmul(l_ps[:, n % 2, :], w3s[:, k, n * P:(n + 1) * P], xn[:, k, :], start=(k == 0), stop=(k == KT - 1))
                        mm.then_inc(lin_done, 1)
                    if n >= 1:
                        f = n - 1
                        if f == 0:
                            pe.wait_ge(added, i * SUB)
                        pe.wait_ge(hid_done, i * FB + f + 1)
                        for s in range(SUB):
                            mm = pe.matmul(out_ps[:, s, :], hid[:, f % 2, s * P:(s + 1) * P], w2b[:, f, :], start=(f == 0), stop=(f == FB - 1))
                        mm.then_inc(out_done, 1)
            run_turns(pe, TT, turn)

        @block.scalar
        def _(act):
            for f in range(FB):
                act.wait_ge(had_done, f + 1)
                act.activation(w2b[:, f, :], out_ps[:, f % 4, :], ACT.Copy, scale=float(F) ** -0.5).then_inc(had_copied, 1)
            def turn(i):
                for n in range(FB):
                    act.wait_ge(gate_done, i * FB + n + 1)
                    act.wait_ge(hid_done, i * FB + max(n - 1, 0))
                    act.activation(gate[:, n % 2, :], g_ps[:, n % 2, :], ACT.Silu).then_inc(silu_done, 1)
            run_turns(act, TT, turn)

        @block.vector
        def _(dve):
            dve.wait_ge(had_copied, FB)
            src, dst = w2b, w2a
            for stage in range(4):
                step = 1 << stage
                dve.wait_ge(fly, 2 * stage)
                s = src[:, :, :].rearrange("p (a two b) n -> p a two (b n)", two=2, b=step)
                d = dst[:, :, :].rearrange("p (a two b) n -> p a two (b n)", two=2, b=step)
                dve.tensor_tensor(d[:, :, 0], s[:, :, 0], s[:, :, 1], ALU.add).then_inc(fly, 1)
                dve.tensor_tensor(d[:, :, 1], s[:, :, 0], s[:, :, 1], ALU.subtract).then_inc(fly, 1)
                src, dst = dst, src
            def turn(i):
                for n in range(FB):
                    dve.wait_ge(silu_done, i * FB + n + 1)
                    dve.wait_ge(lin_done, i * FB + n + 1)
                    dve.wait_ge(out_done, i * FB + max(n - 1, 0))
                    dve.tensor_tensor(hid[:, n % 2, :], gate[:, n % 2, :], l_ps[:, n % 2, :], ALU.mult).then_inc(hid_done, 1)
                dve.wait_ge(out_done, (i + 1) * FB)
                dve.wait_ge(x_in, (i + 1) * 16)
                for s in range(SUB):
                    dve.tensor_tensor(xs[:, s, :], xs[:, s, :], out_ps[:, s, :], ALU.add).then_inc(added, 1)
            run_turns(dve, TT, turn)


H = 16
C = 16
RING = 128
CHUNK = RING // 2
BPC = CHUNK // C
BPR = RING // C
GH = P // C
ROWS = 4
NR = C // ROWS
KB, QQ, KK, VB, AA = range(5)


def scan_phase(nc, streams, decays, o_dram, ident, head_mask, T):
    NB = T // C
    TURNS = T // RING
    with ExitStack() as ctx:
        m = Memory(nc, ctx, "scan")
        sb, ps, sem = m.sb, m.ps, m.sem
        ring = sb("ring", [P, 5, H, RING])
        blk = sb("blk", [P, 2, 5, C, H])
        stage = sb("stage", [P, 2, ROWS * ROWS * H * (NR * (NR + 1) // 2)])
        krow = sb("krow", [P, 2, C, C + 2, H])
        qrow = sb("qrow", [P, 2, C, C + 1, H])
        ud = sb("ud", [P, C, C + 2, H])
        prod = sb("prod", [P, (C + 1) * H])
        ktin = sb("ktin", [P, 2, C, GH])
        last_ud = sb("last_ud", [P, 2, C + 1, GH])
        ST = sb("ST", [P, H, P])
        abar = sb("abar", [P, H, P])
        kbd = sb("kbd", [P, 2, GH, P])
        uT = sb("uT", [P, 2, P])
        oring = sb("oring", [P, H, RING])
        idt = sb("idt", [P, P])
        ones = sb("ones", [P, P])
        hmask = sb("hmask", [P, GH])

        bc_ps = ps("bc_ps", [P, 2, 512])
        pq_ps = ps("pq_ps", [P, H, 2, C])
        tr_ps = ps("tr_ps", [P, 4, P])
        ds_ps = ps("ds_ps", [P, 4, 4, P])

        const_in = sem("const_in")
        init_done = sem("init_done")
        ud_zeroed = sem("ud_zeroed")
        chunk_in = [sem("chunk_in0"), sem("chunk_in1")]
        blk_ready = sem("blk_ready")
        kk_staged = sem("kk_staged")
        qk_staged = sem("qk_staged")
        bcast_done = sem("bcast_done")
        bcast_evac = sem("bcast_evac")
        kt_done = sem("kt_done")
        kbd_ready = sem("kbd_ready")
        pq_done = sem("pq_done")
        p_copied = sem("p_copied")
        q_copied = sem("q_copied")
        abar_in = sem("abar_in")
        u_step = sem("u_step")
        dec_step = sem("dec_step")
        dot_step = sem("dot_step")
        ut_done = sem("ut_done")
        ut_copied = sem("ut_copied")
        ds_done = sem("ds_done")
        s_decayed = sem("s_decayed")
        s_added = sem("s_added")
        po_done = sem("po_done")
        o_reduced = sem("o_reduced")
        o_stored = [sem("o_stored0"), sem("o_stored1")]
        NINIT = 5
        soff = [ROWS * ROWS * H * (r * (r + 1) // 2) for r in range(NR)]
        npair = [ROWS * (r + 1) for r in range(NR)]

        def stage_rows(eng, w, r, u):
            n = npair[r]
            left = blk[:, u % 2, w, ROWS * r:ROWS * (r + 1), :].unsqueeze(2).to_broadcast([P, ROWS, n, H])
            right = blk[:, u % 2, KK, 0:n, :].unsqueeze(1).to_broadcast([P, ROWS, n, H])
            out = stage[:, w, soff[r]:soff[r] + ROWS * n * H].rearrange("p (t j h) -> p t j h", t=ROWS, h=H)
            return eng.tensor_tensor(out, left, right, ALU.mult)

        def run(eng, prologue, body):
            prologue()
            for u in range(BPR):
                body(0, u, 2)
            with eng.Fori(1, TURNS - 1) as it:
                for u in range(BPR):
                    body(it, u, 2)
            for u in range(BPR):
                body(TURNS - 1, u, BPR - 1 - u)

        block = ctx.enter_context(nc.Block())

        @block.sync
        def _(sp):
            sp.dma_start(idt[:, :], ident).then_inc(const_in, 16)
            sp.dma_start(hmask[:, :], head_mask).then_inc(const_in, 16)

            def load(it, half):
                for w in range(5):
                    sp.dma_start(ring[:, w, :, half * CHUNK:(half + 1) * CHUNK],
                                 streams[w][:, :, bass.ds(it * RING + half * CHUNK, CHUNK)]
                                 .rearrange("h p t -> p h t")).then_inc(chunk_in[half], 16)

            def store(it, half):
                sp.wait_ge(o_reduced, ((it * 2 + half + 1) * BPC) * NR)
                sp.dma_start(o_dram[:, :, bass.ds(it * RING + half * CHUNK, CHUNK)]
                             .rearrange("h p t -> p h t"),
                             oring[:, :, half * CHUNK:(half + 1) * CHUNK]).then_inc(o_stored[half], 16)
            def load_abar(b):
                sp.dma_start(abar[:, :, :].rearrange("p h i -> p (h i)"),
                             decays[bass.ds(b, 1), :].to_broadcast([P, H * P])).then_inc(abar_in, 16)
            load(0, 0)
            load(0, 1)
            load_abar(0)
            with sp.Fori(0, TURNS - 1) as it:
                for u in range(BPR):
                    sp.wait_ge(s_decayed, 4 * (it * BPR + u + 1))
                    load_abar(it * BPR + u + 1)
                    if u % BPC == BPC - 1:
                        sp.wait_ge(blk_ready, it * BPR + u + 1)
                        load(it + 1, u // BPC)
                        store(it, u // BPC)
            for u in range(BPR):
                if u < BPR - 1:
                    sp.wait_ge(s_decayed, 4 * (NB - BPR + u + 1))
                    load_abar(NB - BPR + u + 1)
                if u % BPC == BPC - 1:
                    store(TURNS - 1, u // BPC)
            for half in range(2):
                sp.wait_ge(o_stored[half], 16 * TURNS)

        @block.scalar
        def _(act):
            def copy_block(it, u):
                it, u = (it + 1, u - BPR) if u >= BPR else (it, u)
                b = it * BPR + u
                act.wait_ge(chunk_in[u // BPC], 80 * (it + 1))
                if not (isinstance(b, int) and b < 1):
                    act.wait_ge(kt_done, b)
                if not (isinstance(b, int) and b < 2):
                    act.wait_ge(pq_done, b - 1)
                    act.wait_ge(u_step, C * (b - 1))
                    act.wait_ge(dec_step, C * (b - 1))
                act.activation(krow[:, u % 2, :, 0, :].rearrange("p t h -> p h t"),
                               ring[:, VB, :, u * C:(u + 1) * C], ACT.Copy)
                act.activation(blk[:, u % 2].rearrange("p w t h -> p w h t"),
                               ring[:, :, :, u * C:(u + 1) * C], ACT.Copy)
                for g in range(2):
                    last = act.activation(ktin[:, g].rearrange("p t h -> p h t"),
                                          ring[:, KK, g * GH:(g + 1) * GH, u * C:(u + 1) * C], ACT.Copy)
                last.then_inc(blk_ready, 1)

            def spread(it, u):
                it, u = (it + 1, u - BPR) if u >= BPR else (it, u)
                b = it * BPR + u
                n = 0
                for r in range(NR):
                    for w in range(2):
                        for p in range(2):
                            act.wait_ge(bcast_done, 16 * b + n + 1)
                            t = r * ROWS + 2 * p
                            rows = (krow[:, u % 2, t:t + 2, 2:2 + npair[r], :], qrow[:, u % 2, t:t + 2, 1:1 + npair[r], :])
                            act.activation(rows[w],
                                           bc_ps[:, n % 2, 0:2 * npair[r] * H]
                                           .rearrange("p (t j h) -> p t j h", t=2, h=H),
                                           ACT.Copy, scale=(-1.0, 1.0)[w]).then_inc(bcast_evac, 1)
                            n += 1

            def block_diagonal(it, u):
                it, u = (it + 1, u - BPR) if u >= BPR else (it, u)
                b = it * BPR + u
                act.wait_ge(kt_done, b + 1)
                if not (isinstance(b, int) and b < 1):
                    act.wait_ge(ds_done, 4 * b)
                for g in range(2):
                    for h in range(GH):
                        last = act.activation(kbd[:, g, h, :], tr_ps[:, g, :], ACT.Copy,
                                              scale=hmask[:, h:h + 1])
                last.then_inc(kbd_ready, 1)

            def prologue():
                act.wait_ge(const_in, 32)
                act.wait_ge(init_done, NINIT)
                copy_block(0, 0)
                spread(0, 0)
                block_diagonal(0, 0)
                copy_block(0, 1)

            def body(it, u, left):
                b = it * BPR + u
                first = isinstance(b, int) and b == 0
                act.wait_ge(pq_done, b + 1)
                act.activation(krow[:, u % 2, :, 1, :].rearrange("p t h -> p h t"), pq_ps[:, :, 0, :], ACT.Copy,
                               scale=-1.0).then_inc(p_copied, 1)
                act.activation(qrow[:, u % 2, :, 0, :].rearrange("p t h -> p h t"), pq_ps[:, :, 1, :], ACT.Copy).then_inc(q_copied, 1)
                if left >= 1:
                    if not first:
                        act.wait_ge(o_reduced, NR * b)
                    spread(it, u + 1)
                act.wait_ge(ut_done, b + 1)
                act.activation(uT[:, :, :], tr_ps[:, 2:4, :], ACT.Copy).then_inc(ut_copied, 1)
                if left >= 2:
                    copy_block(it, u + 2)
                if left >= 1:
                    block_diagonal(it, u + 1)
            run(act, prologue, body)

        @block.tensor
        def _(pe):
            def prep(it, u):
                it, u = (it + 1, u - BPR) if u >= BPR else (it, u)
                b = it * BPR + u
                pe.wait_ge(blk_ready, b + 1)
                if not (isinstance(b, int) and b < 1):
                    pe.wait_ge(kbd_ready, b)
                for g in range(2):
                    tr = pe.transpose(tr_ps[:, g, :], ktin[:, g].rearrange("p t h -> p (t h)"), idt[:, :])
                tr.then_inc(kt_done, 1)
                n = 0
                for r in range(NR):
                    for w in range(2):
                        pe.wait_ge((kk_staged, qk_staged)[w], NR * b + r + 1)
                        for p in range(2):
                            if isinstance(b, int) and 16 * b + n < 2:
                                pass
                            else:
                                pe.wait_ge(bcast_evac, 16 * b + n - 1)
                            m = 2 * npair[r] * H
                            pe.matmul(bc_ps[:, n % 2, 0:m], ones[:, :],
                                      stage[:, w, soff[r] + p * m:soff[r] + (p + 1) * m],
                                      start=True, stop=True).then_inc(bcast_done, 1)
                            n += 1

            def prologue():
                pe.wait_ge(const_in, 32)
                pe.wait_ge(init_done, NINIT)
                prep(0, 0)

            def body(it, u, left):
                b = it * BPR + u
                first = isinstance(b, int) and b == 0
                if not first:
                    pe.wait_ge(p_copied, b)
                    pe.wait_ge(q_copied, b)
                for q in range(4):
                    if not first:
                        pe.wait_ge(s_added, 4 * (b - 1) + q + 1)
                    for h in range(4 * q, 4 * q + 4):
                        m = pe.matmul(pq_ps[:, h], ST[:, h, :], blk[:, u % 2, 0:2, :, h], start=True, stop=True)
                m.then_inc(pq_done, 1)
                if left >= 1:
                    prep(it, u + 1)
                pe.wait_ge(u_step, C * (b + 1))
                pe.wait_ge(dec_step, C * (b + 1))
                for g in range(2):
                    tr = pe.transpose(tr_ps[:, 2 + g, :], last_ud[:, g, 1:C + 1, :].rearrange("p t h -> p (t h)"), idt[:, :])
                tr.then_inc(ut_done, 1)
                pe.wait_ge(kbd_ready, b + 1)
                pe.wait_ge(ut_copied, b + 1)
                for q in range(4):
                    for h in range(4):
                        m = pe.matmul(ds_ps[:, q, h, :], kbd[:, q // 2, 4 * (q % 2) + h, :], uT[:, q // 2, :],
                                      start=True, stop=True)
                    m.then_inc(ds_done, 1)
            run(pe, prologue, body)

        @block.gpsimd
        def _(pool):
            def stage_kk(it, u):
                it, u = (it + 1, u - BPR) if u >= BPR else (it, u)
                b = it * BPR + u
                pool.wait_ge(blk_ready, b + 1)
                for r in range(NR):
                    if not (isinstance(b, int) and b < 1):
                        pool.wait_ge(bcast_done, 16 * (b - 1) + 4 * r + 2)
                    stage_rows(pool, 0, r, u).then_inc(kk_staged, 1)

            def prologue():
                pool.memset(ud[:, :, :, :], 0.0).then_inc(ud_zeroed, 1)
                pool.wait_ge(ud_zeroed, 1)
                pool.memset(ud[:, :, 0, :], 1.0).then_inc(ud_zeroed, 1)
                pool.wait_ge(ud_zeroed, 2)
                pool.memset(ud[:, 0, 1, :], 1.0).then_inc(init_done, 1)
                pool.memset(krow[:, :, :, :, :], 0.0).then_inc(init_done, 1)
                pool.memset(qrow[:, :, :, :, :], 0.0).then_inc(init_done, 1)
                pool.wait_ge(init_done, NINIT)
                stage_kk(0, 0)
                stage_kk(0, 1)

            def body(it, u, left):
                b = it * BPR + u
                first = isinstance(b, int) and b == 0
                if not first:
                    pool.wait_ge(po_done, (NR + 1) * b)
                    pool.wait_ge(ut_done, b)
                    pool.wait_ge(u_step, C * b)
                for t in range(C):
                    if t:
                        pool.wait_ge(u_step, C * b + t)
                        pool.wait_ge(dec_step, C * b + t)
                    decay = blk[:, u % 2, AA, t, :].unsqueeze(1).to_broadcast([P, t + 1, H])
                    if t < C - 1:
                        pool.tensor_tensor(ud[:, t + 1, 1:t + 2, :], ud[:, t, 1:t + 2, :], decay, ALU.mult).then_inc(dec_step, 1)
                    else:
                        pool.tensor_tensor(last_ud[:, :, 0:C, :].rearrange("p g s h -> p s g h"),
                                           ud[:, t, 1:t + 2, :].rearrange("p s (g h) -> p s g h", g=2),
                                           decay.rearrange("p s (g h) -> p s g h", g=2), ALU.mult).then_inc(dec_step, 1)
                pool.wait_ge(u_step, C * (b + 1))
                pool.wait_ge(dec_step, C * (b + 1))
                pool.wait_ge(q_copied, b + 1)
                for r in range(NR):
                    t, n, m = ROWS * r, ROWS * (r + 1) + 1, ROWS - (r == NR - 1)
                    pool.tensor_tensor(qrow[:, u % 2, t:t + m, 0:n, :], qrow[:, u % 2, t:t + m, 0:n, :],
                                       ud[:, t + 1:t + 1 + m, 1:n + 1, :], ALU.mult).then_inc(po_done, 1)
                pool.tensor_tensor(qrow[:, u % 2, C - 1].rearrange("p s (g h) -> p s g h", g=2),
                                   qrow[:, u % 2, C - 1].rearrange("p s (g h) -> p s g h", g=2),
                                   last_ud[:, :, :, :].rearrange("p g s h -> p s g h"), ALU.mult).then_inc(po_done, 1)
                if left >= 2:
                    stage_kk(it, u + 2)
            run(pool, prologue, body)

        @block.vector
        def _(dve):
            def stage_qk(it, u):
                it, u = (it + 1, u - BPR) if u >= BPR else (it, u)
                b = it * BPR + u
                dve.wait_ge(blk_ready, b + 1)
                for r in range(NR):
                    if not (isinstance(b, int) and b < 1):
                        dve.wait_ge(bcast_done, 16 * (b - 1) + 4 * r + 4)
                    stage_rows(dve, 1, r, u).then_inc(qk_staged, 1)

            def prologue():
                dve.memset(ST[:, :, :], 0.0).then_inc(init_done, 1)
                dve.memset(ones[:, :], 1.0).then_inc(init_done, 1)
                dve.wait_ge(init_done, NINIT)
                stage_qk(0, 0)
                stage_qk(0, 1)

            def body(it, u, left):
                b = it * BPR + u
                first = isinstance(b, int) and b == 0
                dve.wait_ge(p_copied, b + 1)
                dve.wait_ge(bcast_evac, 16 * (b + 1))
                if not first:
                    dve.wait_ge(po_done, (NR + 1) * b)
                    dve.wait_ge(ut_done, b)
                for t in range(C):
                    if not (first and t == 0):
                        dve.wait_ge(dec_step, C * b + t)
                        dve.wait_ge(u_step, C * b + t)
                    n = (t + 2) * H
                    step = C * b + t
                    dve.tensor_tensor(prod[:, 0:n].rearrange("p (s h) -> p s h", h=H),
                                      krow[:, u % 2, t, 0:t + 2, :], ud[:, t, 0:t + 2, :],
                                      ALU.mult).then_inc(dot_step, 1)
                    dve.wait_ge(dot_step, step + 1)
                    if t < C - 1:
                        dve.tensor_reduce(ud[:, t + 1, t + 2, :], prod[:, 0:n].rearrange("p (s h) -> p h s", h=H),
                                          AX.X, ALU.add).then_inc(u_step, 1)
                    else:
                        dve.tensor_reduce(last_ud[:, :, C, :], prod[:, 0:n].rearrange("p (s g h) -> p g h s", g=2, h=GH),
                                          AX.X, ALU.add).then_inc(u_step, 1)
                dve.wait_ge(abar_in, 16 * (b + 1))
                dve.wait_ge(pq_done, b + 1)
                if not first:
                    dve.wait_ge(s_added, 4 * b)
                for q in range(4):
                    h = slice(4 * q, 4 * q + 4)
                    dve.tensor_tensor(ST[:, h, :], ST[:, h, :], abar[:, h, :], ALU.mult).then_inc(s_decayed, 1)
                for q in range(4):
                    h = slice(4 * q, 4 * q + 4)
                    dve.wait_ge(s_decayed, 4 * b + q + 1)
                    dve.wait_ge(ds_done, 4 * b + q + 1)
                    dve.tensor_tensor(ST[:, h, :], ST[:, h, :], ds_ps[:, q], ALU.add).then_inc(s_added, 1)
                if left >= 2:
                    stage_qk(it, u + 2)
                half = u // BPC
                if u % BPC == 0 and not (isinstance(it, int) and it == 0):
                    dve.wait_ge(o_stored[half], 16 * it)
                for r in range(NR):
                    t, n = ROWS * r, ROWS * (r + 1) + 1
                    dve.wait_ge(po_done, (NR + 1) * b + r + 1 + (r == NR - 1))
                    dve.tensor_reduce(oring[:, :, u * C + t:u * C + t + ROWS].rearrange("p h t -> p t h"),
                                      qrow[:, u % 2, t:t + ROWS, 0:n, :].rearrange("p t s h -> p t h s"),
                                      AX.X, ALU.add).then_inc(o_reduced, 1)
            run(dve, prologue, body)


NEG = -1.0e30
FIRST_BIG = 1.0e30


def rope_phase(nc, xnT, w_rot, wv, cos, sin, qk_dram, v_dram, T):
    phase = "rope"
    TT = T // TOK
    NT = T // P
    CB = D // P
    with ExitStack() as ctx:
        m = Memory(nc, ctx, phase)
        xn = m.sb("xn", [P, KT, T])
        w = m.sb("w", [P, 4, KT, D])
        wvs = m.sb("wv", [P, KT, D])
        tab = m.sb("tab", [P, 2, T])
        part = m.sb("part", [P, 2, 2, TOK])
        rot = m.sb("rot", [P, 4, TOK])
        high = m.sb("high", [P, 4, TOK], F32R)
        low = m.sb("low", [P, 4, TOK], F32R)
        vrow = m.sb("vrow", [P, 4, D])
        acc = m.ps("acc", [P, 3, 2, TOK])
        v_ps = m.ps("v_ps", [P, 2, D])
        loaded = m.sem("loaded")
        pair_done = m.sem("pair_done")
        turned = m.sem("turned")
        rot_done = m.sem("rot_done")
        rot_stored = [m.sem(f"rot_stored{i}") for i in range(4)]
        high_done = m.sem("high_done")
        low_done = m.sem("low_done")
        v_done = m.sem("v_done")
        v_copied = m.sem("v_copied")
        v_stored = [m.sem(f"v_stored{i}") for i in range(4)]
        NLOAD = 2 * KT + 4 * KT + 2
        units = [(c, j, t) for c in range(CB) for j in range(2) for t in range(TT)]
        block = ctx.enter_context(nc.Block())

        @block.sync
        def _(sp):
            for k in range(KT):
                sp.dma_start(xn[:, k, :], xnT[k]).then_inc(loaded, 16)
                sp.dma_start(wvs[:, k, :], wv[k * P:(k + 1) * P, :]).then_inc(loaded, 16)
                for j in range(4):
                    sp.dma_start(w[:, j, k, :], w_rot[j][k * P:(k + 1) * P, :]).then_inc(loaded, 16)
            sp.dma_start(tab[:, 0, :], cos).then_inc(loaded, 16)
            sp.dma_start(tab[:, 1, :], sin).then_inc(loaded, 16)
            for n, (c, j, t) in enumerate(units):
                sp.wait_ge(high_done, n + 1)
                sp.dma_start(qk_dram[j, 0, c * P:(c + 1) * P, t * TOK:(t + 1) * TOK], high[:, n % 4, :].bitcast(F32)).then_inc(rot_stored[n % 4], 16)
                sp.wait_ge(low_done, n + 1)
                sp.dma_start(qk_dram[j, 1, c * P:(c + 1) * P, t * TOK:(t + 1) * TOK], low[:, n % 4, :].bitcast(F32)).then_inc(rot_stored[n % 4], 16)
                if n % 2:
                    v = n // 2
                    sp.wait_ge(v_copied, v + 1)
                    sp.dma_start(v_dram[v * P:(v + 1) * P, :], vrow[:, v % 4, :]).then_inc(v_stored[v % 4], 16)
            for r in range(4):
                sp.wait_ge(rot_stored[r], 32 * (len(units) // 4))
                sp.wait_ge(v_stored[r], 16 * (NT // 4))

        @block.tensor
        def _(pe):
            pe.wait_ge(loaded, 16 * NLOAD)
            for n, (c, j, t) in enumerate(units):
                if n >= 3:
                    pe.wait_ge(rot_done, n - 2)
                for r in range(2):
                    for k in range(KT):
                        mm = pe.matmul(acc[:, n % 3, r, :], w[:, 2 * j + r, k, c * P:(c + 1) * P],
                                       xn[:, k, t * TOK:(t + 1) * TOK], start=(k == 0), stop=(k == KT - 1))
                mm.then_inc(pair_done, 1)
                if n % 2:
                    v = n // 2
                    if v >= 2:
                        pe.wait_ge(v_copied, v - 1)
                    for k in range(KT):
                        mm = pe.matmul(v_ps[:, v % 2, :], xn[:, k, v * P:(v + 1) * P], wvs[:, k, :], start=(k == 0), stop=(k == KT - 1))
                    mm.then_inc(v_done, 1)

        @block.vector
        def _(dve):
            dve.wait_ge(loaded, 16 * NLOAD)
            for n, (c, j, t) in enumerate(units):
                dve.wait_ge(pair_done, n + 1)
                if n >= 2:
                    dve.wait_ge(rot_done, n - 1)
                for r in range(2):
                    dve.tensor_tensor(part[:, n % 2, r, :], acc[:, n % 3, r, :], tab[:, r, t * TOK:(t + 1) * TOK], ALU.mult).then_inc(turned, 1)
                dve.wait_ge(turned, 2 * n + 2)
                if n >= 4:
                    dve.wait_ge(low_done, n - 3)
                dve.tensor_tensor(rot[:, n % 4, :], part[:, n % 2, 0, :], part[:, n % 2, 1, :], ALU.add).then_inc(rot_done, 1)

        @block.scalar
        def _(act):
            for n in range(len(units)):
                act.wait_ge(rot_done, n + 1)
                if n >= 4:
                    act.wait_ge(rot_stored[n % 4], 32 * (n // 4))
                    act.wait_ge(low_done, n - 3)
                act.activation(high[:, n % 4, :], rot[:, n % 4, :], ACT.Copy).then_inc(high_done, 1)
                if n % 2:
                    v = n // 2
                    act.wait_ge(v_done, v + 1)
                    if v >= 4:
                        act.wait_ge(v_stored[v % 4], 16 * (v // 4))
                    act.activation(vrow[:, v % 4, :], v_ps[:, v % 2, :], ACT.Copy).then_inc(v_copied, 1)

        @block.gpsimd
        def _(pool):
            for n in range(len(units)):
                pool.wait_ge(high_done, n + 1)
                if n >= 4:
                    pool.wait_ge(rot_stored[n % 4], 32 * (n // 4))
                pool.tensor_tensor(low[:, n % 4, :], rot[:, n % 4, :], high[:, n % 4, :].bitcast(F32), ALU.subtract).then_inc(low_done, 1)


def chunks_of(q):
    n = (q + 1) * P
    return [(c, min(TOK, n - c)) for c in range(0, n, TOK)]


def load_stacks(sp, dst, qk_dram, h, DH, done):
    for j, halves in ((0, (0, 1, 0)), (1, (0, 0, 1))):
        for s, half in enumerate(halves):
            sp.dma_start(dst[s * DH:(s + 1) * DH, j, :].bitcast(F32), qk_dram[j, half, bass.ds(h * DH, DH), :]).then_inc(done, 16)


def column_sum_phase(nc, qk_dram, causal, sums, T, NH, DH):
    phase = "csum"
    NT = T // P
    NC = T // TOK
    SCALE = float(DH) ** -0.5
    order = list(range(NT - 1, -1, -1))
    with ExitStack() as ctx:
        m = Memory(nc, ctx, phase)
        qk = m.sb("qk", [3 * DH, 2, 2, T], F32R)
        cm = m.sb("cm", [P, 2, P], F32R)
        cmf = m.sb("cmf", [P, 2, P])
        e = m.sb("e", [P, 2, T])
        mx = m.sb("mx", [P, 2])
        nb = m.sb("nb", [P, 2])
        rsum = m.sb("rsum", [P, 2])
        rinv = m.sb("rinv", [P, 2])
        tot = m.sb("tot", [P, T])
        ones = m.sb("ones", [P, 1])
        row = m.sb("row", [1, T])
        sc = m.ps("sc", [P, 2, T])
        cm_in = m.sem("cm_in")
        init = m.sem("init")
        qk_in = [m.sem("qk_in0"), m.sem("qk_in1")]
        scored = m.sem("scored")
        maxed = m.sem("maxed")
        biased = m.sem("biased")
        expd = m.sem("expd")
        inverted = m.sem("inverted")
        totalled = m.sem("totalled")
        summed = m.sem("summed")
        row_done = m.sem("row_done")
        row_stored = m.sem("row_stored")
        block = ctx.enter_context(nc.Block())
        TILES = NT

        @block.sync
        def _(sp):

            for j in range(2):
                sp.dma_start(cmf[:, j, :], causal[j]).then_inc(cm_in, 16)

            def load(h, u):
                load_stacks(sp, qk[:, u], qk_dram, h, DH, qk_in[u])
            load(0, 0)
            load(1, 1)
            def turn(i):
                for u in range(2):
                    sp.wait_ge(summed, i * 2 + u + 1)
                    load(i * 2 + u + 2, u)
                    sp.wait_ge(row_done, i * 2 + u + 1)
                    sp.dma_start(sums[bass.ds(i * 2 + u, 1), :], row[:, :]).then_inc(row_stored, 16)
            run_turns(sp, NH // 2 - 1, turn)
            for u in range(2):
                sp.wait_ge(row_done, NH - 1 + u)
                sp.dma_start(sums[NH - 2 + u:NH - 1 + u, :], row[:, :]).then_inc(row_stored, 16)
            sp.wait_ge(row_stored, 16 * NH)

        @block.tensor
        def _(pe):
            pe.wait_ge(init, 3)
            def turn(i):
                for u in range(2):
                    h = i * 2 + u
                    pe.wait_ge(qk_in[u], (i + 1) * 96)
                    for n, q in enumerate(order):
                        g = h * TILES + n
                        if n >= 2:
                            pe.wait_ge(expd, g - 1)
                        else:
                            pe.wait_ge(expd, h * TILES)
                            pe.wait_ge(row_done, h)
                        for c, w in chunks_of(q):
                            pe.matmul(sc[:, n % 2, c:c + w], qk[:, u, 0, q * P:(q + 1) * P], qk[:, u, 1, c:c + w],
                                      start=True, stop=(c + w < (q + 1) * P))
                        mm = pe.matmul(sc[:, n % 2, q * P:(q + 1) * P], cm[:, 0, :], cm[:, 1, :], start=False, stop=True)
                        mm.then_inc(scored, 1)
                    pe.wait_ge(totalled, (h + 1) * TILES)
                    pe.wait_ge(expd, (h + 1) * TILES)
                    for c in range(NC):
                        mm = pe.matmul(sc[0:1, 0, c * TOK:(c + 1) * TOK], ones[:, :], tot[:, c * TOK:(c + 1) * TOK], start=True, stop=True)
                    mm.then_inc(summed, 1)
            run_turns(pe, NH // 2, turn)

        @block.scalar
        def _(act):
            def turn(i):
                for u in range(2):
                    h = i * 2 + u
                    for n, q in enumerate(order):
                        g = h * TILES + n
                        act.wait_ge(biased, g + 1)
                        act.wait_ge(totalled, h * TILES + max(n - 1, 0))
                        act.activation(e[:, n % 2, 0:(q + 1) * P], sc[:, n % 2, 0:(q + 1) * P], ACT.Exp,
                                       bias=nb[:, n % 2:n % 2 + 1], scale=SCALE, accum_out=rsum[:, n % 2:n % 2 + 1]).then_inc(expd, 1)
                    act.wait_ge(summed, h + 1)
                    act.wait_ge(row_stored, h * 16)
                    act.activation(row[:, :], sc[0:1, 0, :], ACT.Copy).then_inc(row_done, 1)
            run_turns(act, NH // 2, turn)

        @block.vector
        def _(dve):
            dve.memset(ones[:, :], 1.0).then_inc(init, 1)
            dve.wait_ge(cm_in, 32)
            dve.tensor_copy(cm[:, 0, :], cmf[:, 0, :]).then_inc(init, 1)
            dve.tensor_copy(cm[:, 1, :], cmf[:, 1, :]).then_inc(init, 1)
            def turn(i):
                for u in range(2):
                    h = i * 2 + u

                    def peak(n, q):
                        g = h * TILES + n
                        dve.wait_ge(scored, g + 1)
                        dve.tensor_reduce(mx[:, n % 2:n % 2 + 1], sc[:, n % 2, 0:(q + 1) * P], AX.X, ALU.max).then_inc(maxed, 1)
                        dve.wait_ge(maxed, g + 1)
                        dve.wait_ge(expd, h * TILES + max(n - 1, 0))
                        dve.tensor_scalar(nb[:, n % 2:n % 2 + 1], mx[:, n % 2:n % 2 + 1], -SCALE, None, ALU.mult).then_inc(biased, 1)

                    def total(n, q):
                        g = h * TILES + n
                        w = (q + 1) * P
                        dve.wait_ge(expd, g + 1)
                        dve.wait_ge(totalled, g)
                        dve.reciprocal(rinv[:, n % 2:n % 2 + 1], rsum[:, n % 2:n % 2 + 1]).then_inc(inverted, 1)
                        dve.wait_ge(inverted, g + 1)
                        if n == 0:
                            dve.wait_ge(summed, h)
                            dve.tensor_scalar(tot[:, 0:w], e[:, n % 2, 0:w], rinv[:, n % 2:n % 2 + 1], None, ALU.mult).then_inc(totalled, 1)
                        else:
                            dve.scalar_tensor_tensor(tot[:, 0:w], e[:, n % 2, 0:w], rinv[:, n % 2:n % 2 + 1], tot[:, 0:w],
                                                     ALU.mult, ALU.add).then_inc(totalled, 1)
                    for n, q in enumerate(order):
                        peak(n, q)
                        if n:
                            total(n - 1, order[n - 1])
                    total(NT - 1, order[-1])
            run_turns(dve, NH // 2, turn)


def heavy_phase(nc, sums, bias_dram, biasT_dram, ident, T, NH, BUDGET):
    phase = "heavy"
    ROUNDS = -(-BUDGET // 8)
    REST = BUDGET - 8 * (ROUNDS - 1)
    with ExitStack() as ctx:
        m = Memory(nc, ctx, phase)
        s = m.sb("s", [NH, T])
        top = m.sb("top", [NH, 8])
        bias = m.sb("bias", [NH, T])
        idt = m.sb("ident", [NH, NH])
        biasT = m.sb("biasT", [P, NH, T // P])
        tr = m.ps("tr", [P, T // P, NH])
        s_in = m.sem("s_in")
        turned = m.sem("turned")
        copied = m.sem("copied")
        step = m.sem("step")
        bias_done = m.sem("bias_done")
        stored = m.sem("stored")
        block = ctx.enter_context(nc.Block())

        @block.sync
        def _(sp):
            sp.dma_start(s[:, :], sums).then_inc(s_in, 16)
            sp.dma_start(idt[:, :], ident[0:NH, 0:NH]).then_inc(s_in, 16)
            sp.wait_ge(bias_done, 1)
            sp.dma_start(bias_dram, bias[:, :]).then_inc(stored, 16)
            sp.wait_ge(copied, 1)
            sp.dma_start(biasT_dram.rearrange("h p n -> p h n"), biasT[:, :, :]).then_inc(stored, 16)
            sp.wait_ge(stored, 32)

        @block.tensor
        def _(pe):
            pe.wait_ge(s_in, 32)
            pe.wait_ge(bias_done, 1)
            for n in range(T // P):
                t = pe.transpose(tr[:, n, :], bias[:, n * P:(n + 1) * P], idt[:, :])
            t.then_inc(turned, 1)

        @block.scalar
        def _(act):
            act.wait_ge(turned, 1)
            act.activation(biasT[:, :, :].rearrange("p h n -> p n h"), tr[:, :, :], ACT.Copy).then_inc(copied, 1)

        @block.vector
        def _(dve):
            dve.wait_ge(s_in, 32)
            for r in range(ROUNDS):
                if r:
                    dve.wait_ge(step, 2 * r)
                dve.max(top[:, :], s[:, :]).then_inc(step, 1)
                dve.wait_ge(step, 2 * r + 1)
                if r == ROUNDS - 1 and REST < 8:
                    dve.memset(top[:, REST:8], -1.0).then_inc(step, 1)
                    dve.wait_ge(step, 2 * r + 2)
                dve.match_replace(s[:, :], top[:, :], s[:, :], -1.0).then_inc(step, 1)
            dve.wait_ge(step, 2 * ROUNDS + (REST < 8))
            dve.tensor_scalar(bias[:, :], s[:, :], 0.0, NEG, ALU.is_ge, ALU.mult).then_inc(bias_done, 1)


def chosen_max_phase(nc, qk_dram, bias_dram, causal, far_mask, ident, peaks_dram, T, NH, DH, RECENT):
    phase = "cmax"
    NT = T // P
    order = list(range(NT - 1, -1, -1))
    with ExitStack() as ctx:
        m = Memory(nc, ctx, phase)
        qk = m.sb("qk", [3 * DH, 2, 2, T], F32R)
        hb = m.sb("hb", [P, 2, T])
        cmf = m.sb("cmf", [P, 2, P])
        cm = m.sb("cm", [P, 2, P], F32R)
        idt = m.sb("ident", [P, P])
        nm = m.sb("far", [P, P])
        mixed = m.sb("mixed", [P, 2, P])
        waste = m.sb("waste", [P, T])
        part = m.sb("part", [P, 2, 3])
        peak = m.sb("peak", [P, NH * NT])
        high = m.sb("high", [P, NH * NT], F32R)
        low = m.sb("low", [P, NH * NT], F32R)
        rows = m.sb("rows", [P, 2, NH * NT // P, P], F32R)
        sc = m.ps("sc", [P, 2, T])
        consts_in = m.sem("consts_in")
        init = m.sem("init")
        head_in = [m.sem("head_in0"), m.sem("head_in1")]
        scored = m.sem("scored")
        mixed_done = m.sem("mixed_done")
        mixed_sum = m.sem("mixed_sum")
        parts_done = m.sem("parts_done")
        peaked = m.sem("peaked")
        halved = m.sem("halved")
        turned = m.sem("turned")
        copied = m.sem("copied")
        stored = m.sem("stored")
        block = ctx.enter_context(nc.Block())

        @block.sync
        def _(sp):
            for j in range(2):
                sp.dma_start(cmf[:, j, :], causal[j]).then_inc(consts_in, 16)
            sp.dma_start(nm[:, :], far_mask).then_inc(consts_in, 16)
            sp.dma_start(idt[:, :], ident).then_inc(consts_in, 16)

            def load(h, u):
                load_stacks(sp, qk[:, u], qk_dram, h, DH, head_in[u])
                sp.dma_start(hb[:, u, :], bias_dram[bass.ds(h, 1), :].to_broadcast([P, T])).then_inc(head_in[u], 16)
            load(0, 0)
            load(1, 1)

            def turn(i):
                for u in range(2):
                    sp.wait_ge(peaked, (i * 2 + u + 1) * NT)
                    load(i * 2 + u + 2, u)
            run_turns(sp, NH // 2 - 1, turn)
            sp.wait_ge(copied, 1)
            for j in range(2):
                sp.dma_start(peaks_dram[j].rearrange("(a p) n -> p a n", p=P), rows[:, j].bitcast(F32)).then_inc(stored, 16)
            sp.wait_ge(stored, 32)

        @block.tensor
        def _(pe):
            pe.wait_ge(init, 2)
            pe.wait_ge(consts_in, 64)

            def turn(i):
                for u in range(2):
                    h = i * 2 + u
                    pe.wait_ge(head_in[u], (i + 1) * 112)
                    for n, q in enumerate(order):
                        pe.wait_ge(parts_done, h * NT + max(n - 1, 0))
                        for c, w in chunks_of(q):
                            pe.matmul(sc[:, n % 2, c:c + w], qk[:, u, 0, q * P:(q + 1) * P], qk[:, u, 1, c:c + w],
                                      start=True, stop=(c + w < (q + 1) * P))
                        mm = pe.matmul(sc[:, n % 2, q * P:(q + 1) * P], cm[:, 0, :], cm[:, 1, :], start=False, stop=True)
                        mm.then_inc(scored, 1)
            run_turns(pe, NH // 2, turn)
            pe.wait_ge(halved, 2)
            pe.wait_ge(parts_done, NH * NT)
            for j, half in enumerate((high, low)):
                for a in range(NH * NT // P):
                    t = pe.transpose(sc[:, 0, (2 * j + a) * P:(2 * j + a + 1) * P], half[:, a * P:(a + 1) * P].bitcast(F32), idt[:, :])
            t.then_inc(turned, 1)

        @block.scalar
        def _(act):
            act.wait_ge(turned, 1)
            act.activation(rows[:, :, :, :].rearrange("p j a n -> p (j a n)"), sc[:, 0, 0:4 * P], ACT.Copy).then_inc(copied, 1)

        @block.vector
        def _(dve):
            dve.wait_ge(consts_in, 64)
            for j in range(2):
                dve.tensor_copy(cm[:, j, :], cmf[:, j, :]).then_inc(init, 1)

            def turn(i):
                for u in range(2):
                    h = i * 2 + u
                    dve.wait_ge(head_in[u], (i + 1) * 112)
                    for n, q in enumerate(order):
                        g = h * NT + n
                        end = (q + 1) * P
                        far, mid = max(q * P - RECENT, 0), max(end - RECENT, 0)
                        lo = far - (q * P - RECENT)
                        dve.wait_ge(scored, g + 1)
                        dve.wait_ge(peaked, h * NT + max(n - 1, 0))
                        if mid:
                            dve.tensor_tensor(mixed[:, n % 2, lo:P], hb[:, u, far:mid], nm[:, lo:P], ALU.mult).then_inc(mixed_done, 1)
                        else:
                            dve.tensor_copy(mixed[:, n % 2, 0:1], nm[:, 0:1]).then_inc(mixed_done, 1)
                        parts = 1
                        dve.tensor_reduce(part[:, n % 2, 0:1], sc[:, n % 2, mid:end], AX.X, ALU.max)
                        if far:
                            dve.tensor_tensor_reduce(waste[:, 0:far], sc[:, n % 2, 0:far], hb[:, u, 0:far], 1.0, -3.0e38,
                                                     ALU.add, ALU.max, part[:, n % 2, parts:parts + 1])
                            parts += 1
                        dve.wait_ge(mixed_done, g + 1)
                        if mid:
                            dve.tensor_tensor(mixed[:, n % 2, lo:P], sc[:, n % 2, far:mid], mixed[:, n % 2, lo:P], ALU.add).then_inc(mixed_sum, 1)
                        else:
                            dve.tensor_copy(mixed[:, n % 2, 0:1], nm[:, 0:1]).then_inc(mixed_sum, 1)
                        dve.wait_ge(mixed_sum, g + 1)
                        if mid:
                            dve.tensor_reduce(part[:, n % 2, parts:parts + 1], mixed[:, n % 2, lo:P], AX.X, ALU.max).then_inc(parts_done, 1)
                            parts += 1
                        else:
                            dve.tensor_copy(part[:, n % 2, 1:2], nm[:, 0:1]).then_inc(parts_done, 1)
                        dve.wait_ge(parts_done, g + 1)
                        dve.tensor_reduce(peak[:, bass.ds(h * NT + q, 1)], part[:, n % 2, 0:parts], AX.X, ALU.max, negate=True).then_inc(peaked, 1)
            run_turns(dve, NH // 2, turn)
            dve.wait_ge(peaked, NH * NT)
            dve.tensor_copy(high[:, :], peak[:, :]).then_inc(halved, 1)
            dve.wait_ge(halved, 1)
            dve.tensor_tensor(low[:, :], peak[:, :], high[:, :].bitcast(F32), ALU.subtract).then_inc(halved, 1)


def attend_phase(nc, qk_dram, v_dram, biasT_dram, peaks_dram, masks, attnT, T, NH, DH, RECENT):
    phase = "attend"
    NT = T // P
    G = TOK // P
    SCALE = float(DH) ** -0.5
    NEAR = -(-(RECENT + 1 - P) // P) + 1
    RINGS = 4
    with ExitStack() as ctx:
        m = Memory(nc, ctx, phase)
        K = 3 * DH + 2
        qk = m.sb("qk", [K, 2, 2, T], F32R)
        v = m.sb("v", [P, 2, NT, 2 * DH])
        hcol = m.sb("hcol", [P, 2, NT])
        cmf = m.sb("cmf", [P, 2, P])
        cm = m.sb("cm", [P, 2, P], F32R)
        fm = m.sb("far", [P, NEAR, P])
        e = m.sb("e", [P, RINGS, TOK])
        inv = m.sb("inv", [DH, 2, TOK])
        orow = m.sb("orow", [DH, 2, T])
        sc = m.ps("sc", [P, RINGS, TOK])
        ot = m.ps("ot", [2 * DH, 2, TOK])
        consts_in = m.sem("consts_in")
        init = m.sem("init")
        head_in = [m.sem("head_in0"), m.sem("head_in1")]
        scored = m.sem("scored")
        biased = m.sem("biased")
        expd = m.sem("expd")
        summed = m.sem("summed")
        inverted = m.sem("inverted")
        scaled = m.sem("scaled")
        out_stored = [m.sem("out_stored0"), m.sem("out_stored1")]
        block = ctx.enter_context(nc.Block())
        units = []
        for g in range(NT // G):
            for kt in range(G * g + G):
                lo = max(kt - G * g, 0) * P
                near = min(max((kt + NEAR + 1 - G * g) * P, lo), TOK)
                mixes = [(j, G * g + j - kt) for j in range(G) if 1 <= G * g + j - kt <= NEAR]
                units.append((g, kt, lo, near, mixes))
        U = len(units)
        NB = sum(len(x[4]) > 0 for x in units)
        NG = NT // G
        last_of = {g: max(x for x, y in enumerate(units) if y[0] == g) for g in range(NG)}

        @block.sync
        def _(sp):
            for j in range(2):
                sp.dma_start(cmf[:, j, :], masks[j]).then_inc(consts_in, 16)
            for j in range(NEAR):
                sp.dma_start(fm[:, j, :], masks[2 + j]).then_inc(consts_in, 16)
            sp.wait_ge(init, 6)

            def load(h, u):
                load_stacks(sp, qk[:, u], qk_dram, h, DH, head_in[u])
                for j in range(2):
                    sp.dma_start(qk[3 * DH + j:3 * DH + j + 1, u, 0, :].bitcast(F32), peaks_dram[j, bass.ds(h * NT, NT), :].rearrange("(o a) n -> o (a n)", o=1)).then_inc(head_in[u], 16)
                sp.dma_start(v[:, u, :, 0:DH], v_dram[:, bass.ds(h * DH, DH)].rearrange("(n p) d -> p n d", p=P)).then_inc(head_in[u], 16)

                sp.dma_start(hcol[:, u, :], biasT_dram[bass.ds(h, 1)].rearrange("o p n -> p (o n)")).then_inc(head_in[u], 16)

            def store(h, u):
                sp.wait_ge(scaled, (h + 1) * NG)
                sp.dma_start(attnT[bass.ds(h * DH, DH), :], orow[:, u, :]).then_inc(out_stored[u], 16)
            load(0, 0)
            load(1, 1)

            def turn(i):
                for u in range(2):
                    store(i * 2 + u, u)
                    load(i * 2 + u + 2, u)
            run_turns(sp, NH // 2 - 1, turn)
            for u in range(2):
                store(NH - 2 + u, u)
                sp.wait_ge(out_stored[u], 16 * (NH // 2))

        @block.tensor
        def _(pe):
            pe.wait_ge(init, 6)

            def turn(i):
                for u in range(2):
                    h = i * 2 + u
                    pe.wait_ge(head_in[u], (i + 1) * 160)

                    def scores(x):
                        g, kt, lo, near, mixes = units[x]
                        pe.wait_ge(expd, h * U + max(x - RINGS + 1, 0))
                        diagonal = kt >= G * g
                        mm = pe.matmul(sc[:, x % RINGS, lo:TOK], qk[:, u, 1, kt * P:(kt + 1) * P],
                                       qk[:, u, 0, g * TOK + lo:(g + 1) * TOK], start=True, stop=not diagonal)
                        if diagonal:
                            mm = pe.matmul(sc[:, x % RINGS, lo:lo + P], cm[:, 0, :], cm[:, 1, :], start=False, stop=True)
                        mm.then_inc(scored, 1)

                    def values(x):
                        g, kt, lo, near, mixes = units[x]
                        pe.wait_ge(expd, h * U + x + 1)
                        if kt == 0:
                            pe.wait_ge(scaled, h * NG + max(g - 1, 0))
                        pe.matmul(ot[:, g % 2, lo:TOK], v[:, u, kt, :], e[:, x % RINGS, lo:TOK],
                                  start=(kt == 0), stop=(x == last_of[g])).then_inc(summed, 1)
                    for x in range(U + 2):
                        if x < U:
                            scores(x)
                        if x >= 2:
                            values(x - 2)
            run_turns(pe, NH // 2, turn)

        @block.scalar
        def _(act):
            act.wait_ge(consts_in, 32 + 16 * NEAR)

            def turn(i):
                for u in range(2):
                    h = i * 2 + u
                    fixed = 0
                    act.wait_ge(head_in[u], (i + 1) * 160)
                    for x, (g, kt, lo, near, mixes) in enumerate(units):
                        fixed += len(mixes) > 0
                        act.wait_ge(scored, h * U + x + 1)
                        if mixes:
                            act.wait_ge(biased, h * NB + fixed)
                        act.wait_ge(summed, h * U + max(x - RINGS + 1, 0))
                        if near > lo:
                            op = act.activation(e[:, x % RINGS, lo:near], sc[:, x % RINGS, lo:near], ACT.Exp, scale=SCALE)
                        if near < TOK:
                            op = act.activation(e[:, x % RINGS, near:TOK], sc[:, x % RINGS, near:TOK], ACT.Exp,
                                                bias=hcol[:, u, kt:kt + 1], scale=SCALE)
                        op.then_inc(expd, 1)
            run_turns(act, NH // 2, turn)

        @block.vector
        def _(dve):
            for u in range(2):
                dve.memset(qk[3 * DH:K, u, 1, :].bitcast(F32), 1.0).then_inc(init, 1)
                dve.memset(v[:, u, :, DH:2 * DH], 1.0).then_inc(init, 1)
            dve.wait_ge(consts_in, 32 + 16 * NEAR)
            for j in range(2):
                dve.tensor_copy(cm[:, j, :], cmf[:, j, :]).then_inc(init, 1)

            def turn(i):
                for u in range(2):
                    h = i * 2 + u

                    def finish(g):
                        k = h * NG + g
                        dve.wait_ge(summed, h * U + last_of[g] + 1)
                        dve.reciprocal(inv[:, g % 2, :], ot[DH:2 * DH, g % 2, :]).then_inc(inverted, 1)
                        dve.wait_ge(inverted, k + 1)
                        if g == 0:
                            dve.wait_ge(out_stored[u], i * 16)
                        dve.tensor_tensor(orow[:, u, g * TOK:(g + 1) * TOK], ot[0:DH, g % 2, :], inv[:, g % 2, :], ALU.mult).then_inc(scaled, 1)
                    dve.wait_ge(head_in[u], (i + 1) * 160)
                    for x, (g, kt, lo, near, mixes) in enumerate(units):
                        if mixes:
                            dve.wait_ge(scored, h * U + x + 1)
                            for j, d in mixes:
                                s = sc[:, x % RINGS, j * P:(j + 1) * P]
                                op = dve.scalar_tensor_tensor(s, fm[:, d - 1, :], hcol[:, u, kt:kt + 1], s, ALU.mult, ALU.add)
                            op.then_inc(biased, 1)
                        if g and kt == 3:
                            finish(g - 1)
                    finish(NG - 1)
            run_turns(dve, NH // 2, turn)


def project_out_phase(nc, attnT, wo, x, x_out, T):
    phase = "oproj"
    NT = T // P
    with ExitStack() as ctx:
        m = Memory(nc, ctx, phase)
        at = m.sb("at", [P, KT, T])
        w = m.sb("w", [P, KT, D])
        xs = m.sb("xs", [P, NT, D])
        acc = m.ps("acc", [P, 4, D])
        w_in = m.sem("w_in")
        x_in = m.sem("x_in")
        done = m.sem("done")
        added = m.sem("added")
        stored = m.sem("stored")
        block = ctx.enter_context(nc.Block())

        @block.sync
        def _(sp):
            for k in range(KT):
                sp.dma_start(at[:, k, :], attnT[k * P:(k + 1) * P, :]).then_inc(w_in, 16)
                sp.dma_start(w[:, k, :], wo[k * P:(k + 1) * P, :]).then_inc(w_in, 16)
            sp.dma_start(xs[:, :, :], x.rearrange("(n p) d -> p n d", p=P)).then_inc(x_in, 16)
            for g in range(NT // 4):
                sp.wait_ge(added, 4 * (g + 1))
                sp.dma_start(x_out[g * 4 * P:(g + 1) * 4 * P, :].rearrange("(n p) d -> p n d", p=P), xs[:, 4 * g:4 * g + 4, :]).then_inc(stored, 16)
            sp.wait_ge(stored, 16 * (NT // 4))

        @block.tensor
        def _(pe):
            pe.wait_ge(w_in, 32 * KT)
            for n in range(NT):
                if n >= 4:
                    pe.wait_ge(added, n - 3)
                for k in range(KT):
                    mm = pe.matmul(acc[:, n % 4, :], at[:, k, n * P:(n + 1) * P], w[:, k, :], start=(k == 0), stop=(k == KT - 1))
                mm.then_inc(done, 1)

        @block.vector
        def _(dve):
            dve.wait_ge(x_in, 16)
            for n in range(NT):
                dve.wait_ge(done, n + 1)
                dve.tensor_tensor(xs[:, n, :], xs[:, n, :], acc[:, n % 4, :], ALU.add).then_inc(added, 1)


HEADS_B = 16
DH = D // HEADS_B
RATIO = 0.1
THETA = 10000.0


def constants(T):
    inv = (1.0 / THETA ** (np.arange(0, DH, 2, dtype=np.float32) / np.float32(DH))).astype(np.float32)
    freqs = np.arange(T, dtype=np.float32)[:, None] * inv[None, :]
    emb = np.concatenate([freqs, freqs], axis=-1)
    sign = np.where(np.arange(DH) < DH // 2, -1.0, 1.0).astype(np.float32)
    cos = np.tile(np.cos(emb).astype(np.float32).T, (P // DH, 1))
    sin = np.tile((np.sin(emb).astype(np.float32) * sign).T, (P // DH, 1))
    had = np.ones((1, 1), np.float32)
    while had.shape[0] < P:
        had = np.block([[had, had], [had, -had]])
    r, c = np.arange(P)[:, None], np.arange(P)[None, :]
    recent = int(RATIO * T)
    return {
        "c_ident": np.eye(P, dtype=np.float32),
        "c_hmask": (r % GH == np.arange(GH)[None, :]).astype(np.float32),
        "c_cos": np.ascontiguousarray(cos), "c_sin": np.ascontiguousarray(sin),
        "c_had": np.ascontiguousarray(had.astype(np.float32)),
        "c_causal": np.where(c <= r, 0.0, NEG).astype(np.float32),
        "c_causalT": np.where(r <= c, 0.0, NEG).astype(np.float32),
        "c_far": (r > c).astype(np.float32),
        "c_farT": np.stack([(d * P + c - r > recent) for d in (1, 2)]).astype(np.float32),
    }


def program(nc, a, out):
    T = a["x"].shape[0]
    F = a["w1"].shape[1]
    scratch = lambda name, shape: nc.dram_tensor(name, shape, F32, kind="Internal").ap()
    xnT = [scratch(f"xnT{i}", (KT, P, T)) for i in range(4)]
    xs = [scratch(f"x{i}", (T, D)) for i in range(3)]
    streams = [scratch(f"stream_{n}", (H, P, T)) for n in ("beta_k", "q", "k", "beta_v", "a")]
    beta = scratch("beta", (H, T))
    blocks = scratch("blocks", (H, P, T // C))
    decays = scratch("decays", (T // C, H * P))
    o = scratch("o", (H, P, T))
    qk = scratch("qk", (2, 2, D, T))
    peaks = scratch("peaks", (2, HEADS_B * T // P, P))
    biasT = scratch("biasT", (HEADS_B, P, T // P))
    v = scratch("v", (T, D))
    sums = scratch("sums", (HEADS_B, T))
    bias = scratch("bias", (HEADS_B, T))
    attnT = scratch("attnT", (D, T))
    layernorm_phase(nc, "ln0", a["x"], xnT[0], a["c_ident"], T)
    project_phase(nc, xnT[0], [a["wk"], a["wv"], a["wq"], a["wa"]], a["wb"],
                  [a["kc_w"], a["vc_w"], a["qc_w"]], [a["kc_b"], a["vc_b"], a["qc_b"]],
                  a["ba"], a["bb"], streams, beta, blocks, T, H, float(P) ** -0.5, C)
    block_decay_phase(nc, blocks, decays, a["c_ident"], T, H, C)
    scan_phase(nc, streams, decays, o, a["c_ident"], a["c_hmask"], T)
    mix_phase(nc, xnT[0], a["wg"], o, a["wo"], a["ln_g"], a["ln_b"], a["x"], xs[0], T, H)
    layernorm_phase(nc, "ln1", xs[0], xnT[1], a["c_ident"], T)
    ffn_phase(nc, "ffn0", xnT[1], a["w1"], a["w3"], a["w2"], a["c_had"], xs[0], xs[1], T, F)
    layernorm_phase(nc, "ln2", xs[1], xnT[2], a["c_ident"], T)
    rope_phase(nc, xnT[2], [a["bq"], a["bq_swap"], a["bk"], a["bk_swap"]], a["bv"], a["c_cos"], a["c_sin"], qk, v, T)
    recent = int(RATIO * T)
    causal = (a["c_ident"], a["c_causal"])
    column_sum_phase(nc, qk, causal, sums, T, HEADS_B, DH)
    heavy_phase(nc, sums, bias, biasT, a["c_ident"], T, HEADS_B, int(RATIO * T))
    chosen_max_phase(nc, qk, bias, causal, a["c_far"], a["c_ident"], peaks, T, HEADS_B, DH, recent)
    attend_phase(nc, qk, v, biasT, peaks, (a["c_ident"], a["c_causalT"], a["c_farT"][0], a["c_farT"][1]), attnT,
                 T, HEADS_B, DH, recent)
    project_out_phase(nc, attnT, a["bo"], xs[1], xs[2], T)
    layernorm_phase(nc, "ln3", xs[2], xnT[3], a["c_ident"], T)
    ffn_phase(nc, "ffn1", xnT[3], a["w1"], a["w3"], a["w2"], a["c_had"], xs[2], out, T, F)


def laid_out(i):
    g = lambda n: np.asarray(i[n])
    t = lambda n: np.ascontiguousarray(g(n).T)
    A, B, FN = "L0_attn_a_", "L0_attn_b_", "L0_ffn_"
    swap = np.arange(D).reshape(HEADS_B, 2, DH // 2)[:, ::-1].reshape(-1)
    per_head = lambda n: np.ascontiguousarray(g(n).reshape(H, P).T)
    taps = lambda n: np.ascontiguousarray(g(n).reshape(H, P, -1).transpose(1, 0, 2))
    return {
        "x": np.ascontiguousarray(g(A + "x")[0]),
        "wq": t(A + "Wq"), "wk": t(A + "Wk"), "wv": t(A + "Wv"), "wa": t(A + "Wa"), "wb": t(A + "Wb"),
        "wg": t(A + "Wg"), "wo": t(A + "Wo"), "ba": np.ascontiguousarray(g(A + "ba").reshape(H, P)),
        "bb": np.ascontiguousarray(g(A + "bb").reshape(H, 1)),
        "qc_w": taps(A + "qc_w"), "kc_w": taps(A + "kc_w"), "vc_w": taps(A + "vc_w"),
        "qc_b": per_head(A + "qc_b"), "kc_b": per_head(A + "kc_b"), "vc_b": per_head(A + "vc_b"),
        "ln_g": np.ascontiguousarray(g(A + "ln_g").reshape(P, 1)),
        "ln_b": np.ascontiguousarray(g(A + "ln_b").reshape(P, 1)),
        "bq": t(B + "Wq"), "bk": t(B + "Wk"), "bv": t(B + "Wv"), "bo": t(B + "Wo"),
        "bq_swap": np.ascontiguousarray(g(B + "Wq")[swap].T),
        "bk_swap": np.ascontiguousarray(g(B + "Wk")[swap].T),
        "w1": t(FN + "W1"), "w3": t(FN + "W3"), "w2": t(FN + "W2"),
    }


def kernel(**inputs):
    import concourse.bacc as bacc
    from concourse.bass_utils import run_bass_kernel_spmd

    arrays = laid_out(inputs)
    T = arrays["x"].shape[0]
    arrays.update(constants(T))
    nc = bacc.Bacc("TRN2", target_bir_lowering=False, num_devices=1)
    a = {n: nc.dram_tensor(f"in_{n}", v.shape, mybir.dt.from_np(v.dtype), kind="ExternalInput").ap()
         for n, v in arrays.items()}
    out = nc.dram_tensor("out", (T, D), F32, kind="ExternalOutput").ap()
    program(nc, a, out)
    r = run_bass_kernel_spmd(nc, [{f"in_{n}": v for n, v in arrays.items()}], core_ids=[0])
    return r.results[0]["out"].reshape(1, T, D)
```

```python
import numpy as np
import concourse.bass as bass
from concourse import mybir
from contextlib import ExitStack

F32 = mybir.dt.float32
F32R = mybir.dt.float32r
ALU = mybir.AluOpType
ACT = mybir.ActivationFunctionType
AX = mybir.AxisListType
P = 128
D = 512
KT = D // P
TOK = 512
EPS = 1e-5


class Memory:

    def __init__(self, nc, ctx, phase):
        self.nc, self.ctx, self.phase = nc, ctx, phase
        self.sems = []
        ctx.callback(self.release)

    def sb(self, name, shape, dtype=F32):
        return self.ctx.enter_context(self.nc.sbuf_tensor(f"{self.phase}_{name}", shape, dtype))

    def ps(self, name, shape):
        return self.ctx.enter_context(self.nc.psum_tensor(f"{self.phase}_{name}", shape, F32))

    def sem(self, name):
        self.sems.append(self.nc.alloc_semaphore(f"{self.phase}_{name}"))
        return self.sems[-1]

    def release(self):
        self.nc.clear_and_free_semaphores(self.sems)
        self.nc.all_engine_barrier()


def run_turns(eng, n, turn):
    turn(0)
    with eng.Fori(1, n) as i:
        turn(i)


def run_all(eng, n, turn):
    run_turns(eng, n - 1, lambda i: turn(i, True))
    turn(n - 1, False)


def layernorm_phase(nc, phase, x, xnT, ident, T, split=True):
    NT = T // P
    HALVES = 2 if split else 1
    with ExitStack() as ctx:
        m = Memory(nc, ctx, phase)
        xs = m.sb("xs", [P, NT, D])
        xn = m.sb("xn", [P, 2, D])
        xt = m.sb("xt", [P, HALVES, 4, KT, P], F32R if split else F32)
        idt = m.sb("ident", [P, P])
        stats = m.sb("stats", [P, NT, nc.vector.BN_STATS_DIM])
        mv = m.sb("mv", [P, NT, nc.vector.BN_AGGR_DIM])
        sd = m.sb("sd", [P, NT])
        rstd = m.sb("rstd", [P, NT])
        tr = m.ps("tr", [P, 2, KT, P])
        x_in = m.sem("x_in")
        ident_in = m.sem("ident_in")
        stat = m.sem("stat")
        var_ready = m.sem("var_ready")
        sd_ready = m.sem("sd_ready")
        rstd_ready = m.sem("rstd_ready")
        normed = m.sem("normed")
        turned = m.sem("turned")
        copied = m.sem("copied")
        low_done = m.sem("low_done")
        stored = m.sem("stored")
        block = ctx.enter_context(nc.Block())

        @block.sync
        def _(sp):
            sp.dma_start(idt[:, :], ident).then_inc(ident_in, 16)
            sp.dma_start(xs[:, :, :], x.rearrange("(n p) d -> p n d", p=P)).then_inc(x_in, 16)
            for g in range(NT // 4):
                sp.wait_ge(low_done if split else copied, 4 * (g + 1))
                for j in range(HALVES):
                    for k in range(KT):
                        sp.dma_start(xnT[j, k, :, g * 4 * P:(g + 1) * 4 * P].rearrange("p (n t) -> p n t", n=4),
                                     xt[:, j, :, k, :].bitcast(F32)).then_inc(stored, 16)
            sp.wait_ge(stored, 16 * HALVES * KT * (NT // 4))

        @block.vector
        def _(dve):
            dve.wait_ge(x_in, 16)
            for n in range(NT):
                dve.bn_stats(stats[:, n, :], xs[:, n, :]).then_inc(stat, 1)
            for n in range(NT):
                dve.wait_ge(stat, n + 1)
                last = dve.bn_aggr(mv[:, n, :], stats[:, n, :])
            last.then_inc(stat, 1)
            dve.wait_ge(stat, NT + 1)
            dve.tensor_scalar(sd[:, :], mv[:, :, 1], EPS, None, ALU.add).then_inc(var_ready, 1)
            dve.wait_ge(sd_ready, 1)
            dve.reciprocal(rstd[:, :], sd[:, :]).then_inc(rstd_ready, 1)
            dve.wait_ge(rstd_ready, 1)
            for n in range(NT + 1):
                if n < NT:
                    if n >= 2:
                        dve.wait_ge(turned, n - 1)
                    dve.tensor_scalar(xn[:, n % 2, :], xs[:, n, :], mv[:, n, 0:1], rstd[:, n:n + 1],
                                      ALU.subtract, ALU.mult).then_inc(normed, 1)
                if n and split:
                    dve.wait_ge(copied, n)
                    if n > 4:
                        dve.wait_ge(stored, 16 * HALVES * KT * ((n - 1) // 4))
                    dve.tensor_tensor(xt[:, 1, (n - 1) % 4], tr[:, (n - 1) % 2], xt[:, 0, (n - 1) % 4].bitcast(F32),
                                      ALU.subtract).then_inc(low_done, 1)

        @block.scalar
        def _(act):
            act.wait_ge(var_ready, 1)
            act.activation(sd[:, :], sd[:, :], ACT.Sqrt).then_inc(sd_ready, 1)
            for n in range(NT):
                act.wait_ge(turned, n + 1)
                if n >= 4:
                    act.wait_ge(stored, 16 * HALVES * KT * (n // 4))
                act.activation(xt[:, 0, n % 4], tr[:, n % 2], ACT.Copy).then_inc(copied, 1)

        @block.tensor
        def _(pe):
            pe.wait_ge(ident_in, 16)
            for n in range(NT):
                pe.wait_ge(normed, n + 1)
                if n >= 2:
                    pe.wait_ge(low_done if split else copied, n - 1)
                for k in range(KT):
                    t = pe.transpose(tr[:, n % 2, k, :], xn[:, n % 2, k * P:(k + 1) * P], idt[:, :])
                t.then_inc(turned, 1)


def project_phase(nc, xnT, w_kvqa, w_beta, conv_w, conv_b, a_bias, beta_bias, streams, beta_dram, blocks_dram, T, H, scale, STEPS):
    phase = "proj"
    TT = T // TOK
    TAPS = 4
    KB, QQ, KK, VB, AA = range(5)
    with ExitStack() as ctx:
        m = Memory(nc, ctx, phase)
        xn = m.sb("xn", [P, 2, KT, T], F32R)
        whole = m.sb("whole", [P, 4, KT, P])
        w = m.sb("w", [P, 2, 2, 4, KT, P], F32R)
        wb_whole = m.sb("wb_whole", [P, KT, H])
        wb = m.sb("wb", [P, 2, KT, H], F32R)
        cw = m.sb("cw", [P, 3, H, TAPS])
        cb = m.sb("cb", [P, 3, H])
        ab = m.sb("ab", [P, 2])
        bb = m.sb("bb", [H, 1])
        beta_rows = m.sb("beta_rows", [P, T])
        raw = m.sb("raw", [P, 2, TAPS - 1 + T])
        y = m.sb("y", [P, 2, T])
        gate = m.sb("gate", [P, T])
        beta = gate[0:H]
        res = m.sb("res", [P, 2, T])
        resb = m.sb("resb", [P, 2, T])
        decay = m.sb("decay", [P, T])
        folds = STEPS.bit_length() - 1
        fold = m.sb("fold", [P, T // STEPS, STEPS])
        product = m.sb("product", [P, 2, T // STEPS])
        acc = m.ps("acc", [P, 8, TOK])
        params_in = m.sem("params_in")
        w_in = m.sem("w_in")
        w_high = m.sem("w_high")
        w_low = m.sem("w_low")
        wb_high = m.sem("wb_high")
        wb_low = m.sem("wb_low")
        beta_in = m.sem("beta_in")
        zeroed = m.sem("zeroed")
        beta_mm = m.sem("beta_mm")
        beta_done = m.sem("beta_done")
        beta_stored = m.sem("beta_stored")
        unit_done = m.sem("unit_done")
        evacuated = m.sem("evacuated")
        conv_step = m.sem("conv_step")
        gated = m.sem("gated")
        res_done = m.sem("res_done")
        resb_done = m.sem("resb_done")
        res_stored = [m.sem("res_stored0"), m.sem("res_stored1")]
        resb_stored = [m.sem("resb_stored0"), m.sem("resb_stored1")]
        decay_stored = m.sem("decay_stored")
        folded = m.sem("folded")
        fold_stored = [m.sem("fold_stored0"), m.sem("fold_stored1")]
        block = ctx.enter_context(nc.Block())
        OUT = [KK, None, QQ]
        OUTB = [KB, VB, None]
        PASSES = ((0, 0), (0, 1), (1, 0))

        def evac0(j, t, TT):
            return max(j * TT + t - 7, 0)

        def res_count(i, s):
            before = sum(1 for r in range(s) if r % 2 == s % 2 and r % 3 != 1)
            return (i * 2 + before) * 16

        @block.sync
        def _(sp):
            for j in range(2):
                for k in range(KT):
                    sp.dma_start(xn[:, j, k, :].bitcast(F32), xnT[j, k]).then_inc(params_in, 16)
            sp.dma_start(wb_whole[:, :, :], w_beta.rearrange("(k p) h -> p k h", p=P)).then_inc(params_in, 16)
            for j in range(3):
                sp.dma_start(cw[:, j], conv_w[j]).then_inc(params_in, 16)
            sp.dma_start(bb[:, :], beta_bias).then_inc(params_in, 16)
            for j in range(3):
                sp.dma_start(cb[:, j], conv_b[j]).then_inc(params_in, 16)

            def load(h, u):
                for j in range(4):
                    sp.dma_start(whole[:, j], w_kvqa[j][:, bass.ds(h * P, P)].rearrange("(k p) c -> p k c", p=P)).then_inc(w_in, 16)
                sp.dma_start(ab[:, u:u + 1], a_bias[bass.ds(h, 1), :].rearrange("o p -> p o")).then_inc(w_in, 16)

            def load_beta(h):
                sp.dma_start(beta_rows[:, :], beta_dram[bass.ds(h, 1), :].to_broadcast([P, T])).then_inc(beta_in, 16)
            load(0, 0)
            sp.wait_ge(beta_done, TT)
            sp.dma_start(beta_dram, beta[:, :]).then_inc(beta_stored, 16)
            sp.wait_ge(w_low, 1)
            load(1, 1)
            sp.wait_ge(beta_stored, 16)
            load_beta(0)

            def stores(i, u, follow):
                h = i * 2 + u
                for j in range(3):
                    s = 3 * u + j
                    if OUT[j] is not None:
                        sp.wait_ge(res_done, i * 6 + s + 1)
                        sp.dma_start(streams[OUT[j]][bass.ds(h, 1)].rearrange("o p t -> p (o t)"), res[:, s % 2]).then_inc(res_stored[s % 2], 16)
                    if OUTB[j] is not None:
                        sp.wait_ge(resb_done, h * 2 + j + 1)
                        sp.dma_start(streams[OUTB[j]][bass.ds(h, 1)].rearrange("o p t -> p (o t)"), resb[:, s % 2]).then_inc(resb_stored[s % 2], 16)
                sp.wait_ge(evacuated, (h + 1) * 4 * TT)
                sp.dma_start(streams[AA][bass.ds(h, 1)].rearrange("o p t -> p (o t)"), decay[:, :]).then_inc(decay_stored, 16)
                sp.wait_ge(folded, (h + 1) * folds)
                sp.dma_start(blocks_dram[bass.ds(h, 1)].rearrange("o p n -> p (o n)"), product[:, u, :]).then_inc(fold_stored[u], 16)
                if follow >= 1:
                    sp.wait_ge(resb_done, (h + 1) * 2)
                    load_beta(h + 1)
                if follow >= 2:
                    sp.wait_ge(w_low, h + 2)
                    load(h + 2, u)
            def turn(i):
                for u in range(2):
                    stores(i, u, 2)
            run_turns(sp, H // 2 - 1, turn)
            for u in range(2):
                stores(H // 2 - 1, u, 1 - u)
            sp.wait_ge(decay_stored, 16 * H)
            for u in range(2):
                sp.wait_ge(fold_stored[u], 16 * (H // 2))
                sp.wait_ge(res_stored[u], 16 * (H // 2) * 2)
                sp.wait_ge(resb_stored[u], 16 * (H // 2) * 2)

        @block.tensor
        def _(pe):
            pe.wait_ge(params_in, 16 * (2 * KT + 1 + 3 + 3 + 1))
            pe.wait_ge(wb_low, 1)
            for t in range(TT):
                for p, (wh, xh) in enumerate(PASSES):
                    for k in range(KT):
                        mm = pe.matmul(acc[0:H, 4 + t % 4, :], wb[:, wh, k, :], xn[:, xh, k, t * TOK:(t + 1) * TOK],
                                       start=(p == 0 and k == 0), stop=(p == 2 and k == KT - 1))
                mm.then_inc(beta_mm, 1)
            pe.wait_ge(beta_done, TT)
            def turn(i):
                for u in range(2):
                    pe.wait_ge(w_low, i * 2 + u + 1)
                    for j in range(4):
                        for t in range(TT):
                            n = (i * 2 + u) * 4 * TT + j * TT + t
                            if u == 0 and j < 2:
                                pe.wait_ge(evacuated, i * (8 * TT) + evac0(j, t, TT))
                            else:
                                pe.wait_ge(evacuated, n - 7)
                            for p, (wh, xh) in enumerate(PASSES):
                                for k in range(KT):
                                    mm = pe.matmul(acc[:, (j * TT + t) % 8, :], w[:, u, wh, j, k, :], xn[:, xh, k, t * TOK:(t + 1) * TOK],
                                                   start=(p == 0 and k == 0), stop=(p == 2 and k == KT - 1))
                            mm.then_inc(unit_done, 1)
            run_turns(pe, H // 2, turn)

        @block.scalar
        def _(act):
            act.wait_ge(params_in, 16 * (2 * KT + 1 + 3 + 3 + 1))
            act.activation(wb[:, 0], wb_whole[:, :, :], ACT.Copy).then_inc(wb_high, 1)

            def split(h, u):
                act.wait_ge(w_in, (h + 1) * 80)
                act.activation(w[:, u, 0], whole[:, :, :, :], ACT.Copy).then_inc(w_high, 1)
            split(0, 0)
            for t in range(TT):
                act.wait_ge(beta_mm, t + 1)
                act.activation(beta[:, t * TOK:(t + 1) * TOK], acc[0:H, 4 + t % 4, :], ACT.Sigmoid, bias=bb[:, 0:1]).then_inc(beta_done, 1)
            act.wait_ge(zeroed, 2)
            act.wait_ge(beta_stored, 16)

            def gate_unit(i, s):
                act.wait_ge(conv_step, (i * 6 + s + 1) * TAPS)
                act.wait_ge(res_done, i * 6 + s)
                act.activation(gate[:, :], y[:, s % 2, :], ACT.Sigmoid).then_inc(gated, 1)
            def turn(i, more):
                for u in range(2):
                    h = i * 2 + u
                    for j in range(4):
                        s = 3 * u + j
                        if j < 3:
                            if s >= 2:
                                act.wait_ge(conv_step, (i * 6 + s - 1) * TAPS)
                            else:
                                act.wait_ge(conv_step, (i * 6) * TAPS)
                        else:
                            act.wait_ge(decay_stored, h * 16)
                            act.wait_ge(folded, h * folds)
                        for t in range(TT):
                            n = h * 4 * TT + j * TT + t
                            act.wait_ge(unit_done, n + 1)
                            if j < 3:
                                lo = TAPS - 1 + t * TOK
                                act.activation(raw[:, s % 2, lo:lo + TOK], acc[:, (j * TT + t) % 8, :], ACT.Copy).then_inc(evacuated, 1)
                            else:
                                act.activation(decay[:, t * TOK:(t + 1) * TOK], acc[:, (j * TT + t) % 8, :], ACT.Sigmoid,
                                               bias=ab[:, u:u + 1]).then_inc(evacuated, 1)
                        if j < 3 and j > 0:
                            gate_unit(i, s - 1)
                        if j == 1 and (u == 0 or more):
                            act.wait_ge(unit_done, h * 4 * TT)
                            split(h + 1, 1 - u)
                    gate_unit(i, 3 * u + 2)
            run_all(act, H // 2, turn)

        @block.vector
        def _(dve):
            for s in range(2):
                dve.memset(raw[:, s, 0:TAPS - 1], 0.0).then_inc(zeroed, 1)
            dve.wait_ge(params_in, 16 * (2 * KT + 1 + 3 + 3 + 1))
            dve.wait_ge(zeroed, 2)

            def finish(i, s):
                j = s % 3
                dve.wait_ge(gated, i * 6 + s + 1)
                if s >= 2:
                    dve.wait_ge(resb_done, i * 4 + [0, 0, 1, 2, 2, 3][s] )
                else:
                    dve.wait_ge(resb_done, i * 4)
                dve.wait_ge(res_stored[s % 2], res_count(i, s))
                dve.scalar_tensor_tensor(res[:, s % 2, :], y[:, s % 2, :], scale if j == 0 else 1.0, gate[:, :],
                                         ALU.mult, ALU.mult).then_inc(res_done, 1)

            def turn(i):
                for u in range(2):
                    for j in range(3):
                        s = 3 * u + j
                        h = i * 2 + u
                        dve.wait_ge(evacuated, h * 4 * TT + (j + 1) * TT)
                        dve.wait_ge(res_done, i * 6 + max(s - 1, 0))
                        for tap in range(TAPS):
                            src = raw[:, s % 2, tap:tap + T]
                            cwt = cw[:, j, bass.ds(h, 1), tap]
                            if tap == 0:
                                dve.tensor_scalar(y[:, s % 2, :], src, cwt, cb[:, j, bass.ds(h, 1)],
                                                  ALU.mult, ALU.add).then_inc(conv_step, 1)
                            else:
                                dve.wait_ge(conv_step, (i * 6 + s) * TAPS + tap)
                                dve.scalar_tensor_tensor(y[:, s % 2, :], src, cwt, y[:, s % 2, :],
                                                         ALU.mult, ALU.add).then_inc(conv_step, 1)
                        finish(i, s)
            run_turns(dve, H // 2, turn)

        @block.gpsimd
        def _(pool):
            pool.wait_ge(wb_high, 1)
            pool.tensor_tensor(wb[:, 1], wb_whole[:, :, :], wb[:, 0].bitcast(F32), ALU.subtract).then_inc(wb_low, 1)

            def split(h, u):
                pool.wait_ge(w_high, h + 1)
                pool.tensor_tensor(w[:, u, 1], whole[:, :, :, :], w[:, u, 0].bitcast(F32), ALU.subtract).then_inc(w_low, 1)
            split(0, 0)

            def turn(i, more):
                for u in range(2):
                    for j in range(2):
                        s = 3 * u + j
                        if j == 0:
                            pool.wait_ge(beta_in, (i * 2 + u + 1) * 16)
                        pool.wait_ge(res_done, i * 6 + s + 1)
                        before = sum(1 for r in range(s) if r % 2 == s % 2 and r % 3 != 2)
                        pool.wait_ge(resb_stored[s % 2], (i * 2 + before) * 16)
                        pool.tensor_tensor(resb[:, s % 2, :], res[:, s % 2, :], beta_rows[:, :], ALU.mult).then_inc(resb_done, 1)
                        if j == 0 and (u == 0 or more):
                            split(i * 2 + u + 1, 1 - u)
                    h = i * 2 + u
                    pool.wait_ge(evacuated, (h + 1) * 4 * TT)
                    pool.wait_ge(fold_stored[u], i * 16)
                    tokens = decay[:, :].rearrange("p (n s) -> p n s", s=STEPS)
                    src, at = tokens, 0
                    for f in range(folds):
                        n = STEPS >> (f + 1)
                        dst = (STEPS // 2, 0)[f % 2]
                        out = product[:, u, :].unsqueeze(2) if n == 1 else fold[:, :, dst:dst + n]
                        if f:
                            pool.wait_ge(folded, h * folds + f)
                        pool.tensor_tensor(out, src[:, :, at:at + n], src[:, :, at + n:at + 2 * n],
                                           ALU.mult).then_inc(folded, 1)
                        src, at = fold, dst
            run_all(pool, H // 2, turn)


def block_decay_phase(nc, blocks_dram, decays, ident, T, H, STEPS):
    NB = T // STEPS
    with ExitStack() as ctx:
        m = Memory(nc, ctx, "decays")
        cm = m.sb("cm", [P, H, NB])
        rows = m.sb("rows", [NB, H, P])
        idt = m.sb("ident", [P, P])
        tr = m.ps("tr", [NB, H, P])
        loaded = m.sem("loaded")
        turned = m.sem("turned")
        copied = m.sem("copied")
        stored = m.sem("stored")
        block = ctx.enter_context(nc.Block())

        @block.sync
        def _(sp):
            sp.dma_start(idt[:, :], ident).then_inc(loaded, 16)
            sp.dma_start(cm[:, :, :], blocks_dram.rearrange("h p n -> p h n")).then_inc(loaded, 16)
            sp.wait_ge(copied, H // 4)
            sp.dma_start(decays, rows[:, :, :].rearrange("n h p -> n (h p)")).then_inc(stored, 16)
            sp.wait_ge(stored, 16)

        @block.tensor
        def _(pe):
            pe.wait_ge(loaded, 32)
            for g in range(H // 4):
                for h in range(4 * g, 4 * g + 4):
                    t = pe.transpose(tr[:, h, :], cm[:, h, :], idt[:, :])
                t.then_inc(turned, 1)

        @block.vector
        def _(dve):
            for g in range(H // 4):
                dve.wait_ge(turned, g + 1)
                dve.tensor_copy(rows[:, 4 * g:4 * g + 4, :], tr[:, 4 * g:4 * g + 4, :]).then_inc(copied, 1)


def mix_phase(nc, xnT, wg, o_dram, wo, ln_g, ln_b, x, x_out, T, H):
    phase = "mix"
    TT = T // TOK
    SUB = TOK // P
    with ExitStack() as ctx:
        m = Memory(nc, ctx, phase)
        whole = m.sb("whole", [P, 2, H * P])
        wgs = m.sb("wg", [P, 2, KT, H * P], F32R)
        wos = m.sb("wo", [P, H, D])
        xn = m.sb("xn", [P, 2, KT, TOK], F32R)
        o = m.sb("o", [P, 4, TOK])
        oc = m.sb("oc", [P, 4, TOK])
        sq = m.sb("sq", [P, 2, TOK])
        sd = m.sb("sd", [P, 2, TOK])
        rs = m.sb("rs", [P, 2, TOK])
        sg = m.sb("sg", [P, 4, TOK])
        of = m.sb("of", [P, 2, TOK])
        mean_w = m.sb("mean_w", [P, P])
        gb = m.sb("gb", [P, 2])
        eps = m.sb("eps", [P, 1])
        xs = m.sb("xs", [P, 2, SUB, D])
        out_ps = m.ps("out", [P, SUB, D])
        g_ps = m.ps("g", [P, 2, TOK])
        mean_ps = m.ps("mean", [P, TOK])
        var_ps = m.ps("var", [P, TOK])
        w_in = m.sem("w_in")
        wg_in = [m.sem("wg_in0"), m.sem("wg_in1")]
        wg_high = m.sem("wg_high")
        wg_low = m.sem("wg_low")
        init = m.sem("init")
        xn_in = m.sem("xn_in")
        x_in = m.sem("x_in")
        o_in = [m.sem(f"o_in{i}") for i in range(4)]
        g_done = m.sem("g_done")
        mean_done = m.sem("mean_done")
        var_done = m.sem("var_done")
        out_done = m.sem("out_done")
        centred = m.sem("centred")
        squared = m.sem("squared")
        sd_done = m.sem("sd_done")
        sg_done = m.sem("sg_done")
        rs_done = m.sem("rs_done")
        norm_step = m.sem("norm_step")
        of_done = m.sem("of_done")
        added = m.sem("added")
        stored = m.sem("stored")
        block = ctx.enter_context(nc.Block())

        @block.sync
        def _(sp):
            for k in range(KT):
                if k >= 2:
                    sp.wait_ge(wg_low, k - 1)
                sp.dma_start(whole[:, k % 2, :], wg[k * P:(k + 1) * P, :]).then_inc(wg_in[k % 2], 16)
            sp.dma_start(wos[:, :, :], wo.rearrange("(h p) n -> p h n", p=P)).then_inc(w_in, 16)
            sp.dma_start(gb[:, 0:1], ln_g).then_inc(w_in, 16)
            sp.dma_start(gb[:, 1:2], ln_b).then_inc(w_in, 16)
            def turn(i):
                sp.wait_ge(g_done, i * H)
                for j in range(2):
                    sp.dma_start(xn[:, j].bitcast(F32), xnT[j, :, :, bass.ds(i * TOK, TOK)].rearrange("k p t -> p k t")).then_inc(xn_in, 16)
                sp.wait_ge(stored, i * 16)
                sp.dma_start(xs[:, 0, :, :], x[bass.ds(i * TOK, TOK), :].rearrange("(s p) d -> p s d", p=P)).then_inc(x_in, 16)
                for h in range(H):
                    if h >= 4:
                        sp.wait_ge(centred, i * H + h - 3)
                    else:
                        sp.wait_ge(centred, i * H)
                    sp.dma_start(o[:, h % 4, :], o_dram[h, :, bass.ds(i * TOK, TOK)]).then_inc(o_in[h % 4], 16)
                sp.wait_ge(added, (i + 1) * SUB)
                sp.dma_start(x_out[bass.ds(i * TOK, TOK), :].rearrange("(s p) d -> p s d", p=P), xs[:, 1, :, :]).then_inc(stored, 16)
            run_turns(sp, TT, turn)
            sp.wait_ge(stored, 16 * TT)

        @block.tensor
        def _(pe):
            pe.wait_ge(w_in, 16 * 3)
            pe.wait_ge(init, 2)
            pe.wait_ge(wg_low, KT)
            def turn(i):
                pe.wait_ge(xn_in, (i + 1) * 32)
                for n in range(H + 3):
                    if n < H:
                        h = n
                        if h < 2:
                            pe.wait_ge(sg_done, i * H)
                        else:
                            pe.wait_ge(sg_done, i * H + h - 1)
                        for p, (wh, xh) in enumerate(((0, 0), (0, 1), (1, 0))):
                            for k in range(KT):
                                mm = pe.matmul(g_ps[:, h % 2, :], wgs[:, wh, k, h * P:(h + 1) * P], xn[:, xh, k, :],
                                               start=(p == 0 and k == 0), stop=(p == 2 and k == KT - 1))
                        mm.then_inc(g_done, 1)
                        pe.wait_ge(o_in[h % 4], i * 64 + (h // 4 + 1) * 16)
                        pe.wait_ge(centred, i * H + h)
                        pe.matmul(mean_ps[:, :], mean_w[:, :], o[:, h % 4, :], start=True, stop=True).then_inc(mean_done, 1)
                    if 1 <= n <= H:
                        h = n - 1
                        pe.wait_ge(squared, i * H + h + 1)
                        pe.wait_ge(sd_done, i * H + h)
                        pe.matmul(var_ps[:, :], mean_w[:, :], sq[:, h % 2, :], start=True, stop=True).then_inc(var_done, 1)
                    if n >= 3:
                        h = n - 3
                        if h == 0:
                            pe.wait_ge(added, i * SUB)
                        pe.wait_ge(of_done, i * H + h + 1)
                        for s in range(SUB):
                            mm = pe.matmul(out_ps[:, s, :], of[:, h % 2, s * P:(s + 1) * P], wos[:, h, :], start=(h == 0), stop=(h == H - 1))
                        mm.then_inc(out_done, 1)
            run_turns(pe, TT, turn)

        @block.scalar
        def _(act):
            act.wait_ge(init, 2)
            for k in range(KT):
                act.wait_ge(wg_in[k % 2], 16 * (k // 2 + 1))
                act.activation(wgs[:, 0, k, :], whole[:, k % 2, :], ACT.Copy).then_inc(wg_high, 1)
            def turn(i):
                for n in range(H + 1):
                    if n < H:
                        h = n
                        act.wait_ge(g_done, i * H + h + 1)
                        act.wait_ge(of_done, i * H + max(h - 3, 0))
                        act.activation(sg[:, h % 4, :], g_ps[:, h % 2, :], ACT.Sigmoid).then_inc(sg_done, 1)
                    if n >= 1:
                        h = n - 1
                        act.wait_ge(var_done, i * H + h + 1)
                        act.wait_ge(rs_done, i * H + max(h - 1, 0))
                        act.activation(sd[:, h % 2, :], var_ps[:, :], ACT.Sqrt, bias=eps[:, 0:1]).then_inc(sd_done, 1)
            run_turns(act, TT, turn)

        @block.gpsimd
        def _(pool):
            def turn(i):
                for h in range(H):
                    pool.wait_ge(centred, i * H + h + 1)
                    pool.wait_ge(var_done, i * H + max(h - 1, 0))
                    pool.tensor_tensor(sq[:, h % 2, :], oc[:, h % 4, :], oc[:, h % 4, :], ALU.mult).then_inc(squared, 1)
            run_turns(pool, TT, turn)

        @block.vector
        def _(dve):
            dve.memset(mean_w[:, :], 1.0 / P).then_inc(init, 1)
            dve.memset(eps[:, :], EPS).then_inc(init, 1)
            for k in range(KT):
                dve.wait_ge(wg_high, k + 1)
                dve.tensor_tensor(wgs[:, 1, k, :], whole[:, k % 2, :], wgs[:, 0, k, :].bitcast(F32), ALU.subtract).then_inc(wg_low, 1)
            dve.wait_ge(w_in, 16 * 3)
            def turn(i):
                for n in range(H + 2):
                    if n < H:
                        h = n
                        dve.wait_ge(mean_done, i * H + h + 1)
                        dve.wait_ge(squared, i * H + max(h - 3, 0))
                        dve.wait_ge(of_done, i * H + max(h - 3, 0))
                        dve.tensor_tensor(oc[:, h % 4, :], o[:, h % 4, :], mean_ps[:, :], ALU.subtract).then_inc(centred, 1)
                    if n >= 2:
                        h = n - 2
                        g = i * H + h
                        dve.wait_ge(sd_done, g + 1)
                        dve.wait_ge(norm_step, i * H + max(h - 1, 0))
                        dve.reciprocal(rs[:, h % 2, :], sd[:, h % 2, :]).then_inc(rs_done, 1)
                        dve.wait_ge(rs_done, g + 1)
                        dve.scalar_tensor_tensor(oc[:, h % 4, :], oc[:, h % 4, :], gb[:, 0:1], rs[:, h % 2, :], ALU.mult, ALU.mult).then_inc(norm_step, 1)
                        dve.wait_ge(norm_step, g + 1)
                        dve.wait_ge(sg_done, g + 1)
                        dve.wait_ge(out_done, i * H + max(h - 1, 0))
                        dve.scalar_tensor_tensor(of[:, h % 2, :], oc[:, h % 4, :], gb[:, 1:2], sg[:, h % 4, :], ALU.add, ALU.mult).then_inc(of_done, 1)
                dve.wait_ge(out_done, (i + 1) * H)
                dve.wait_ge(x_in, (i + 1) * 16)
                dve.wait_ge(stored, i * 16)
                for s in range(SUB):
                    dve.tensor_tensor(xs[:, 1, s, :], xs[:, 0, s, :], out_ps[:, s, :], ALU.add).then_inc(added, 1)
            run_turns(dve, TT, turn)


def transform_phase(nc, w2, hadamard, w2t, F):
    FB = F // P
    STAGES = FB.bit_length() - 1
    with ExitStack() as ctx:
        m = Memory(nc, ctx, "w2")
        a = m.sb("a", [P, FB, D])
        b = m.sb("b", [P, FB, D])
        had = m.sb("had", [P, P])
        ps = m.ps("ps", [P, 4, D])
        w_in = m.sem("w_in")
        had_done = m.sem("had_done")
        had_copied = m.sem("had_copied")
        fly = m.sem("fly")
        stored = m.sem("stored")
        block = ctx.enter_context(nc.Block())
        final = (b, a)[STAGES % 2]

        @block.sync
        def _(sp):
            sp.dma_start(a[:, :, :], w2.rearrange("(f p) n -> p f n", p=P)).then_inc(w_in, 16)
            sp.dma_start(had[:, :], hadamard).then_inc(w_in, 16)
            sp.wait_ge(fly, 2 * STAGES)
            sp.dma_start(w2t.rearrange("(f p) n -> p f n", p=P), final[:, :, :]).then_inc(stored, 16)
            sp.wait_ge(stored, 16)

        @block.tensor
        def _(pe):
            pe.wait_ge(w_in, 32)
            for f in range(FB):
                if f >= 4:
                    pe.wait_ge(had_copied, f - 3)
                pe.matmul(ps[:, f % 4, :], had[:, :], a[:, f, :], start=True, stop=True).then_inc(had_done, 1)

        @block.scalar
        def _(act):
            for f in range(FB):
                act.wait_ge(had_done, f + 1)
                act.activation(b[:, f, :], ps[:, f % 4, :], ACT.Copy, scale=float(F) ** -0.5).then_inc(had_copied, 1)

        @block.vector
        def _(dve):
            dve.wait_ge(had_copied, FB)
            src, dst = b, a
            for stage in range(STAGES):
                step = 1 << stage
                dve.wait_ge(fly, 2 * stage)
                s = src[:, :, :].rearrange("p (a two b) n -> p a two (b n)", two=2, b=step)
                d = dst[:, :, :].rearrange("p (a two b) n -> p a two (b n)", two=2, b=step)
                dve.tensor_tensor(d[:, :, 0], s[:, :, 0], s[:, :, 1], ALU.add).then_inc(fly, 1)
                dve.tensor_tensor(d[:, :, 1], s[:, :, 0], s[:, :, 1], ALU.subtract).then_inc(fly, 1)
                src, dst = dst, src


def ffn_phase(nc, phase, ident, w1, w3, w2t, x, x_out, T, F):
    TT = T // TOK
    NT = T // P
    SUB = TOK // P
    NF = 2
    PIECE = NF * P
    PIECES = F // PIECE
    TILES = 2 * TT * NF
    with ExitStack() as ctx:
        m = Memory(nc, ctx, phase)
        raw = [m.sb("raw1", [P, KT, PIECE]), m.sb("raw3", [P, KT, PIECE]), m.sb("raw2", [P, NF, D])]
        w1s = m.sb("w1", [P, 2, 2, KT, PIECE], F32R)
        w3s = m.sb("w3", [P, 2, 2, KT, PIECE], F32R)
        w2s = m.sb("w2", [P, 2, 2, NF, D], F32R)
        xn = m.sb("xn", [P, 2, KT, T], F32R)
        gate = m.sb("gate", [P, 2, TOK])
        hid = m.sb("hid", [P, 2, TOK])
        hid_high = m.sb("hid_high", [P, 2, TOK], F32R)
        hid_low = m.sb("hid_low", [P, 2, TOK], F32R)
        xs = m.sb("xs", [P, NT, D])
        normal = m.sb("normal", [P, 2, D])
        idt = m.sb("ident", [P, P])
        stats = m.sb("stats", [P, NT, nc.vector.BN_STATS_DIM])
        mv = m.sb("mv", [P, NT, nc.vector.BN_AGGR_DIM])
        sd = m.sb("sd", [P, NT])
        rstd = m.sb("rstd", [P, NT])
        out_ps = m.ps("out", [P, SUB, D])
        g_ps = m.ps("g", [P, 2, TOK])
        l_ps = m.ps("l", [P, 2, TOK])
        w_in = m.sem("w_in")
        w_high = m.sem("w_high")
        w_low = m.sem("w_low")
        x_in = [m.sem(f"x_in{g}") for g in range(TT)]
        ident_in = m.sem("ident_in")
        stat = m.sem("stat")
        var_ready = m.sem("var_ready")
        sd_ready = m.sem("sd_ready")
        rstd_ready = m.sem("rstd_ready")
        normed = m.sem("normed")
        turned = m.sem("turned")
        xn_high = m.sem("xn_high")
        xn_low = m.sem("xn_low")
        gate_done = m.sem("gate_done")
        lin_done = m.sem("lin_done")
        silu_done = m.sem("silu_done")
        hid_done = m.sem("hid_done")
        high_done = m.sem("high_done")
        low_done = m.sem("low_done")
        out_done = m.sem("out_done")
        added = m.sem("added")
        stored = m.sem("stored")
        block = ctx.enter_context(nc.Block())
        tiles = [(u, t, n) for u in range(2) for t in range(TT) for n in range(NF)]
        HIGH, LOW = 0, 1
        PASSES = ((HIGH, HIGH), (HIGH, LOW), (LOW, HIGH))
        ADDS = TT * SUB

        def split(eng, u, count, op):
            for j, w in enumerate((w1s, w3s, w2s)):
                op(w[:, u, HIGH], w[:, u, LOW], raw[j], count + j)

        @block.sync
        def _(sp):
            def load(q):
                sp.dma_start(raw[0][:, :, :], w1[:, bass.ds(q * PIECE, PIECE)].rearrange("(k p) f -> p k f", p=P)).then_inc(w_in, 16)
                sp.dma_start(raw[1][:, :, :], w3[:, bass.ds(q * PIECE, PIECE)].rearrange("(k p) f -> p k f", p=P)).then_inc(w_in, 16)
                sp.dma_start(raw[2][:, :, :], w2t[bass.ds(q * PIECE, PIECE), :].rearrange("(f p) n -> p f n", p=P)).then_inc(w_in, 16)
            for g in range(TT):
                sp.dma_start(xs[:, g * SUB:(g + 1) * SUB, :], x[g * TOK:(g + 1) * TOK, :].rearrange("(n p) d -> p n d", p=P)).then_inc(x_in[g], 16)
            sp.dma_start(idt[:, :], ident).then_inc(ident_in, 16)
            load(0)
            with sp.Fori(1, PIECES) as q:
                sp.wait_ge(w_low, 3 * q)
                load(q)
            for t in range(TT):
                sp.wait_ge(added, (PIECES - 1) * ADDS + (t + 1) * SUB)
                sp.dma_start(x_out[t * TOK:(t + 1) * TOK, :].rearrange("(s p) d -> p s d", p=P),
                             xs[:, t * SUB:(t + 1) * SUB, :]).then_inc(stored, 16)
            sp.wait_ge(stored, 16 * TT)

        @block.tensor
        def _(pe):
            pe.wait_ge(ident_in, 16)
            for n in range(NT):
                pe.wait_ge(normed, n + 1)
                if n >= SUB:
                    pe.wait_ge(xn_low, n - SUB + 1)
                for k in range(KT):
                    tr = pe.transpose(out_ps[:, n % SUB, k * P:(k + 1) * P], normal[:, n % 2, k * P:(k + 1) * P], idt[:, :])
                tr.then_inc(turned, 1)
            pe.wait_ge(xn_low, NT)

            def turn(i, more):
                base = i * TILES

                def project(ps, w, x, done):
                    u, t, n = tiles[x]
                    for a, (wh, xh) in enumerate(PASSES):
                        for k in range(KT):
                            mm = pe.matmul(ps[:, x % 2, :], w[:, u, wh, k, n * P:(n + 1) * P], xn[:, xh, k, t * TOK:(t + 1) * TOK],
                                           start=(a == 0 and k == 0), stop=(a == 2 and k == KT - 1))
                    mm.then_inc(done, 1)

                def output(x):
                    u, t, n = tiles[x]
                    if n == 0:
                        pe.wait_ge(added, i * 2 * ADDS + (u * TT + t) * SUB)
                    pe.wait_ge(low_done, base + x + 1)
                    for s in range(SUB):
                        for a, (hh, wh) in enumerate(PASSES):
                            mm = pe.matmul(out_ps[:, s, :], (hid_high, hid_low)[hh][:, x % 2, s * P:(s + 1) * P], w2s[:, u, wh, n, :],
                                           start=(n == 0 and a == 0), stop=(n == NF - 1 and a == 2))
                    mm.then_inc(out_done, 1)
                for x in range(TILES):
                    u, t, n = tiles[x]
                    if t == 0 and n == 0:
                        pe.wait_ge(w_low, (i * 2 + u + 1) * 3)
                    pe.wait_ge(silu_done, base + max(x - 1, 0))
                    project(g_ps, w1s, x, gate_done)
                    pe.wait_ge(hid_done, base + max(x - 1, 0))
                    project(l_ps, w3s, x, lin_done)
                    if x:
                        output(x - 1)
                output(TILES - 1)
            run_all(pe, PIECES // 2, turn)

        @block.scalar
        def _(act):
            def copy(high, low, whole, count):
                act.activation(high, whole[:, :, :], ACT.Copy).then_inc(w_high, 1)
            act.wait_ge(var_ready, 1)
            act.activation(sd[:, :], sd[:, :], ACT.Sqrt).then_inc(sd_ready, 1)
            for n in range(NT):
                act.wait_ge(turned, n + 1)
                act.activation(xn[:, HIGH, :, n * P:(n + 1) * P], out_ps[:, n % SUB, :].rearrange("p (k t) -> p k t", k=KT),
                               ACT.Copy).then_inc(xn_high, 1)
            act.wait_ge(w_in, 48)
            split(act, 0, 0, copy)

            def turn(i, more):
                base = i * TILES
                for x, (u, t, n) in enumerate(tiles):
                    if t == TT // 2 and n == 0 and (u == 0 or more):
                        act.wait_ge(w_in, (i * 2 + u + 2) * 48)
                        act.wait_ge(out_done, base + u * TT * NF)
                        split(act, 1 - u, 0, copy)
                    act.wait_ge(gate_done, base + x + 1)
                    act.wait_ge(hid_done, base + max(x - 1, 0))
                    act.activation(gate[:, x % 2, :], g_ps[:, x % 2, :], ACT.Silu).then_inc(silu_done, 1)
                    act.wait_ge(hid_done, base + x + 1)
                    act.wait_ge(out_done, base + max(x - 1, 0))
                    act.activation(hid_high[:, x % 2, :], hid[:, x % 2, :], ACT.Copy).then_inc(high_done, 1)
            run_all(act, PIECES // 2, turn)

        @block.gpsimd
        def _(pool):
            def turn(i, more):
                base = i * TILES
                for x in range(TILES):
                    pool.wait_ge(high_done, base + x + 1)
                    pool.wait_ge(out_done, base + max(x - 1, 0))
                    pool.tensor_tensor(hid_low[:, x % 2, :], hid[:, x % 2, :], hid_high[:, x % 2, :].bitcast(F32),
                                       ALU.subtract).then_inc(low_done, 1)
            run_all(pool, PIECES // 2, turn)

        @block.vector
        def _(dve):
            def rest(high, low, whole, count):
                dve.wait_ge(w_high, count + 1)
                dve.tensor_tensor(low, whole[:, :, :], high.bitcast(F32), ALU.subtract).then_inc(w_low, 1)
            for n in range(NT):
                if n % SUB == 0:
                    dve.wait_ge(x_in[n // SUB], 16)
                dve.bn_stats(stats[:, n, :], xs[:, n, :]).then_inc(stat, 1)
            for n in range(NT):
                dve.wait_ge(stat, n + 1)
                aggregate = dve.bn_aggr(mv[:, n, :], stats[:, n, :])
            aggregate.then_inc(stat, 1)
            dve.wait_ge(stat, NT + 1)
            dve.tensor_scalar(sd[:, :], mv[:, :, 1], EPS, None, ALU.add).then_inc(var_ready, 1)
            dve.wait_ge(sd_ready, 1)
            dve.reciprocal(rstd[:, :], sd[:, :]).then_inc(rstd_ready, 1)
            dve.wait_ge(rstd_ready, 1)
            for n in range(NT + 1):
                if n < NT:
                    if n >= 2:
                        dve.wait_ge(turned, n - 1)
                    dve.tensor_scalar(normal[:, n % 2, :], xs[:, n, :], mv[:, n, 0:1], rstd[:, n:n + 1],
                                      ALU.subtract, ALU.mult).then_inc(normed, 1)
                if n:
                    b = n - 1
                    dve.wait_ge(xn_high, n)
                    dve.tensor_tensor(xn[:, LOW, :, b * P:n * P], out_ps[:, b % SUB, :].rearrange("p (k t) -> p k t", k=KT),
                                      xn[:, HIGH, :, b * P:n * P].bitcast(F32), ALU.subtract).then_inc(xn_low, 1)
            split(dve, 0, 0, rest)

            def turn(i, more):
                base = i * TILES

                def add(x):
                    u, t, n = tiles[x]
                    dve.wait_ge(out_done, base + x + 1)
                    dve.wait_ge(added, i * 2 * ADDS + u * ADDS)
                    for s in range(SUB):
                        y = xs[:, t * SUB + s, :]
                        dve.tensor_tensor(y, y, out_ps[:, s, :], ALU.add).then_inc(added, 1)
                for x, (u, t, n) in enumerate(tiles):
                    if t == TT // 2 and n == 0 and (u == 0 or more):
                        split(dve, 1 - u, (i * 2 + u + 1) * 3, rest)
                    dve.wait_ge(silu_done, base + x + 1)
                    dve.wait_ge(lin_done, base + x + 1)
                    dve.wait_ge(low_done, base + max(x - 1, 0))
                    dve.tensor_tensor(hid[:, x % 2, :], gate[:, x % 2, :], l_ps[:, x % 2, :], ALU.mult).then_inc(hid_done, 1)
                    if x and tiles[x - 1][2] == NF - 1:
                        add(x - 1)
                add(TILES - 1)
            run_all(dve, PIECES // 2, turn)


H = 16
C = 16
RING = 128
CHUNK = RING // 2
BPC = CHUNK // C
BPR = RING // C
GH = P // C
ROWS = 4
NR = C // ROWS
KB, QQ, KK, VB, AA = range(5)


def scan_phase(nc, streams, decays, o_dram, ident, head_mask, T):
    NB = T // C
    TURNS = T // RING
    with ExitStack() as ctx:
        m = Memory(nc, ctx, "scan")
        sb, ps, sem = m.sb, m.ps, m.sem
        ring = sb("ring", [P, 5, H, RING])
        blk = sb("blk", [P, 2, 5, C, H])
        stage = sb("stage", [P, 2, ROWS * ROWS * H * (NR * (NR + 1) // 2)])
        krow = sb("krow", [P, 2, C, C + 2, H])
        qrow = sb("qrow", [P, 2, C, C + 1, H])
        ud = sb("ud", [P, C, C + 2, H])
        prod = sb("prod", [P, (C + 1) * H])
        ktin = sb("ktin", [P, 2, C, GH])
        last_ud = sb("last_ud", [P, 2, C + 1, GH])
        ST = sb("ST", [P, H, P])
        abar = sb("abar", [P, H, P])
        kbd = sb("kbd", [P, 2, GH, P])
        uT = sb("uT", [P, 2, P])
        oring = sb("oring", [P, H, RING])
        idt = sb("idt", [P, P])
        ones = sb("ones", [P, P])
        hmask = sb("hmask", [P, GH])

        bc_ps = ps("bc_ps", [P, 2, 512])
        pq_ps = ps("pq_ps", [P, H, 2, C])
        tr_ps = ps("tr_ps", [P, 4, P])
        ds_ps = ps("ds_ps", [P, 4, 4, P])

        const_in = sem("const_in")
        init_done = sem("init_done")
        ud_zeroed = sem("ud_zeroed")
        chunk_in = [sem("chunk_in0"), sem("chunk_in1")]
        blk_ready = sem("blk_ready")
        kk_staged = sem("kk_staged")
        qk_staged = sem("qk_staged")
        bcast_done = sem("bcast_done")
        bcast_evac = sem("bcast_evac")
        kt_done = sem("kt_done")
        kbd_ready = sem("kbd_ready")
        pq_done = sem("pq_done")
        p_copied = sem("p_copied")
        q_copied = sem("q_copied")
        abar_in = sem("abar_in")
        u_step = sem("u_step")
        dec_step = sem("dec_step")
        dot_step = sem("dot_step")
        ut_done = sem("ut_done")
        ut_copied = sem("ut_copied")
        ds_done = sem("ds_done")
        s_decayed = sem("s_decayed")
        s_added = sem("s_added")
        po_done = sem("po_done")
        o_reduced = sem("o_reduced")
        o_stored = [sem("o_stored0"), sem("o_stored1")]
        NINIT = 5
        soff = [ROWS * ROWS * H * (r * (r + 1) // 2) for r in range(NR)]
        npair = [ROWS * (r + 1) for r in range(NR)]

        def stage_rows(eng, w, r, u):
            n = npair[r]
            left = blk[:, u % 2, w, ROWS * r:ROWS * (r + 1), :].unsqueeze(2).to_broadcast([P, ROWS, n, H])
            right = blk[:, u % 2, KK, 0:n, :].unsqueeze(1).to_broadcast([P, ROWS, n, H])
            out = stage[:, w, soff[r]:soff[r] + ROWS * n * H].rearrange("p (t j h) -> p t j h", t=ROWS, h=H)
            return eng.tensor_tensor(out, left, right, ALU.mult)

        def run(eng, prologue, body):
            prologue()
            for u in range(BPR):
                body(0, u, 2)
            with eng.Fori(1, TURNS - 1) as it:
                for u in range(BPR):
                    body(it, u, 2)
            for u in range(BPR):
                body(TURNS - 1, u, BPR - 1 - u)

        block = ctx.enter_context(nc.Block())

        @block.sync
        def _(sp):
            sp.dma_start(idt[:, :], ident).then_inc(const_in, 16)
            sp.dma_start(hmask[:, :], head_mask).then_inc(const_in, 16)

            def load(it, half):
                for w in range(5):
                    sp.dma_start(ring[:, w, :, half * CHUNK:(half + 1) * CHUNK],
                                 streams[w][:, :, bass.ds(it * RING + half * CHUNK, CHUNK)]
                                 .rearrange("h p t -> p h t")).then_inc(chunk_in[half], 16)

            def store(it, half):
                sp.wait_ge(o_reduced, ((it * 2 + half + 1) * BPC) * NR)
                sp.dma_start(o_dram[:, :, bass.ds(it * RING + half * CHUNK, CHUNK)]
                             .rearrange("h p t -> p h t"),
                             oring[:, :, half * CHUNK:(half + 1) * CHUNK]).then_inc(o_stored[half], 16)
            def load_abar(b):
                sp.dma_start(abar[:, :, :].rearrange("p h i -> p (h i)"),
                             decays[bass.ds(b, 1), :].to_broadcast([P, H * P])).then_inc(abar_in, 16)
            load(0, 0)
            load(0, 1)
            load_abar(0)
            with sp.Fori(0, TURNS - 1) as it:
                for u in range(BPR):
                    sp.wait_ge(s_decayed, 4 * (it * BPR + u + 1))
                    load_abar(it * BPR + u + 1)
                    if u % BPC == BPC - 1:
                        sp.wait_ge(blk_ready, it * BPR + u + 1)
                        load(it + 1, u // BPC)
                        store(it, u // BPC)
            for u in range(BPR):
                if u < BPR - 1:
                    sp.wait_ge(s_decayed, 4 * (NB - BPR + u + 1))
                    load_abar(NB - BPR + u + 1)
                if u % BPC == BPC - 1:
                    store(TURNS - 1, u // BPC)
            for half in range(2):
                sp.wait_ge(o_stored[half], 16 * TURNS)

        @block.scalar
        def _(act):
            def copy_block(it, u):
                it, u = (it + 1, u - BPR) if u >= BPR else (it, u)
                b = it * BPR + u
                act.wait_ge(chunk_in[u // BPC], 80 * (it + 1))
                if not (isinstance(b, int) and b < 1):
                    act.wait_ge(kt_done, b)
                if not (isinstance(b, int) and b < 2):
                    act.wait_ge(pq_done, b - 1)
                    act.wait_ge(u_step, C * (b - 1))
                    act.wait_ge(dec_step, C * (b - 1))
                act.activation(krow[:, u % 2, :, 0, :].rearrange("p t h -> p h t"),
                               ring[:, VB, :, u * C:(u + 1) * C], ACT.Copy)
                act.activation(blk[:, u % 2].rearrange("p w t h -> p w h t"),
                               ring[:, :, :, u * C:(u + 1) * C], ACT.Copy)
                for g in range(2):
                    last = act.activation(ktin[:, g].rearrange("p t h -> p h t"),
                                          ring[:, KK, g * GH:(g + 1) * GH, u * C:(u + 1) * C], ACT.Copy)
                last.then_inc(blk_ready, 1)

            def spread(it, u):
                it, u = (it + 1, u - BPR) if u >= BPR else (it, u)
                b = it * BPR + u
                n = 0
                for r in range(NR):
                    for w in range(2):
                        for p in range(2):
                            act.wait_ge(bcast_done, 16 * b + n + 1)
                            t = r * ROWS + 2 * p
                            rows = (krow[:, u % 2, t:t + 2, 2:2 + npair[r], :], qrow[:, u % 2, t:t + 2, 1:1 + npair[r], :])
                            act.activation(rows[w],
                                           bc_ps[:, n % 2, 0:2 * npair[r] * H]
                                           .rearrange("p (t j h) -> p t j h", t=2, h=H),
                                           ACT.Copy, scale=(-1.0, 1.0)[w]).then_inc(bcast_evac, 1)
                            n += 1

            def block_diagonal(it, u):
                it, u = (it + 1, u - BPR) if u >= BPR else (it, u)
                b = it * BPR + u
                act.wait_ge(kt_done, b + 1)
                if not (isinstance(b, int) and b < 1):
                    act.wait_ge(ds_done, 4 * b)
                for g in range(2):
                    for h in range(GH):
                        last = act.activation(kbd[:, g, h, :], tr_ps[:, g, :], ACT.Copy,
                                              scale=hmask[:, h:h + 1])
                last.then_inc(kbd_ready, 1)

            def prologue():
                act.wait_ge(const_in, 32)
                act.wait_ge(init_done, NINIT)
                copy_block(0, 0)
                spread(0, 0)
                block_diagonal(0, 0)
                copy_block(0, 1)

            def body(it, u, left):
                b = it * BPR + u
                first = isinstance(b, int) and b == 0
                act.wait_ge(pq_done, b + 1)
                act.activation(krow[:, u % 2, :, 1, :].rearrange("p t h -> p h t"), pq_ps[:, :, 0, :], ACT.Copy,
                               scale=-1.0).then_inc(p_copied, 1)
                act.activation(qrow[:, u % 2, :, 0, :].rearrange("p t h -> p h t"), pq_ps[:, :, 1, :], ACT.Copy).then_inc(q_copied, 1)
                if left >= 1:
                    if not first:
                        act.wait_ge(o_reduced, NR * b)
                    spread(it, u + 1)
                act.wait_ge(ut_done, b + 1)
                act.activation(uT[:, :, :], tr_ps[:, 2:4, :], ACT.Copy).then_inc(ut_copied, 1)
                if left >= 2:
                    copy_block(it, u + 2)
                if left >= 1:
                    block_diagonal(it, u + 1)
            run(act, prologue, body)

        @block.tensor
        def _(pe):
            def prep(it, u):
                it, u = (it + 1, u - BPR) if u >= BPR else (it, u)
                b = it * BPR + u
                pe.wait_ge(blk_ready, b + 1)
                if not (isinstance(b, int) and b < 1):
                    pe.wait_ge(kbd_ready, b)
                for g in range(2):
                    tr = pe.transpose(tr_ps[:, g, :], ktin[:, g].rearrange("p t h -> p (t h)"), idt[:, :])
                tr.then_inc(kt_done, 1)
                n = 0
                for r in range(NR):
                    for w in range(2):
                        pe.wait_ge((kk_staged, qk_staged)[w], NR * b + r + 1)
                        for p in range(2):
                            if isinstance(b, int) and 16 * b + n < 2:
                                pass
                            else:
                                pe.wait_ge(bcast_evac, 16 * b + n - 1)
                            m = 2 * npair[r] * H
                            pe.matmul(bc_ps[:, n % 2, 0:m], ones[:, :],
                                      stage[:, w, soff[r] + p * m:soff[r] + (p + 1) * m],
                                      start=True, stop=True).then_inc(bcast_done, 1)
                            n += 1

            def prologue():
                pe.wait_ge(const_in, 32)
                pe.wait_ge(init_done, NINIT)
                prep(0, 0)

            def body(it, u, left):
                b = it * BPR + u
                first = isinstance(b, int) and b == 0
                if not first:
                    pe.wait_ge(p_copied, b)
                    pe.wait_ge(q_copied, b)
                for q in range(4):
                    if not first:
                        pe.wait_ge(s_added, 4 * (b - 1) + q + 1)
                    for h in range(4 * q, 4 * q + 4):
                        m = pe.matmul(pq_ps[:, h], ST[:, h, :], blk[:, u % 2, 0:2, :, h], start=True, stop=True)
                m.then_inc(pq_done, 1)
                if left >= 1:
                    prep(it, u + 1)
                pe.wait_ge(u_step, C * (b + 1))
                pe.wait_ge(dec_step, C * (b + 1))
                for g in range(2):
                    tr = pe.transpose(tr_ps[:, 2 + g, :], last_ud[:, g, 1:C + 1, :].rearrange("p t h -> p (t h)"), idt[:, :])
                tr.then_inc(ut_done, 1)
                pe.wait_ge(kbd_ready, b + 1)
                pe.wait_ge(ut_copied, b + 1)
                for q in range(4):
                    for h in range(4):
                        m = pe.matmul(ds_ps[:, q, h, :], kbd[:, q // 2, 4 * (q % 2) + h, :], uT[:, q // 2, :],
                                      start=True, stop=True)
                    m.then_inc(ds_done, 1)
            run(pe, prologue, body)

        @block.gpsimd
        def _(pool):
            def stage_kk(it, u):
                it, u = (it + 1, u - BPR) if u >= BPR else (it, u)
                b = it * BPR + u
                pool.wait_ge(blk_ready, b + 1)
                for r in range(NR):
                    if not (isinstance(b, int) and b < 1):
                        pool.wait_ge(bcast_done, 16 * (b - 1) + 4 * r + 2)
                    stage_rows(pool, 0, r, u).then_inc(kk_staged, 1)

            def prologue():
                pool.memset(ud[:, :, :, :], 0.0).then_inc(ud_zeroed, 1)
                pool.wait_ge(ud_zeroed, 1)
                pool.memset(ud[:, :, 0, :], 1.0).then_inc(ud_zeroed, 1)
                pool.wait_ge(ud_zeroed, 2)
                pool.memset(ud[:, 0, 1, :], 1.0).then_inc(init_done, 1)
                pool.memset(krow[:, :, :, :, :], 0.0).then_inc(init_done, 1)
                pool.memset(qrow[:, :, :, :, :], 0.0).then_inc(init_done, 1)
                pool.wait_ge(init_done, NINIT)
                stage_kk(0, 0)
                stage_kk(0, 1)

            def body(it, u, left):
                b = it * BPR + u
                first = isinstance(b, int) and b == 0
                if not first:
                    pool.wait_ge(po_done, (NR + 1) * b)
                    pool.wait_ge(ut_done, b)
                    pool.wait_ge(u_step, C * b)
                for t in range(C):
                    if t:
                        pool.wait_ge(u_step, C * b + t)
                        pool.wait_ge(dec_step, C * b + t)
                    decay = blk[:, u % 2, AA, t, :].unsqueeze(1).to_broadcast([P, t + 1, H])
                    if t < C - 1:
                        pool.tensor_tensor(ud[:, t + 1, 1:t + 2, :], ud[:, t, 1:t + 2, :], decay, ALU.mult).then_inc(dec_step, 1)
                    else:
                        pool.tensor_tensor(last_ud[:, :, 0:C, :].rearrange("p g s h -> p s g h"),
                                           ud[:, t, 1:t + 2, :].rearrange("p s (g h) -> p s g h", g=2),
                                           decay.rearrange("p s (g h) -> p s g h", g=2), ALU.mult).then_inc(dec_step, 1)
                pool.wait_ge(u_step, C * (b + 1))
                pool.wait_ge(dec_step, C * (b + 1))
                pool.wait_ge(q_copied, b + 1)
                for r in range(NR):
                    t, n, m = ROWS * r, ROWS * (r + 1) + 1, ROWS - (r == NR - 1)
                    pool.tensor_tensor(qrow[:, u % 2, t:t + m, 0:n, :], qrow[:, u % 2, t:t + m, 0:n, :],
                                       ud[:, t + 1:t + 1 + m, 1:n + 1, :], ALU.mult).then_inc(po_done, 1)
                pool.tensor_tensor(qrow[:, u % 2, C - 1].rearrange("p s (g h) -> p s g h", g=2),
                                   qrow[:, u % 2, C - 1].rearrange("p s (g h) -> p s g h", g=2),
                                   last_ud[:, :, :, :].rearrange("p g s h -> p s g h"), ALU.mult).then_inc(po_done, 1)
                if left >= 2:
                    stage_kk(it, u + 2)
            run(pool, prologue, body)

        @block.vector
        def _(dve):
            def stage_qk(it, u):
                it, u = (it + 1, u - BPR) if u >= BPR else (it, u)
                b = it * BPR + u
                dve.wait_ge(blk_ready, b + 1)
                for r in range(NR):
                    if not (isinstance(b, int) and b < 1):
                        dve.wait_ge(bcast_done, 16 * (b - 1) + 4 * r + 4)
                    stage_rows(dve, 1, r, u).then_inc(qk_staged, 1)

            def prologue():
                dve.memset(ST[:, :, :], 0.0).then_inc(init_done, 1)
                dve.memset(ones[:, :], 1.0).then_inc(init_done, 1)
                dve.wait_ge(init_done, NINIT)
                stage_qk(0, 0)
                stage_qk(0, 1)

            def body(it, u, left):
                b = it * BPR + u
                first = isinstance(b, int) and b == 0
                dve.wait_ge(p_copied, b + 1)
                dve.wait_ge(bcast_evac, 16 * (b + 1))
                if not first:
                    dve.wait_ge(po_done, (NR + 1) * b)
                    dve.wait_ge(ut_done, b)
                for t in range(C):
                    if not (first and t == 0):
                        dve.wait_ge(dec_step, C * b + t)
                        dve.wait_ge(u_step, C * b + t)
                    n = (t + 2) * H
                    step = C * b + t
                    dve.tensor_tensor(prod[:, 0:n].rearrange("p (s h) -> p s h", h=H),
                                      krow[:, u % 2, t, 0:t + 2, :], ud[:, t, 0:t + 2, :],
                                      ALU.mult).then_inc(dot_step, 1)
                    dve.wait_ge(dot_step, step + 1)
                    if t < C - 1:
                        dve.tensor_reduce(ud[:, t + 1, t + 2, :], prod[:, 0:n].rearrange("p (s h) -> p h s", h=H),
                                          AX.X, ALU.add).then_inc(u_step, 1)
                    else:
                        dve.tensor_reduce(last_ud[:, :, C, :], prod[:, 0:n].rearrange("p (s g h) -> p g h s", g=2, h=GH),
                                          AX.X, ALU.add).then_inc(u_step, 1)
                dve.wait_ge(abar_in, 16 * (b + 1))
                dve.wait_ge(pq_done, b + 1)
                if not first:
                    dve.wait_ge(s_added, 4 * b)
                for q in range(4):
                    h = slice(4 * q, 4 * q + 4)
                    dve.tensor_tensor(ST[:, h, :], ST[:, h, :], abar[:, h, :], ALU.mult).then_inc(s_decayed, 1)
                for q in range(4):
                    h = slice(4 * q, 4 * q + 4)
                    dve.wait_ge(s_decayed, 4 * b + q + 1)
                    dve.wait_ge(ds_done, 4 * b + q + 1)
                    dve.tensor_tensor(ST[:, h, :], ST[:, h, :], ds_ps[:, q], ALU.add).then_inc(s_added, 1)
                if left >= 2:
                    stage_qk(it, u + 2)
                half = u // BPC
                if u % BPC == 0 and not (isinstance(it, int) and it == 0):
                    dve.wait_ge(o_stored[half], 16 * it)
                for r in range(NR):
                    t, n = ROWS * r, ROWS * (r + 1) + 1
                    dve.wait_ge(po_done, (NR + 1) * b + r + 1 + (r == NR - 1))
                    dve.tensor_reduce(oring[:, :, u * C + t:u * C + t + ROWS].rearrange("p h t -> p t h"),
                                      qrow[:, u % 2, t:t + ROWS, 0:n, :].rearrange("p t s h -> p t h s"),
                                      AX.X, ALU.add).then_inc(o_reduced, 1)
            run(dve, prologue, body)


NEG = -2.0 ** 100


def rope_phase(nc, xnT, w_rot, wv, cos, sin, qk_dram, v_dram, T):
    phase = "rope"
    TT = T // TOK
    NT = T // P
    CB = D // P
    with ExitStack() as ctx:
        m = Memory(nc, ctx, phase)
        xn = m.sb("xn", [P, KT, T])
        w = m.sb("w", [P, 4, KT, D])
        wvs = m.sb("wv", [P, KT, D])
        tab = m.sb("tab", [P, 2, T])
        part = m.sb("part", [P, 2, 2, TOK])
        rot = m.sb("rot", [P, 4, TOK])
        high = m.sb("high", [P, 4, TOK], F32R)
        low = m.sb("low", [P, 4, TOK], F32R)
        vrow = m.sb("vrow", [P, 4, D])
        acc = m.ps("acc", [P, 3, 2, TOK])
        v_ps = m.ps("v_ps", [P, 2, D])
        loaded = m.sem("loaded")
        pair_done = m.sem("pair_done")
        turned = m.sem("turned")
        rot_done = m.sem("rot_done")
        rot_stored = [m.sem(f"rot_stored{i}") for i in range(4)]
        high_done = m.sem("high_done")
        low_done = m.sem("low_done")
        v_done = m.sem("v_done")
        v_copied = m.sem("v_copied")
        v_stored = [m.sem(f"v_stored{i}") for i in range(4)]
        NLOAD = 2 * KT + 4 * KT + 2
        units = [(c, j, t) for c in range(CB) for j in range(2) for t in range(TT)]
        block = ctx.enter_context(nc.Block())

        @block.sync
        def _(sp):
            for k in range(KT):
                sp.dma_start(xn[:, k, :], xnT[0, k]).then_inc(loaded, 16)
                sp.dma_start(wvs[:, k, :], wv[k * P:(k + 1) * P, :]).then_inc(loaded, 16)
                for j in range(4):
                    sp.dma_start(w[:, j, k, :], w_rot[j][k * P:(k + 1) * P, :]).then_inc(loaded, 16)
            sp.dma_start(tab[:, 0, :], cos).then_inc(loaded, 16)
            sp.dma_start(tab[:, 1, :], sin).then_inc(loaded, 16)
            for n, (c, j, t) in enumerate(units):
                sp.wait_ge(high_done, n + 1)
                sp.dma_start(qk_dram[j, 0, c * P:(c + 1) * P, t * TOK:(t + 1) * TOK], high[:, n % 4, :].bitcast(F32)).then_inc(rot_stored[n % 4], 16)
                sp.wait_ge(low_done, n + 1)
                sp.dma_start(qk_dram[j, 1, c * P:(c + 1) * P, t * TOK:(t + 1) * TOK], low[:, n % 4, :].bitcast(F32)).then_inc(rot_stored[n % 4], 16)
                if n % 2:
                    v = n // 2
                    sp.wait_ge(v_copied, v + 1)
                    sp.dma_start(v_dram[v * P:(v + 1) * P, :], vrow[:, v % 4, :]).then_inc(v_stored[v % 4], 16)
            for r in range(4):
                sp.wait_ge(rot_stored[r], 32 * (len(units) // 4))
                sp.wait_ge(v_stored[r], 16 * (NT // 4))

        @block.tensor
        def _(pe):
            pe.wait_ge(loaded, 16 * NLOAD)
            for n, (c, j, t) in enumerate(units):
                if n >= 3:
                    pe.wait_ge(rot_done, n - 2)
                for r in range(2):
                    for k in range(KT):
                        mm = pe.matmul(acc[:, n % 3, r, :], w[:, 2 * j + r, k, c * P:(c + 1) * P],
                                       xn[:, k, t * TOK:(t + 1) * TOK], start=(k == 0), stop=(k == KT - 1))
                mm.then_inc(pair_done, 1)
                if n % 2:
                    v = n // 2
                    if v >= 2:
                        pe.wait_ge(v_copied, v - 1)
                    for k in range(KT):
                        mm = pe.matmul(v_ps[:, v % 2, :], xn[:, k, v * P:(v + 1) * P], wvs[:, k, :], start=(k == 0), stop=(k == KT - 1))
                    mm.then_inc(v_done, 1)

        @block.vector
        def _(dve):
            dve.wait_ge(loaded, 16 * NLOAD)
            for n, (c, j, t) in enumerate(units):
                dve.wait_ge(pair_done, n + 1)
                if n >= 2:
                    dve.wait_ge(rot_done, n - 1)
                for r in range(2):
                    dve.tensor_tensor(part[:, n % 2, r, :], acc[:, n % 3, r, :], tab[:, r, t * TOK:(t + 1) * TOK], ALU.mult).then_inc(turned, 1)
                dve.wait_ge(turned, 2 * n + 2)
                if n >= 4:
                    dve.wait_ge(low_done, n - 3)
                dve.tensor_tensor(rot[:, n % 4, :], part[:, n % 2, 0, :], part[:, n % 2, 1, :], ALU.add).then_inc(rot_done, 1)

        @block.scalar
        def _(act):
            for n in range(len(units)):
                act.wait_ge(rot_done, n + 1)
                if n >= 4:
                    act.wait_ge(rot_stored[n % 4], 32 * (n // 4))
                    act.wait_ge(low_done, n - 3)
                act.activation(high[:, n % 4, :], rot[:, n % 4, :], ACT.Copy).then_inc(high_done, 1)
                if n % 2:
                    v = n // 2
                    act.wait_ge(v_done, v + 1)
                    if v >= 4:
                        act.wait_ge(v_stored[v % 4], 16 * (v // 4))
                    act.activation(vrow[:, v % 4, :], v_ps[:, v % 2, :], ACT.Copy).then_inc(v_copied, 1)

        @block.gpsimd
        def _(pool):
            for n in range(len(units)):
                pool.wait_ge(high_done, n + 1)
                if n >= 4:
                    pool.wait_ge(rot_stored[n % 4], 32 * (n // 4))
                pool.tensor_tensor(low[:, n % 4, :], rot[:, n % 4, :], high[:, n % 4, :].bitcast(F32), ALU.subtract).then_inc(low_done, 1)


def chunks_of(q):
    n = (q + 1) * P
    return [(c, min(TOK, n - c)) for c in range(0, n, TOK)]


def load_stacks(sp, dst, qk_dram, h, DH, done):
    for j, halves in ((0, (0, 1, 0)), (1, (0, 0, 1))):
        for s, half in enumerate(halves):
            sp.dma_start(dst[s * DH:(s + 1) * DH, j, :].bitcast(F32), qk_dram[j, half, bass.ds(h * DH, DH), :]).then_inc(done, 16)


def column_sum_phase(nc, qk_dram, causal, sums, T, NH, DH):
    phase = "csum"
    NT = T // P
    NC = T // TOK
    SCALE = float(DH) ** -0.5
    order = list(range(NT - 1, -1, -1))
    with ExitStack() as ctx:
        m = Memory(nc, ctx, phase)
        qk = m.sb("qk", [3 * DH, 2, 2, T], F32R)
        cm = m.sb("cm", [P, 2, P], F32R)
        cmf = m.sb("cmf", [P, 2, P])
        e = m.sb("e", [P, 2, T])
        mx = m.sb("mx", [P, 2])
        nb = m.sb("nb", [P, 2])
        rsum = m.sb("rsum", [P, 2])
        rinv = m.sb("rinv", [P, 2])
        tot = m.sb("tot", [P, T])
        ones = m.sb("ones", [P, 1])
        row = m.sb("row", [1, T])
        sc = m.ps("sc", [P, 2, T])
        cm_in = m.sem("cm_in")
        init = m.sem("init")
        qk_in = [m.sem("qk_in0"), m.sem("qk_in1")]
        scored = m.sem("scored")
        maxed = m.sem("maxed")
        biased = m.sem("biased")
        expd = m.sem("expd")
        inverted = m.sem("inverted")
        totalled = m.sem("totalled")
        summed = m.sem("summed")
        row_done = m.sem("row_done")
        row_stored = m.sem("row_stored")
        block = ctx.enter_context(nc.Block())
        TILES = NT

        @block.sync
        def _(sp):
            for j in range(2):
                sp.dma_start(cmf[:, j, :], causal[j]).then_inc(cm_in, 16)

            def load(h, u):
                load_stacks(sp, qk[:, u], qk_dram, h, DH, qk_in[u])
            load(0, 0)
            load(1, 1)
            def turn(i):
                for u in range(2):
                    sp.wait_ge(summed, i * 2 + u + 1)
                    load(i * 2 + u + 2, u)
                    sp.wait_ge(row_done, i * 2 + u + 1)
                    sp.dma_start(sums[bass.ds(i * 2 + u, 1), :], row[:, :]).then_inc(row_stored, 16)
            run_turns(sp, NH // 2 - 1, turn)
            for u in range(2):
                sp.wait_ge(row_done, NH - 1 + u)
                sp.dma_start(sums[NH - 2 + u:NH - 1 + u, :], row[:, :]).then_inc(row_stored, 16)
            sp.wait_ge(row_stored, 16 * NH)

        @block.tensor
        def _(pe):
            pe.wait_ge(init, 3)
            def turn(i):
                for u in range(2):
                    h = i * 2 + u
                    pe.wait_ge(qk_in[u], (i + 1) * 96)
                    for n, q in enumerate(order):
                        g = h * TILES + n
                        if n >= 2:
                            pe.wait_ge(expd, g - 1)
                        else:
                            pe.wait_ge(expd, h * TILES)
                            pe.wait_ge(row_done, h)
                        for c, w in chunks_of(q):
                            pe.matmul(sc[:, n % 2, c:c + w], qk[:, u, 0, q * P:(q + 1) * P], qk[:, u, 1, c:c + w],
                                      start=True, stop=(c + w < (q + 1) * P))
                        mm = pe.matmul(sc[:, n % 2, q * P:(q + 1) * P], cm[:, 0, :], cm[:, 1, :], start=False, stop=True)
                        mm.then_inc(scored, 1)
                    pe.wait_ge(totalled, (h + 1) * TILES)
                    pe.wait_ge(expd, (h + 1) * TILES)
                    for c in range(NC):
                        mm = pe.matmul(sc[0:1, 0, c * TOK:(c + 1) * TOK], ones[:, :], tot[:, c * TOK:(c + 1) * TOK], start=True, stop=True)
                    mm.then_inc(summed, 1)
            run_turns(pe, NH // 2, turn)

        @block.scalar
        def _(act):
            def turn(i):
                for u in range(2):
                    h = i * 2 + u
                    for n, q in enumerate(order):
                        g = h * TILES + n
                        act.wait_ge(maxed, g + 1)
                        act.wait_ge(expd, h * TILES + max(n - 1, 0))
                        act.activation(nb[:, n % 2:n % 2 + 1], mx[:, n % 2:n % 2 + 1], ACT.Copy, scale=SCALE).then_inc(biased, 1)
                        act.wait_ge(biased, g + 1)
                        act.wait_ge(totalled, h * TILES + max(n - 1, 0))
                        act.activation(e[:, n % 2, 0:(q + 1) * P], sc[:, n % 2, 0:(q + 1) * P], ACT.Exp,
                                       bias=nb[:, n % 2:n % 2 + 1], scale=SCALE, accum_out=rsum[:, n % 2:n % 2 + 1]).then_inc(expd, 1)
                    act.wait_ge(summed, h + 1)
                    act.wait_ge(row_stored, h * 16)
                    act.activation(row[:, :], sc[0:1, 0, :], ACT.Copy).then_inc(row_done, 1)
            run_turns(act, NH // 2, turn)

        @block.vector
        def _(dve):
            dve.memset(ones[:, :], 1.0).then_inc(init, 1)
            dve.wait_ge(cm_in, 32)
            dve.tensor_copy(cm[:, 0, :], cmf[:, 0, :]).then_inc(init, 1)
            dve.tensor_copy(cm[:, 1, :], cmf[:, 1, :]).then_inc(init, 1)
            def turn(i):
                for u in range(2):
                    h = i * 2 + u

                    def peak(n, q):
                        g = h * TILES + n
                        dve.wait_ge(scored, g + 1)
                        dve.tensor_reduce(mx[:, n % 2:n % 2 + 1], sc[:, n % 2, 0:(q + 1) * P], AX.X, ALU.max,
                                          negate=True).then_inc(maxed, 1)

                    def total(n, q):
                        g = h * TILES + n
                        w = (q + 1) * P
                        dve.wait_ge(expd, g + 1)
                        dve.wait_ge(totalled, g)
                        dve.reciprocal(rinv[:, n % 2:n % 2 + 1], rsum[:, n % 2:n % 2 + 1]).then_inc(inverted, 1)
                        dve.wait_ge(inverted, g + 1)
                        if n == 0:
                            dve.wait_ge(summed, h)
                            dve.tensor_scalar(tot[:, 0:w], e[:, n % 2, 0:w], rinv[:, n % 2:n % 2 + 1], None, ALU.mult).then_inc(totalled, 1)
                        else:
                            dve.scalar_tensor_tensor(tot[:, 0:w], e[:, n % 2, 0:w], rinv[:, n % 2:n % 2 + 1], tot[:, 0:w],
                                                     ALU.mult, ALU.add).then_inc(totalled, 1)
                    for n, q in enumerate(order):
                        peak(n, q)
                        if n:
                            total(n - 1, order[n - 1])
                    total(NT - 1, order[-1])
            run_turns(dve, NH // 2, turn)


def heavy_phase(nc, sums, bias_dram, biasT_dram, ident, T, NH, BUDGET, RECENT):
    phase = "heavy"
    ROUNDS = -(-BUDGET // 8)
    REST = BUDGET - 8 * (ROUNDS - 1)
    with ExitStack() as ctx:
        m = Memory(nc, ctx, phase)
        s = m.sb("s", [NH, T])
        top = m.sb("top", [NH, 8])
        PAD = RECENT - P
        padded = m.sb("padded", [NH, PAD + T])
        bias = padded[:, PAD:PAD + T]
        idt = m.sb("ident", [NH, NH])
        biasT = m.sb("biasT", [P, 2, NH, T // P])
        tr = m.ps("tr", [P, 2, T // P, NH])
        s_in = m.sem("s_in")
        turned = m.sem("turned")
        copied = m.sem("copied")
        step = m.sem("step")
        cleared = m.sem("cleared")
        bias_done = m.sem("bias_done")
        stored = m.sem("stored")
        block = ctx.enter_context(nc.Block())

        @block.sync
        def _(sp):
            sp.dma_start(s[:, :], sums).then_inc(s_in, 16)
            sp.dma_start(idt[:, :], ident[0:NH, 0:NH]).then_inc(s_in, 16)
            sp.wait_ge(bias_done, 1)
            sp.dma_start(bias_dram, bias[:, :]).then_inc(stored, 16)
            sp.wait_ge(copied, 1)
            for j in range(2):
                sp.dma_start(biasT_dram[j].rearrange("h p n -> p h n"), biasT[:, j]).then_inc(stored, 16)
            sp.wait_ge(stored, 48)

        @block.tensor
        def _(pe):
            pe.wait_ge(s_in, 32)
            pe.wait_ge(cleared, 1)
            pe.wait_ge(bias_done, 1)
            for j, first in enumerate((PAD, 0)):
                for n in range(T // P):
                    t = pe.transpose(tr[:, j, n, :], padded[:, first + n * P:first + (n + 1) * P], idt[:, :])
            t.then_inc(turned, 1)

        @block.scalar
        def _(act):
            act.wait_ge(turned, 1)
            act.activation(biasT[:, :, :, :].rearrange("p j h n -> p j n h"), tr[:, :, :, :], ACT.Copy).then_inc(copied, 1)

        @block.vector
        def _(dve):
            dve.memset(padded[:, 0:PAD], 0.0).then_inc(cleared, 1)
            dve.wait_ge(s_in, 32)
            for r in range(ROUNDS):
                if r:
                    dve.wait_ge(step, 2 * r)
                dve.max(top[:, :], s[:, :]).then_inc(step, 1)
                dve.wait_ge(step, 2 * r + 1)
                if r == ROUNDS - 1 and REST < 8:
                    dve.memset(top[:, REST:8], -1.0).then_inc(step, 1)
                    dve.wait_ge(step, 2 * r + 2)
                dve.match_replace(s[:, :], top[:, :], s[:, :], -1.0).then_inc(step, 1)
            dve.wait_ge(step, 2 * ROUNDS + (REST < 8))
            dve.tensor_scalar(bias[:, :], s[:, :], 0.0, NEG, ALU.is_ge, ALU.mult).then_inc(bias_done, 1)


def chosen_max_phase(nc, qk_dram, bias_dram, biasT_dram, causal, before_mask, ident, peaks_dram, T, NH, DH, RECENT):
    phase = "cmax"
    NT = T // P
    K = 3 * DH
    order = list(range(NT - 1, -1, -1))
    WINDOWS = NT - 1
    with ExitStack() as ctx:
        m = Memory(nc, ctx, phase)
        qk = m.sb("qk", [K + 1, 2, 2, T], F32R)
        hcol = m.sb("hcol", [P, 2, NT])
        cmf = m.sb("cmf", [P, 3, P])
        cm = m.sb("cm", [P, 3, P], F32R)
        diag = m.sb("diag", [P, 4, P], F32R)
        peak = m.sb("peak", [P, NH * NT])
        high = m.sb("high", [P, NH * NT], F32R)
        low = m.sb("low", [P, NH * NT], F32R)
        rows = m.sb("rows", [P, 2, NH * NT // P, P], F32R)
        sc = m.ps("sc", [P, 2, T])
        consts_in = m.sem("consts_in")
        init = m.sem("init")
        head_in = [m.sem("head_in0"), m.sem("head_in1")]
        diag_done = m.sem("diag_done")
        scored = m.sem("scored")
        peaked = m.sem("peaked")
        halved = m.sem("halved")
        turned = m.sem("turned")
        copied = m.sem("copied")
        stored = m.sem("stored")
        block = ctx.enter_context(nc.Block())

        @block.sync
        def _(sp):
            for j, mask in enumerate((causal[0], causal[1], before_mask)):
                sp.dma_start(cmf[:, j, :], mask).then_inc(consts_in, 16)

            def load(h, u):
                load_stacks(sp, qk[:, u], qk_dram, h, DH, head_in[u])
                sp.dma_start(qk[K:K + 1, u, 1, :].bitcast(F32), bias_dram[bass.ds(h, 1), :]).then_inc(head_in[u], 16)
                sp.dma_start(hcol[:, u, :], biasT_dram[1, bass.ds(h, 1)].rearrange("o p n -> p (o n)")).then_inc(head_in[u], 16)
            load(0, 0)
            load(1, 1)

            def turn(i):
                for u in range(2):
                    sp.wait_ge(peaked, (i * 2 + u + 1) * NT)
                    load(i * 2 + u + 2, u)
            run_turns(sp, NH // 2 - 1, turn)
            sp.wait_ge(copied, 1)
            for j in range(2):
                sp.dma_start(peaks_dram[j].rearrange("(a p) n -> p a n", p=P), rows[:, j].bitcast(F32)).then_inc(stored, 16)
            sp.wait_ge(stored, 32)

        @block.tensor
        def _(pe):
            pe.wait_ge(init, 5)

            def turn(i):
                for u in range(2):
                    h = i * 2 + u
                    pe.wait_ge(head_in[u], (i + 1) * 128)
                    for n, q in enumerate(order):
                        end, far = (q + 1) * P, q * P - RECENT
                        queries = qk[:, u, 0, q * P:end]
                        pe.wait_ge(peaked, h * NT + max(n - 1, 0))
                        for c, w in chunks_of(q):
                            split = min(max(far, c), c + w)
                            if split > c:
                                pe.matmul(sc[:, n % 2, c:split], queries, qk[:, u, 1, c:split], start=True, stop=True)
                            if split < c + w:
                                pe.matmul(sc[:, n % 2, split:c + w], queries[0:K], qk[0:K, u, 1, split:c + w], start=True, stop=False)
                        if q:
                            pe.wait_ge(diag_done, h * WINDOWS + n + 1)
                            cuts = sorted({max(far, 0), far + P} | {c for c in range(0, T, TOK) if max(far, 0) < c < far + P})
                            for a, b in zip(cuts, cuts[1:]):
                                pe.matmul(sc[:, n % 2, a:b], cm[:, 2, :], diag[:, n % 4, a - far:b - far],
                                          start=False, stop=(a // TOK != q * P // TOK))
                        mm = pe.matmul(sc[:, n % 2, q * P:end], cm[:, 0, :], cm[:, 1, :], start=False, stop=True)
                        mm.then_inc(scored, 1)
            run_turns(pe, NH // 2, turn)
            pe.wait_ge(halved, 2)
            pe.wait_ge(peaked, NH * NT)
            for j, half in enumerate((high, low)):
                for a in range(NH * NT // P):
                    t = pe.transpose(sc[:, 0, (2 * j + a) * P:(2 * j + a + 1) * P], half[:, a * P:(a + 1) * P].bitcast(F32), cmf[:, 0, :])
            t.then_inc(turned, 1)

        @block.scalar
        def _(act):
            act.wait_ge(consts_in, 48)

            def turn(i):
                for u in range(2):
                    h = i * 2 + u
                    act.wait_ge(head_in[u], (i + 1) * 128)
                    for n, q in enumerate(order[:WINDOWS]):
                        act.wait_ge(scored, h * NT + max(n - 3, 0))
                        act.activation(diag[:, n % 4, :], cmf[:, 0, :], ACT.Copy, scale=hcol[:, u, q - 1:q]).then_inc(diag_done, 1)
            run_turns(act, NH // 2, turn)
            act.wait_ge(turned, 1)
            act.activation(rows[:, :, :, :].rearrange("p j a n -> p (j a n)"), sc[:, 0, 0:4 * P], ACT.Copy).then_inc(copied, 1)

        @block.vector
        def _(dve):
            for u in range(2):
                dve.memset(qk[K:K + 1, u, 0, :].bitcast(F32), 1.0).then_inc(init, 1)
            dve.wait_ge(consts_in, 48)
            for j in range(3):
                dve.tensor_copy(cm[:, j, :], cmf[:, j, :]).then_inc(init, 1)

            def turn(i):
                for u in range(2):
                    h = i * 2 + u
                    for n, q in enumerate(order):
                        dve.wait_ge(scored, h * NT + n + 1)
                        dve.tensor_reduce(peak[:, bass.ds(h * NT + q, 1)], sc[:, n % 2, 0:(q + 1) * P], AX.X, ALU.max,
                                          negate=True).then_inc(peaked, 1)
            run_turns(dve, NH // 2, turn)
            dve.wait_ge(peaked, NH * NT)
            dve.tensor_copy(high[:, :], peak[:, :]).then_inc(halved, 1)
            dve.wait_ge(halved, 1)
            dve.tensor_tensor(low[:, :], peak[:, :], high[:, :].bitcast(F32), ALU.subtract).then_inc(halved, 1)


def attend_phase(nc, qk_dram, v_dram, biasT_dram, peaks_dram, masks, attnT, T, NH, DH, RECENT):
    phase = "attend"
    NT = T // P
    G = TOK // P
    SCALE = float(DH) ** -0.5
    NEAR = -(-(RECENT + 1 - P) // P) + 1
    RINGS = 4
    with ExitStack() as ctx:
        m = Memory(nc, ctx, phase)
        K = 3 * DH + 2
        qk = m.sb("qk", [K, 2, 2, T], F32R)
        v = m.sb("v", [P, 2, NT, 2 * DH])
        hcol = m.sb("hcol", [P, 2, NT])
        cmf = m.sb("cmf", [P, 2, P])
        cm = m.sb("cm", [P, 2, P], F32R)
        fm = m.sb("far", [P, NEAR, P])
        e = m.sb("e", [P, RINGS, TOK])
        inv = m.sb("inv", [DH, 2, TOK])
        orow = m.sb("orow", [DH, 2, T])
        sc = m.ps("sc", [P, RINGS, TOK])
        ot = m.ps("ot", [2 * DH, 2, TOK])
        consts_in = m.sem("consts_in")
        init = m.sem("init")
        head_in = [m.sem("head_in0"), m.sem("head_in1")]
        scored = m.sem("scored")
        biased = m.sem("biased")
        expd = m.sem("expd")
        summed = m.sem("summed")
        inverted = m.sem("inverted")
        scaled = m.sem("scaled")
        out_stored = [m.sem("out_stored0"), m.sem("out_stored1")]
        block = ctx.enter_context(nc.Block())
        units = []
        for g in range(NT // G):
            for kt in range(G * g + G):
                lo = max(kt - G * g, 0) * P
                near = min(max((kt + NEAR + 1 - G * g) * P, lo), TOK)
                mixes = [(j, G * g + j - kt) for j in range(G) if 1 <= G * g + j - kt <= NEAR]
                units.append((g, kt, lo, near, mixes))
        U = len(units)
        NB = sum(len(x[4]) > 0 for x in units)
        NG = NT // G
        last_of = {g: max(x for x, y in enumerate(units) if y[0] == g) for g in range(NG)}

        @block.sync
        def _(sp):
            for j in range(2):
                sp.dma_start(cmf[:, j, :], masks[j]).then_inc(consts_in, 16)
            for j in range(NEAR):
                sp.dma_start(fm[:, j, :], masks[2 + j]).then_inc(consts_in, 16)
            sp.wait_ge(init, 6)

            def load(h, u):
                load_stacks(sp, qk[:, u], qk_dram, h, DH, head_in[u])
                for j in range(2):
                    sp.dma_start(qk[3 * DH + j:3 * DH + j + 1, u, 0, :].bitcast(F32), peaks_dram[j, bass.ds(h * NT, NT), :].rearrange("(o a) n -> o (a n)", o=1)).then_inc(head_in[u], 16)
                sp.dma_start(v[:, u, :, 0:DH], v_dram[:, bass.ds(h * DH, DH)].rearrange("(n p) d -> p n d", p=P)).then_inc(head_in[u], 16)
                sp.dma_start(hcol[:, u, :], biasT_dram[0, bass.ds(h, 1)].rearrange("o p n -> p (o n)")).then_inc(head_in[u], 16)

            def store(h, u):
                sp.wait_ge(scaled, (h + 1) * NG)
                sp.dma_start(attnT[bass.ds(h * DH, DH), :], orow[:, u, :]).then_inc(out_stored[u], 16)
            load(0, 0)
            load(1, 1)

            def turn(i):
                for u in range(2):
                    store(i * 2 + u, u)
                    load(i * 2 + u + 2, u)
            run_turns(sp, NH // 2 - 1, turn)
            for u in range(2):
                store(NH - 2 + u, u)
                sp.wait_ge(out_stored[u], 16 * (NH // 2))

        @block.tensor
        def _(pe):
            pe.wait_ge(init, 6)

            def turn(i):
                for u in range(2):
                    h = i * 2 + u
                    pe.wait_ge(head_in[u], (i + 1) * 160)

                    def scores(x):
                        g, kt, lo, near, mixes = units[x]
                        pe.wait_ge(expd, h * U + max(x - RINGS + 1, 0))
                        diagonal = kt >= G * g
                        mm = pe.matmul(sc[:, x % RINGS, lo:TOK], qk[:, u, 1, kt * P:(kt + 1) * P],
                                       qk[:, u, 0, g * TOK + lo:(g + 1) * TOK], start=True, stop=not diagonal)
                        if diagonal:
                            mm = pe.matmul(sc[:, x % RINGS, lo:lo + P], cm[:, 0, :], cm[:, 1, :], start=False, stop=True)
                        mm.then_inc(scored, 1)

                    def values(x):
                        g, kt, lo, near, mixes = units[x]
                        pe.wait_ge(expd, h * U + x + 1)
                        if kt == 0:
                            pe.wait_ge(scaled, h * NG + max(g - 1, 0))
                        pe.matmul(ot[:, g % 2, lo:TOK], v[:, u, kt, :], e[:, x % RINGS, lo:TOK],
                                  start=(kt == 0), stop=(x == last_of[g])).then_inc(summed, 1)
                    for x in range(U + 2):
                        if x < U:
                            scores(x)
                        if x >= 2:
                            values(x - 2)
            run_turns(pe, NH // 2, turn)

        @block.scalar
        def _(act):
            act.wait_ge(consts_in, 32 + 16 * NEAR)

            def turn(i):
                for u in range(2):
                    h = i * 2 + u
                    fixed = 0
                    act.wait_ge(head_in[u], (i + 1) * 160)
                    for x, (g, kt, lo, near, mixes) in enumerate(units):
                        fixed += len(mixes) > 0
                        act.wait_ge(scored, h * U + x + 1)
                        if mixes:
                            act.wait_ge(biased, h * NB + fixed)
                        act.wait_ge(summed, h * U + max(x - RINGS + 1, 0))
                        if near > lo:
                            op = act.activation(e[:, x % RINGS, lo:near], sc[:, x % RINGS, lo:near], ACT.Exp, scale=SCALE)
                        if near < TOK:
                            op = act.activation(e[:, x % RINGS, near:TOK], sc[:, x % RINGS, near:TOK], ACT.Exp,
                                                bias=hcol[:, u, kt:kt + 1], scale=SCALE)
                        op.then_inc(expd, 1)
            run_turns(act, NH // 2, turn)

        @block.vector
        def _(dve):
            for u in range(2):
                dve.memset(qk[3 * DH:K, u, 1, :].bitcast(F32), 1.0).then_inc(init, 1)
                dve.memset(v[:, u, :, DH:2 * DH], 1.0).then_inc(init, 1)
            dve.wait_ge(consts_in, 32 + 16 * NEAR)
            for j in range(2):
                dve.tensor_copy(cm[:, j, :], cmf[:, j, :]).then_inc(init, 1)

            def turn(i):
                for u in range(2):
                    h = i * 2 + u

                    def finish(g):
                        k = h * NG + g
                        dve.wait_ge(summed, h * U + last_of[g] + 1)
                        dve.reciprocal(inv[:, g % 2, :], ot[DH:2 * DH, g % 2, :]).then_inc(inverted, 1)
                        dve.wait_ge(inverted, k + 1)
                        if g == 0:
                            dve.wait_ge(out_stored[u], i * 16)
                        dve.tensor_tensor(orow[:, u, g * TOK:(g + 1) * TOK], ot[0:DH, g % 2, :], inv[:, g % 2, :], ALU.mult).then_inc(scaled, 1)
                    dve.wait_ge(head_in[u], (i + 1) * 160)
                    for x, (g, kt, lo, near, mixes) in enumerate(units):
                        if mixes:
                            dve.wait_ge(scored, h * U + x + 1)
                            for j, d in mixes:
                                s = sc[:, x % RINGS, j * P:(j + 1) * P]
                                op = dve.scalar_tensor_tensor(s, fm[:, d - 1, :], hcol[:, u, kt:kt + 1], s, ALU.mult, ALU.add)
                            op.then_inc(biased, 1)
                        if g and kt == 3:
                            finish(g - 1)
                    finish(NG - 1)
            run_turns(dve, NH // 2, turn)


def project_out_phase(nc, attnT, wo, x, x_out, T):
    phase = "oproj"
    NT = T // P
    with ExitStack() as ctx:
        m = Memory(nc, ctx, phase)
        at = m.sb("at", [P, KT, T])
        w = m.sb("w", [P, KT, D])
        xs = m.sb("xs", [P, NT, D])
        acc = m.ps("acc", [P, 4, D])
        w_in = m.sem("w_in")
        x_in = m.sem("x_in")
        done = m.sem("done")
        added = m.sem("added")
        stored = m.sem("stored")
        block = ctx.enter_context(nc.Block())

        @block.sync
        def _(sp):
            for k in range(KT):
                sp.dma_start(at[:, k, :], attnT[k * P:(k + 1) * P, :]).then_inc(w_in, 16)
                sp.dma_start(w[:, k, :], wo[k * P:(k + 1) * P, :]).then_inc(w_in, 16)
            sp.dma_start(xs[:, :, :], x.rearrange("(n p) d -> p n d", p=P)).then_inc(x_in, 16)
            for g in range(NT // 4):
                sp.wait_ge(added, 4 * (g + 1))
                sp.dma_start(x_out[g * 4 * P:(g + 1) * 4 * P, :].rearrange("(n p) d -> p n d", p=P), xs[:, 4 * g:4 * g + 4, :]).then_inc(stored, 16)
            sp.wait_ge(stored, 16 * (NT // 4))

        @block.tensor
        def _(pe):
            pe.wait_ge(w_in, 32 * KT)
            for n in range(NT):
                if n >= 4:
                    pe.wait_ge(added, n - 3)
                for k in range(KT):
                    mm = pe.matmul(acc[:, n % 4, :], at[:, k, n * P:(n + 1) * P], w[:, k, :], start=(k == 0), stop=(k == KT - 1))
                mm.then_inc(done, 1)

        @block.vector
        def _(dve):
            dve.wait_ge(x_in, 16)
            for n in range(NT):
                dve.wait_ge(done, n + 1)
                dve.tensor_tensor(xs[:, n, :], xs[:, n, :], acc[:, n % 4, :], ALU.add).then_inc(added, 1)


HEADS_B = 16
DH = D // HEADS_B
RATIO = 0.1
THETA = 10000.0


def constants(T):
    inv = (1.0 / THETA ** (np.arange(0, DH, 2, dtype=np.float32) / np.float32(DH))).astype(np.float32)
    freqs = np.arange(T, dtype=np.float32)[:, None] * inv[None, :]
    emb = np.concatenate([freqs, freqs], axis=-1)
    sign = np.where(np.arange(DH) < DH // 2, -1.0, 1.0).astype(np.float32)
    cos = np.tile(np.cos(emb).astype(np.float32).T, (P // DH, 1))
    sin = np.tile((np.sin(emb).astype(np.float32) * sign).T, (P // DH, 1))
    had = np.ones((1, 1), np.float32)
    while had.shape[0] < P:
        had = np.block([[had, had], [had, -had]])
    r, c = np.arange(P)[:, None], np.arange(P)[None, :]
    recent = int(RATIO * T)
    return {
        "c_ident": np.eye(P, dtype=np.float32),
        "c_hmask": (r % GH == np.arange(GH)[None, :]).astype(np.float32),
        "c_cos": np.ascontiguousarray(cos), "c_sin": np.ascontiguousarray(sin),
        "c_had": np.ascontiguousarray(had.astype(np.float32)),
        "c_causal": np.where(c <= r, 0.0, NEG).astype(np.float32),
        "c_causalT": np.where(r <= c, 0.0, NEG).astype(np.float32),
        "c_before": (r < c).astype(np.float32),
        "c_farT": np.stack([(d * P + c - r > recent) for d in (1, 2)]).astype(np.float32),
    }


def program(nc, a, out):
    T = a["x"].shape[0]
    F = a["w1"].shape[1]
    scratch = lambda name, shape: nc.dram_tensor(name, shape, F32, kind="Internal").ap()
    xnT = [scratch(f"xnT{i}", (2, KT, P, T)) for i in range(2)]
    xs = [scratch(f"x{i}", (T, D)) for i in range(3)]
    streams = [scratch(f"stream_{n}", (H, P, T)) for n in ("beta_k", "q", "k", "beta_v", "a")]
    beta = scratch("beta", (H, T))
    blocks = scratch("blocks", (H, P, T // C))
    decays = scratch("decays", (T // C, H * P))
    o = scratch("o", (H, P, T))
    qk = scratch("qk", (2, 2, D, T))
    peaks = scratch("peaks", (2, HEADS_B * T // P, P))
    biasT = scratch("biasT", (2, HEADS_B, P, T // P))
    v = scratch("v", (T, D))
    sums = scratch("sums", (HEADS_B, T))
    bias = scratch("bias", (HEADS_B, T))
    attnT = scratch("attnT", (D, T))
    w2t = scratch("w2t", (F, D))
    transform_phase(nc, a["w2"], a["c_had"], w2t, F)
    layernorm_phase(nc, "ln0", a["x"], xnT[0], a["c_ident"], T)
    project_phase(nc, xnT[0], [a["wk"], a["wv"], a["wq"], a["wa"]], a["wb"],
                  [a["kc_w"], a["vc_w"], a["qc_w"]], [a["kc_b"], a["vc_b"], a["qc_b"]],
                  a["ba"], a["bb"], streams, beta, blocks, T, H, float(P) ** -0.5, C)
    block_decay_phase(nc, blocks, decays, a["c_ident"], T, H, C)
    scan_phase(nc, streams, decays, o, a["c_ident"], a["c_hmask"], T)
    mix_phase(nc, xnT[0], a["wg"], o, a["wo"], a["ln_g"], a["ln_b"], a["x"], xs[0], T, H)
    ffn_phase(nc, "ffn0", a["c_ident"], a["w1"], a["w3"], w2t, xs[0], xs[1], T, F)
    layernorm_phase(nc, "ln2", xs[1], xnT[1], a["c_ident"], T, split=False)
    rope_phase(nc, xnT[1], [a["bq"], a["bq_swap"], a["bk"], a["bk_swap"]], a["bv"], a["c_cos"], a["c_sin"], qk, v, T)
    recent = int(RATIO * T)
    causal = (a["c_ident"], a["c_causal"])
    column_sum_phase(nc, qk, causal, sums, T, HEADS_B, DH)
    heavy_phase(nc, sums, bias, biasT, a["c_ident"], T, HEADS_B, recent, recent)
    chosen_max_phase(nc, qk, bias, biasT, causal, a["c_before"], a["c_ident"], peaks, T, HEADS_B, DH, recent)
    attend_phase(nc, qk, v, biasT, peaks, (a["c_ident"], a["c_causalT"], a["c_farT"][0], a["c_farT"][1]), attnT,
                 T, HEADS_B, DH, recent)
    project_out_phase(nc, attnT, a["bo"], xs[1], xs[2], T)
    ffn_phase(nc, "ffn1", a["c_ident"], a["w1"], a["w3"], w2t, xs[2], out, T, F)


def laid_out(i):
    g = lambda n: np.asarray(i[n])
    t = lambda n: np.ascontiguousarray(g(n).T)
    A, B, FN = "L0_attn_a_", "L0_attn_b_", "L0_ffn_"
    swap = np.arange(D).reshape(HEADS_B, 2, DH // 2)[:, ::-1].reshape(-1)
    per_head = lambda n: np.ascontiguousarray(g(n).reshape(H, P).T)
    taps = lambda n: np.ascontiguousarray(g(n).reshape(H, P, -1).transpose(1, 0, 2))
    return {
        "x": np.ascontiguousarray(g(A + "x")[0]),
        "wq": t(A + "Wq"), "wk": t(A + "Wk"), "wv": t(A + "Wv"), "wa": t(A + "Wa"), "wb": t(A + "Wb"),
        "wg": t(A + "Wg"), "wo": t(A + "Wo"), "ba": np.ascontiguousarray(g(A + "ba").reshape(H, P)),
        "bb": np.ascontiguousarray(g(A + "bb").reshape(H, 1)),
        "qc_w": taps(A + "qc_w"), "kc_w": taps(A + "kc_w"), "vc_w": taps(A + "vc_w"),
        "qc_b": per_head(A + "qc_b"), "kc_b": per_head(A + "kc_b"), "vc_b": per_head(A + "vc_b"),
        "ln_g": np.ascontiguousarray(g(A + "ln_g").reshape(P, 1)),
        "ln_b": np.ascontiguousarray(g(A + "ln_b").reshape(P, 1)),
        "bq": t(B + "Wq"), "bk": t(B + "Wk"), "bv": t(B + "Wv"), "bo": t(B + "Wo"),
        "bq_swap": np.ascontiguousarray(g(B + "Wq")[swap].T),
        "bk_swap": np.ascontiguousarray(g(B + "Wk")[swap].T),
        "w1": t(FN + "W1"), "w3": t(FN + "W3"), "w2": t(FN + "W2"),
    }


def kernel(**inputs):
    import concourse.bacc as bacc
    from concourse.bass_utils import run_bass_kernel_spmd

    arrays = laid_out(inputs)
    T = arrays["x"].shape[0]
    arrays.update(constants(T))
    nc = bacc.Bacc("TRN2", target_bir_lowering=False, num_devices=1)
    a = {n: nc.dram_tensor(f"in_{n}", v.shape, mybir.dt.from_np(v.dtype), kind="ExternalInput").ap()
         for n, v in arrays.items()}
    out = nc.dram_tensor("out", (T, D), F32, kind="ExternalOutput").ap()
    program(nc, a, out)
    r = run_bass_kernel_spmd(nc, [{f"in_{n}": v for n, v in arrays.items()}], core_ids=[0])
    return r.results[0]["out"].reshape(1, T, D)
```
